# Optimizing a Trainium2 kernel written in Bass

```python
import numpy as np
import jax
import jax.numpy as jnp

def _softmax(x, axis=-1):
    return jax.nn.softmax(x, axis=axis)

def _gelu(x):
    return jax.nn.gelu(x, approximate=True)

def _silu(x):
    return jax.nn.silu(x)

def _sigmoid(x):
    return jax.nn.sigmoid(x)

def _layernorm(x, axis=-1, eps=1e-05):
    m = jnp.mean(x, axis=axis, keepdims=True)
    v = jnp.var(x, axis=axis, keepdims=True)
    return (x - m) / jnp.sqrt(v + eps)

def _scatter_add(tgt, idx, src, axis=0):
    return tgt.at[idx].add(src)

def _segment_sum(src, seg, n):
    return jax.ops.segment_sum(src, seg, n)
kernel_name = 'mk_prb_d1_jaxref_r8_db2e30'

def setup_inputs(seed: int=0):
    np.random.seed(seed)
    _w = jnp.asarray

    def _L0_attn_setup():
        import jax, jax.numpy as jnp
        import numpy as np
        B, T, D = (4, 256, 128)
        H, Kd = (4, 32)
        Vd = 64
        KEY_DIM, VAL_DIM = (H * Kd, H * Vd)
        CONV = 4
        EPS = 1e-06
        LN_EPS = 1e-05

        def _layernorm(x, g, b):
            m = jnp.mean(x, -1, keepdims=True)
            v = jnp.mean((x - m) ** 2, -1, keepdims=True)
            return (x - m) * jax.lax.rsqrt(v + LN_EPS) * g + b

        def _rmsnorm(x, w):
            return x * jax.lax.rsqrt(jnp.mean(x * x, -1, keepdims=True) + EPS) * w

        def _l2norm(x):
            return x * jax.lax.rsqrt(jnp.sum(x * x, -1, keepdims=True) + EPS)

        def _causal_conv_silu(x, w):
            t = x.shape[1]
            xp = jnp.pad(x, ((0, 0), (CONV - 1, 0), (0, 0)))
            y = xp[:, 0:t, :] * w[:, 0]
            for i in range(1, CONV):
                y = y + xp[:, i:i + t, :] * w[:, i]
            return jax.nn.silu(y)

        def _gated_delta_rule(q, k, v, g, beta):
            qT = jnp.moveaxis(q, 1, 0)
            kT = jnp.moveaxis(k, 1, 0)
            vT = jnp.moveaxis(v, 1, 0)
            gT = jnp.moveaxis(g, 1, 0)
            bT = jnp.moveaxis(beta, 1, 0)
            S0 = jnp.zeros((q.shape[0], H, Kd, Vd), q.dtype)

            def step(S, inp):
                q_t, k_t, v_t, g_t, b_t = inp
                S = S * jnp.exp(g_t)[..., None, None]
                kv = jnp.einsum('bhk,bhkv->bhv', k_t, S)
                delta = (v_t - kv) * b_t[..., None]
                S = S + k_t[..., :, None] * delta[..., None, :]
                o = jnp.einsum('bhk,bhkv->bhv', q_t, S)
                return (S, o)
            _, o = jax.lax.scan(step, S0, (qT, kT, vT, gT, bT))
            return jnp.moveaxis(o, 0, 1)

        def _forward(x, ln1_g, ln1_b, ln2_g, ln2_b, rms_in_w, Wq, Wk, Wv, conv_q_w, conv_k_w, conv_v_w, Wa, dt_bias, A_log, Wb, Wg, o_norm_w, Wo, W2, b2):
            b, t, _ = x.shape
            h = _layernorm(x, ln1_g, ln1_b)
            h = _rmsnorm(h, rms_in_w)
            q = _causal_conv_silu(h @ Wq, conv_q_w).reshape(b, t, H, Kd)
            k = _causal_conv_silu(h @ Wk, conv_k_w).reshape(b, t, H, Kd)
            v = _causal_conv_silu(h @ Wv, conv_v_w).reshape(b, t, H, Vd)
            q = _l2norm(q) * Kd ** (-0.5)
            k = _l2norm(k)
            g = -jnp.exp(A_log) * jax.nn.softplus(h @ Wa + dt_bias)
            beta = jax.nn.sigmoid(h @ Wb)
            o = _gated_delta_rule(q, k, v, g, beta)
            gate = (h @ Wg).reshape(b, t, H, Vd)
            o = _rmsnorm(o, o_norm_w) * jax.nn.silu(gate)
            enc = o.reshape(b, t, VAL_DIM) @ Wo
            x = x + enc
            h2 = _layernorm(x, ln2_g, ln2_b)
            x_out = jax.nn.gelu(h2 @ W2 + b2, approximate=False) + x
            return x_out
        key = jax.random.key(seed)
        ks = jax.random.split(key, 16)
        r = lambda k, shp, s=0.02: jax.random.normal(k, shp, dtype=jnp.float32) * s
        return {'x': jax.random.normal(ks[0], (B, T, D), dtype=jnp.float32), 'ln1_g': jnp.ones((D,), jnp.float32), 'ln1_b': jnp.zeros((D,), jnp.float32), 'ln2_g': jnp.ones((D,), jnp.float32), 'ln2_b': jnp.zeros((D,), jnp.float32), 'rms_in_w': jnp.ones((D,), jnp.float32), 'Wq': r(ks[1], (D, KEY_DIM)), 'Wk': r(ks[2], (D, KEY_DIM)), 'Wv': r(ks[3], (D, VAL_DIM)), 'conv_q_w': r(ks[4], (KEY_DIM, CONV), 0.3), 'conv_k_w': r(ks[5], (KEY_DIM, CONV), 0.3), 'conv_v_w': r(ks[6], (VAL_DIM, CONV), 0.3), 'Wa': r(ks[7], (D, H)), 'dt_bias': r(ks[8], (H,), 0.5), 'A_log': jnp.log(jax.random.uniform(ks[9], (H,), minval=1.0, maxval=16.0)), 'Wb': r(ks[10], (D, H)), 'Wg': r(ks[11], (D, VAL_DIM)), 'o_norm_w': jnp.ones((Vd,), jnp.float32), 'Wo': r(ks[12], (VAL_DIM, D)), 'W2': r(ks[13], (D, D)), 'b2': jnp.zeros((D,), jnp.float32)}
    _L0_attn_in = _L0_attn_setup()

    def _L0_ffn_setup():
        import jax, jax.numpy as jnp
        import numpy as np
        H_DIM, E_DIM = (128, 64)
        N_SHARED, N_ROUTED, TOP_K = (2, 16, 4)
        B, S = (4, 256)
        key = jax.random.key(seed)
        ks = jax.random.split(key, 6)
        sc = 1.0 / np.sqrt(H_DIM)
        ec = 1.0 / np.sqrt(E_DIM)
        return {'x': jax.random.normal(ks[0], (B, S, H_DIM), dtype=jnp.float32), 'shared_up': jax.random.uniform(ks[1], (N_SHARED, E_DIM, H_DIM), jnp.float32, -sc, sc), 'shared_down': jax.random.uniform(ks[2], (N_SHARED, H_DIM, E_DIM), jnp.float32, -ec, ec), 'routed_up': jax.random.uniform(ks[3], (N_ROUTED, E_DIM, H_DIM), jnp.float32, -sc, sc), 'routed_down': jax.random.uniform(ks[4], (N_ROUTED, H_DIM, E_DIM), jnp.float32, -ec, ec), 'router_w': jax.random.uniform(ks[5], (N_ROUTED, H_DIM), jnp.float32, -sc, sc)}
    _L0_ffn_in = _L0_ffn_setup()
    _d = {'L0_attn_x': _L0_attn_in['x'], 'L0_attn_ln1_g': _L0_attn_in['ln1_g'], 'L0_attn_ln1_b': _L0_attn_in['ln1_b'], 'L0_attn_ln2_g': _L0_attn_in['ln2_g'], 'L0_attn_ln2_b': _L0_attn_in['ln2_b'], 'L0_attn_rms_in_w': _L0_attn_in['rms_in_w'], 'L0_attn_Wq': _L0_attn_in['Wq'], 'L0_attn_Wk': _L0_attn_in['Wk'], 'L0_attn_Wv': _L0_attn_in['Wv'], 'L0_attn_conv_q_w': _L0_attn_in['conv_q_w'], 'L0_attn_conv_k_w': _L0_attn_in['conv_k_w'], 'L0_attn_conv_v_w': _L0_attn_in['conv_v_w'], 'L0_attn_Wa': _L0_attn_in['Wa'], 'L0_attn_dt_bias': _L0_attn_in['dt_bias'], 'L0_attn_A_log': _L0_attn_in['A_log'], 'L0_attn_Wb': _L0_attn_in['Wb'], 'L0_attn_Wg': _L0_attn_in['Wg'], 'L0_attn_o_norm_w': _L0_attn_in['o_norm_w'], 'L0_attn_Wo': _L0_attn_in['Wo'], 'L0_attn_W2': _L0_attn_in['W2'], 'L0_attn_b2': _L0_attn_in['b2'], 'L0_ffn_shared_up': _L0_ffn_in['shared_up'], 'L0_ffn_shared_down': _L0_ffn_in['shared_down'], 'L0_ffn_routed_up': _L0_ffn_in['routed_up'], 'L0_ffn_routed_down': _L0_ffn_in['routed_down'], 'L0_ffn_router_w': _L0_ffn_in['router_w']}
    _x0 = _d['L0_attn_x']
    _d['L0_attn_x'] = jax.random.normal(jax.random.fold_in(jax.random.key(seed), 1), (32, 256, 128), dtype=_x0.dtype)
    del _x0
    return _d

def reference(L0_attn_x, L0_attn_ln1_g, L0_attn_ln1_b, L0_attn_ln2_g, L0_attn_ln2_b, L0_attn_rms_in_w, L0_attn_Wq, L0_attn_Wk, L0_attn_Wv, L0_attn_conv_q_w, L0_attn_conv_k_w, L0_attn_conv_v_w, L0_attn_Wa, L0_attn_dt_bias, L0_attn_A_log, L0_attn_Wb, L0_attn_Wg, L0_attn_o_norm_w, L0_attn_Wo, L0_attn_W2, L0_attn_b2, L0_ffn_shared_up, L0_ffn_shared_down, L0_ffn_routed_up, L0_ffn_routed_down, L0_ffn_router_w):

    def _L0_attn_ref(x, ln1_g, ln1_b, ln2_g, ln2_b, rms_in_w, Wq, Wk, Wv, conv_q_w, conv_k_w, conv_v_w, Wa, dt_bias, A_log, Wb, Wg, o_norm_w, Wo, W2, b2):
        import jax, jax.numpy as jnp
        import numpy as np
        B, T, D = (4, 256, 128)
        H, Kd = (4, 32)
        Vd = 64
        KEY_DIM, VAL_DIM = (H * Kd, H * Vd)
        CONV = 4
        EPS = 1e-06
        LN_EPS = 1e-05

        def _layernorm(x, g, b):
            m = jnp.mean(x, -1, keepdims=True)
            v = jnp.mean((x - m) ** 2, -1, keepdims=True)
            return (x - m) * jax.lax.rsqrt(v + LN_EPS) * g + b

        def _rmsnorm(x, w):
            return x * jax.lax.rsqrt(jnp.mean(x * x, -1, keepdims=True) + EPS) * w

        def _l2norm(x):
            return x * jax.lax.rsqrt(jnp.sum(x * x, -1, keepdims=True) + EPS)

        def _causal_conv_silu(x, w):
            t = x.shape[1]
            xp = jnp.pad(x, ((0, 0), (CONV - 1, 0), (0, 0)))
            y = xp[:, 0:t, :] * w[:, 0]
            for i in range(1, CONV):
                y = y + xp[:, i:i + t, :] * w[:, i]
            return jax.nn.silu(y)

        def _gated_delta_rule(q, k, v, g, beta):
            qT = jnp.moveaxis(q, 1, 0)
            kT = jnp.moveaxis(k, 1, 0)
            vT = jnp.moveaxis(v, 1, 0)
            gT = jnp.moveaxis(g, 1, 0)
            bT = jnp.moveaxis(beta, 1, 0)
            S0 = jnp.zeros((q.shape[0], H, Kd, Vd), q.dtype)

            def step(S, inp):
                q_t, k_t, v_t, g_t, b_t = inp
                S = S * jnp.exp(g_t)[..., None, None]
                kv = jnp.einsum('bhk,bhkv->bhv', k_t, S)
                delta = (v_t - kv) * b_t[..., None]
                S = S + k_t[..., :, None] * delta[..., None, :]
                o = jnp.einsum('bhk,bhkv->bhv', q_t, S)
                return (S, o)
            _, o = jax.lax.scan(step, S0, (qT, kT, vT, gT, bT))
            return jnp.moveaxis(o, 0, 1)

        def _forward(x, ln1_g, ln1_b, ln2_g, ln2_b, rms_in_w, Wq, Wk, Wv, conv_q_w, conv_k_w, conv_v_w, Wa, dt_bias, A_log, Wb, Wg, o_norm_w, Wo, W2, b2):
            b, t, _ = x.shape
            h = _layernorm(x, ln1_g, ln1_b)
            h = _rmsnorm(h, rms_in_w)
            q = _causal_conv_silu(h @ Wq, conv_q_w).reshape(b, t, H, Kd)
            k = _causal_conv_silu(h @ Wk, conv_k_w).reshape(b, t, H, Kd)
            v = _causal_conv_silu(h @ Wv, conv_v_w).reshape(b, t, H, Vd)
            q = _l2norm(q) * Kd ** (-0.5)
            k = _l2norm(k)
            g = -jnp.exp(A_log) * jax.nn.softplus(h @ Wa + dt_bias)
            beta = jax.nn.sigmoid(h @ Wb)
            o = _gated_delta_rule(q, k, v, g, beta)
            gate = (h @ Wg).reshape(b, t, H, Vd)
            o = _rmsnorm(o, o_norm_w) * jax.nn.silu(gate)
            enc = o.reshape(b, t, VAL_DIM) @ Wo
            x = x + enc
            h2 = _layernorm(x, ln2_g, ln2_b)
            x_out = jax.nn.gelu(h2 @ W2 + b2, approximate=False) + x
            return x_out
        return _forward(x, ln1_g, ln1_b, ln2_g, ln2_b, rms_in_w, Wq, Wk, Wv, conv_q_w, conv_k_w, conv_v_w, Wa, dt_bias, A_log, Wb, Wg, o_norm_w, Wo, W2, b2)

    def _L0_ffn_ref(x, shared_up, shared_down, routed_up, routed_down, router_w):
        import jax, jax.numpy as jnp
        import numpy as np
        H_DIM, E_DIM = (128, 64)
        N_SHARED, N_ROUTED, TOP_K = (2, 16, 4)
        B, S = (4, 256)
        b, s, h = x.shape
        xt = x.reshape(-1, h)
        up_s = jnp.einsum('th,seh->tse', xt, shared_up)
        shared = jnp.einsum('tse,she->th', jax.nn.gelu(up_s, approximate=False), shared_down)
        probs = jax.nn.softmax(xt @ router_w.T, axis=-1)
        topk_p, topk_i = jax.lax.top_k(probs, TOP_K)
        gate = jnp.zeros_like(probs).at[jnp.arange(xt.shape[0])[:, None], topk_i].add(topk_p)
        up_r = jnp.einsum('th,reh->tre', xt, routed_up)
        act = jax.nn.gelu(up_r, approximate=False) * gate[:, :, None]
        routed = jnp.einsum('tre,rhe->th', act, routed_down)
        return (shared + routed).reshape(b, s, h)
    x = L0_attn_x
    xn = _layernorm(x, axis=-1)
    x = x + _L0_attn_ref(xn, L0_attn_ln1_g, L0_attn_ln1_b, L0_attn_ln2_g, L0_attn_ln2_b, L0_attn_rms_in_w, L0_attn_Wq, L0_attn_Wk, L0_attn_Wv, L0_attn_conv_q_w, L0_attn_conv_k_w, L0_attn_conv_v_w, L0_attn_Wa, L0_attn_dt_bias, L0_attn_A_log, L0_attn_Wb, L0_attn_Wg, L0_attn_o_norm_w, L0_attn_Wo, L0_attn_W2, L0_attn_b2) + _L0_ffn_ref(xn, L0_ffn_shared_up, L0_ffn_shared_down, L0_ffn_routed_up, L0_ffn_routed_down, L0_ffn_router_w)
    return x

_drawn_inputs = setup_inputs


def setup_inputs(seed=0):
    import zlib

    import numpy as np

    out = dict(_drawn_inputs(seed))
    spreads = {'L0_attn_ln1_g': (1.0, 0.6),
     'L0_attn_ln1_b': (0.0, 0.8),
     'L0_attn_ln2_g': (1.0, 0.6),
     'L0_attn_ln2_b': (0.0, 0.8),
     'L0_attn_rms_in_w': (1.0, 0.6),
     'L0_attn_o_norm_w': (1.0, 0.6),
     'L0_attn_b2': (0.0, 0.3)}
    factors = {'L0_attn_Wq': 4.512,
     'L0_attn_Wk': 4.483,
     'L0_attn_Wv': 4.498,
     'L0_attn_conv_q_w': 4.507,
     'L0_attn_conv_k_w': 4.418,
     'L0_attn_conv_v_w': 4.343,
     'L0_attn_Wa': 8.0,
     'L0_attn_dt_bias': 8.0,
     'L0_attn_A_log': 8.0,
     'L0_attn_Wb': 8.0,
     'L0_attn_Wg': 4.488,
     'L0_attn_Wo': 4.466,
     'L0_ffn_router_w': 2.788}
    for name, (base, spread) in spreads.items():
        noise = np.random.default_rng([zlib.crc32(name.encode()), seed]).standard_normal(out[name].shape)
        drawn = base * np.exp(spread * noise) if base else spread * noise
        out[name] = jnp.asarray(drawn.astype(out[name].dtype))
    for name, factor in factors.items():
        out[name] = (out[name] * factor).astype(out[name].dtype)
    return out
```

```python
from contextlib import ExitStack

import concourse.bass as bass
from concourse import mybir

F32 = mybir.dt.float32
BF16 = mybir.dt.bfloat16
ALU = mybir.AluOpType
ACT = mybir.ActivationFunctionType
AX = mybir.AxisListType

P = 128
T = 256
SEQ = 4
N = SEQ * T
TILES = N // P
HALF = 512
C = 32
NC_SEQ = T // C
NCH = N // C
H = 4
KD = 32
VD = 64
TAPS = 4
PAD = TAPS - 1
E = 16
TOPK = 4
BLKS = 9
LN_EPS = 1e-5
EPS = 1e-6
G_LEAST = -200.0

C_IDENT, C_MEAN, C_HEAD, C_HEADQ, C_LATER, C_UPTO, C_BEFORE, C_EYE = 0, 128, 256, 384, 512, 640, 672, 704
C_COLS = C_EYE + C * C
W_Q, W_K, W_V, W_G, W_AB = 0, 128, 256, 512, 768
W_COLS = W_AB + 2 * H
(V_LN1G, V_LN1B, V_LN2G, V_LN2B, V_RMS, V_ON0, V_ON1, V_B2, V_CONV) = (0, 1, 2, 3, 4, 5, 6, 7, 8)
V_COLS = V_CONV + 4 * TAPS

FFN_JOBS = {hf: [("up", hf, 0)] + [j for m in range(1, BLKS) for j in (("up", hf, m), ("gate", hf, m))]
            for hf in range(2)}
RING_JOBS = (
    [("xnT", 0), ("xnT", 1), ("xsT", 0), ("xsT", 1), ("rms", 0), ("rms", 1), ("router",), ("ab",)]
    + [("qkv", b, hf) for b in range(4) for hf in range(2)]
    + [("ogate", b, hf) for b in range(2) for hf in range(2)]
    + [("grow", 0), ("grow", 1), ("brow", 0), ("brow", 1), ("decay", 0), ("decay", 1), ("fromstart", 0),
       ("fromstart", 1)]
    + [("l2", b, hf) for b in range(2) for hf in range(2)]
    + [("pairs", q) for q in range(4)]
    + [("gateT",)]
    + FFN_JOBS[0] + FFN_JOBS[1]
    + [("enc", 0), ("enc", 1), ("h2T", 0), ("h2T", 1), ("w2", 0), ("w2", 1), ("final", 0), ("final", 1)])
RING = 4
BANK_Y, BANK_KS, BANK_D, BANK_O = 4, 5, 6, 7


def build(nc, x, consts, sel_in, wproj_in, wup_in, wdown_in, wo_in, w2_in, router_in, vecs_in, rowb_in,
          out, scr_a, scr_t):
    groups = x.shape[0] // N
    ctx = ExitStack()
    with ctx:
        def sb(name, shape, dt=F32):
            return ctx.enter_context(nc.sbuf_tensor(name, shape, dt))

        class Signal:

            def __init__(self, name, per, first=0):
                self.sem = ctx.enter_context(nc.semaphore(name))
                self.per, self.first = per, first

            def at(self, g, k):
                return g * self.per + (self.first + k)

        cst = sb("cst", [P, C_COLS])
        ident_b = sb("ident_b", [P, P], BF16)
        spare = sb("spare", [P, 8])
        sel = sb("sel", [3 * E, (BLKS - 1) * P], BF16)
        wproj = sb("wproj", [P, W_COLS])
        wup = sb("wup", [P, BLKS, P])
        wdown = sb("wdown", [P, BLKS, P])
        wo = sb("wo", [P, 2, P])
        w2 = sb("w2", [P, P])
        wrout = sb("wrout", [P, E])
        vecs = sb("vecs", [P, V_COLS])
        rowb = sb("rowb", [P, 3 * H])
        neg_a = sb("neg_a", [P, H])
        exp_a = sb("exp_a", [P, H])
        small = sb("small", [P, 8])
        K_LNEPS, K_EPS, K_EPSQ, K_ONE, K_MHALF, K_TOPK = range(6)

        def k_(i):
            return small[:, i:i + 1]

        ident = cst[:, C_IDENT:C_IDENT + P]

        xin = sb("xin", [P, TILES, P])
        xn = sb("xn", [P, TILES, P])
        xs = sb("xs", [P, TILES, P])
        st = sb("st", [P, TILES, 6])
        mv = sb("mv", [P, TILES, 2])
        lnw = sb("lnw", [P, 6, TILES])
        rstd = sb("rstd", [P, TILES])
        rs2 = sb("rs2", [P, TILES])
        xnT = sb("xnT", [P, N])
        hT = sb("hT", [P, N])
        hn = sb("hn", [P, N])
        sq = sb("sq", [P, 2, N])
        rln = sb("rln", [P, 2, N])
        rr = sb("rr", [P, 2, N])
        raw = sb("raw", [P, 4, SEQ, PAD + T])
        conv = sb("conv", [P, 4, N])
        act4 = sb("act4", [P, 4, N])
        ogate = sb("ogate", [P, 2, N])
        kq = sb("kq", [P, 2, N])
        zab = sb("zab", [P, TILES, 2 * H])
        zabs = sb("zabs", [P, TILES, 2 * H])
        zexp = sb("zexp", [P, TILES, 2 * H])
        zln = sb("zln", [P, TILES, H])
        zden = sb("zden", [P, TILES, H])
        zrec = sb("zrec", [P, TILES, H])
        znum = sb("znum", [P, TILES, H])
        zsp = sb("zsp", [P, TILES, H])
        zbeta = sb("zbeta", [P, TILES, H])
        zg = sb("zg", [P, TILES, H])
        bcol = sb("bcol", [P, NCH, C])
        brow_am = sb("brow_am", [P, 2, N])
        decay = sb("decay", [P, NCH, C])
        fromst = sb("fromst", [P, NCH, C])
        at = sb("at", [P, NCH, C])
        pt = sb("pt", [P, NCH, C])
        lane_t = sb("lane_t", [P, C, C])
        ttb = sb("ttb", [P, NCH, C])
        state = sb("state", [P, SEQ, VD])
        sdec = sb("sdec", [P, SEQ, VD])
        resid = sb("resid", [P, SEQ, VD])
        delta = sb("delta", [P, SEQ, VD])
        oms = sb("oms", [P, NCH])
        omr = sb("omr", [P, NCH])
        orr = sb("orr", [P, NCH])
        lmax = sb("lmax", [P, TILES])
        lsh = sb("lsh", [P, TILES, E])
        er = sb("er", [P, TILES, E])
        top8 = sb("top8", [P, TILES, 8])
        esum = sb("esum", [P, TILES])
        erec = sb("erec", [P, TILES])
        gt = sb("gt", [P, TILES, E])
        ngt = sb("ngt", [P, TILES])
        cum = sb("cum", [P, 3, TILES, 8 + E])
        cnt = sb("cnt", [P, TILES, E])
        keep = sb("keep", [P, TILES, E])
        keep2 = sb("keep2", [P, TILES, E])
        gun = sb("gun", [P, TILES, E])
        gfull = sb("gfull", [P, TILES, E])
        gres = sb("gres", [P, 2, TILES, E])
        gparts = sb("gparts", [P, TILES, 3, E], BF16)
        gpT = sb("gpT", [3 * E, N], BF16)
        gel = sb("gel", [P, 3, HALF])
        hid = sb("hid", [P, 3, HALF])
        yout = sb("yout", [P, TILES, P])


        def chunks(ap):
            return ap.rearrange("p (c i) -> p c i", i=C)

        brow = chunks(brow_am[:, 0, :])
        am2 = chunks(brow_am[:, 1, :])
        o = brow_am[:, :, :].rearrange("p a (c v) -> p (a c) v", v=VD)
        x2 = decay[:].rearrange("p c i -> p (c i)").rearrange("p (t d) -> p t d", d=P)
        ffnT = at[:].rearrange("p c i -> p (c i)")
        wproj_raw = conv[:, 0, 0:W_COLS]
        sel_f = conv[0:3 * E, 1, :]
        wo_raw = conv[:, 2, 0:2 * P].rearrange("p (a d) -> p a d", d=P)
        gb = rr[:, :, :].rearrange("p k (t h r) -> p k t h r", h=H, r=C)
        h2 = xs
        h2T = hT
        gelT = hn
        sumT = rln[:, 0, :]
        xx2 = rln[:, 1, :].rearrange("p (t d) -> p t d", d=P)
        osq = conv[:, 0:2, :].rearrange("p a (c v) -> p (a c) v", v=VD)
        on = conv[:, 2:4, :].rearrange("p a (c v) -> p (a c) v", v=VD)
        oT = act4[:, 0:2, :]
        og = act4[:, 2:4, :]
        gcol = chunks(rln[:, 1, :])
        am1 = chunks(hT[:, :])
        pmask = chunks(xs[:, :, :].rearrange("p t d -> p (t d)"))
        mcum = chunks(hn[:, :])
        lane_m = sq[:, 0, :]
        ttb0 = chunks(sq[:, 1, :])
        lane_a = chunks(rr[:, 0, :])
        kcol = chunks(rr[:, 1, :])
        vtok = conv[:, 0:2, :].rearrange("p a (c v) -> p (a c) v", v=VD)
        kg = chunks(act4[:, 0, :])
        qg = chunks(act4[:, 1, :])
        kend = chunks(act4[:, 2, :])

        ps = ctx.enter_context(nc.psum_tensor("ps", [P, 8, 512], F32))

        loaded = Signal("weights_loaded", 0)
        cst_ready = Signal("constants_ready", 0)
        per_bank = [len(RING_JOBS[b::RING]) for b in range(RING)]
        full = [Signal(f"bank{b}_full", per_bank[b]) for b in range(RING)]
        free = [Signal(f"bank{b}_free", per_bank[b], 1) for b in range(RING)]
        pool_chain = Signal("pool_chain", 12)
        act_chain = Signal("act_chain", 1)
        dve_chain = Signal("dve_chain", 99)
        x_loaded = Signal("x_loaded", 16)
        y_stored = Signal("y_stored", 16, 1)
        stats1 = Signal("stats1_ready", 1)
        rstd1 = Signal("rstd1_ready", 1)
        xn_ready = Signal("xn_ready", 2)
        hsq_ready = Signal("hsq_ready", 2)
        rms_ready = Signal("rms_ready", 1)
        hn_ready = Signal("hn_ready", 1)
        er_ready = Signal("router_exp_ready", 1)
        gate_ready = Signal("gate_ready", 1)
        gparts_ready = Signal("gate_parts_ready", 1)
        zexp_ready = Signal("zexp_ready", 2)
        gb_ready = Signal("decay_beta_ready", 1)
        conv_ready = Signal("conv_ready", 4)
        act_ready = Signal("act_ready", 4)
        sq_ready = Signal("qk_squares_ready", 2)
        rl2_ready = Signal("qk_scale_ready", 2)
        kq_ready = Signal("kq_ready", 2)
        mcum_ready = Signal("mcum_ready", 1)
        mask_ready = Signal("masked_decay_ready", 2)
        at_ready = Signal("at_ready", 4)
        at_stored = Signal("at_stored", 16)
        lane_ready = Signal("lanes_loaded", 64)
        inv_ready = Signal("inverse_ready", 1)
        inv_stored = Signal("inverse_stored", 16)
        tt_loaded = Signal("tt_loaded", 64)
        ttb_ready = Signal("ttb_ready", 1)
        scaled_ready = Signal("scaled_kq_ready", 3)
        kcol_ready = Signal("kcol_ready", 1)
        vtok_ready = Signal("vtok_ready", 2)
        s_ready = Signal("state_ready", 1 + NC_SEQ)
        ks_full = Signal("ks_full", NC_SEQ)
        r_ready = Signal("resid_ready", NC_SEQ)
        d_full = Signal("delta_full", NC_SEQ)
        d_ready = Signal("delta_ready", NC_SEQ)
        o_full = Signal("o_full", NC_SEQ)
        o_ready = Signal("o_ready", NC_SEQ)
        ds_full = Signal("state_sum_full", NC_SEQ)
        osq_ready = Signal("o_squares_ready", 1)
        oms_ready = Signal("o_mean_ready", 1)
        orr_ready = Signal("o_scale_ready", 1)
        og_ready = Signal("og_ready", 2)
        gel_ready = Signal("gelu_ready", 2 * BLKS)
        hid_ready = Signal("hidden_ready", 2 * (BLKS - 1))
        down_done = Signal("down_done", 2 * BLKS)
        y_evac = Signal("ffn_copied", 2)
        stats2 = Signal("stats2_ready", 1)
        rstd2 = Signal("rstd2_ready", 1)
        x2_ready = Signal("x2_ready", 2)
        h2_ready = Signal("h2_ready", 1)
        xx2_ready = Signal("xx2_ready", 1)
        sumT_ready = Signal("sumT_ready", 1)

        job_at = {job: (n % RING, n // RING) for n, job in enumerate(RING_JOBS)}

        def bank(job):
            return ps[:, job_at[job][0], :]

        def room(g, *job):
            b, n = job_at[job]
            return free[b].sem, free[b].at(g, n)

        def filled(*job):
            return full[job_at[job][0]].sem

        def full_of(g, *job):
            b, n = job_at[job]
            return full[b].sem, full[b].at(g, n + 1)

        def emptied(*job):
            return free[job_at[job][0]].sem

        def copied(g, *job):
            b, n = job_at[job]
            return free[b].sem, free[b].at(g, n + 1)

        def group_before(g):
            b = job_at[("final", 1)][0]
            return free[b].sem, free[b].at(g, 0)

        def half(ap2d, hf):
            return ap2d[:, hf * HALF:(hf + 1) * HALF]

        def bc_mid(ap, n):
            return ap.unsqueeze(1).broadcast_to([ap.shape[0], n, ap.shape[-1]])

        def bc_last(ap, n):
            return ap.unsqueeze(len(ap.shape)).broadcast_to([*ap.shape, n])

        def bseq(t, c):
            return t[:, :, :].rearrange("p (b c) w -> p b c w", c=NC_SEQ)[:, :, c, :]

        block = ctx.enter_context(nc.Block())

        @block.sync
        def _(sp):
            for dst, src in ((cst, consts), (sel_f, sel_in), (wproj_raw, wproj_in), (wo_raw, wo_in),
                             (w2, w2_in), (wrout, router_in), (vecs, vecs_in), (rowb, rowb_in),
                             (wup, wup_in), (wdown, wdown_in)):
                sp.dma_start(dst[:], src).then_inc(loaded.sem, 16)
            with sp.Fori(0, groups) as g:
                sp.wait_ge(*group_before(g))
                sp.dma_start(xin[:], x[bass.ds(g * N, N), :].rearrange("(t p) d -> p t d", p=P)) \
                    .then_inc(x_loaded.sem, 16)
                sp.wait_ge(at_ready.sem, at_ready.at(g, 4))
                sp.dma_start(scr_a.rearrange("h j c i -> (h j) (c i)"), at[:].rearrange("p c i -> p (c i)")) \
                    .then_inc(at_stored.sem, 16)
                sp.wait_ge(at_stored.sem, at_stored.at(g, 16))
                for h in range(H):
                    sp.dma_start(lane_a[h * C:(h + 1) * C, :, :], scr_a[h].rearrange("j c i -> c j i")) \
                        .then_inc(lane_ready.sem, 16)
                sp.wait_ge(inv_ready.sem, inv_ready.at(g, 1))
                sp.dma_start(scr_t.rearrange("h c j i -> (h c) (j i)"), lane_t[:].rearrange("p j i -> p (j i)")) \
                    .then_inc(inv_stored.sem, 16)
                sp.wait_ge(inv_stored.sem, inv_stored.at(g, 16))
                for h in range(H):
                    sp.dma_start(ttb0[h * C:(h + 1) * C, :, :], scr_t[h].rearrange("c j i -> j c i")) \
                        .then_inc(tt_loaded.sem, 16)
                sp.wait_ge(*copied(g, "final", 1))
                sp.dma_start(out[bass.ds(g * N, N), :].rearrange("(t p) d -> p t d", p=P), yout[:]) \
                    .then_inc(y_stored.sem, 16)
            sp.wait_ge(y_stored.sem, 16 * groups + 1)

        @block.gpsimd
        def _(pool):
            with pool.Fori(0, groups) as g:
                chain = [0]

                def link(ins):
                    chain[0] += 1
                    ins.then_inc(pool_chain.sem, 1)
                    pool.wait_ge(pool_chain.sem, pool_chain.at(g, chain[0]))

                def rsqrt_into(dst, src, tmp, eps):
                    link(pool.tensor_tensor(tmp, src, k_(eps).broadcast_to(list(src.shape)), ALU.add))
                    return pool.tensor_tensor(dst, tmp, k_(K_MHALF).broadcast_to(list(src.shape)), ALU.pow)

                pool.wait_ge(stats1.sem, stats1.at(g, 1))
                link(rsqrt_into(rstd[:, :], mv[:, :, 1], lnw[:, 0, :], K_LNEPS))
                link(pool.tensor_tensor(lnw[:, 1, :], mv[:, :, 1], rstd[:, :], ALU.mult))
                link(pool.tensor_tensor(lnw[:, 2, :], lnw[:, 1, :], rstd[:, :], ALU.mult))
                rsqrt_into(rs2[:, :], lnw[:, 2, :], lnw[:, 3, :], K_LNEPS).then_inc(rstd1.sem, 1)

                pool.wait_ge(gate_ready.sem, gate_ready.at(g, 1))
                one = k_(K_ONE).unsqueeze(2).broadcast_to([P, TILES, E])
                link(pool.tensor_tensor(gparts[:, :, 0, :], gfull[:], one, ALU.mult))
                link(pool.tensor_tensor(gres[:, 0], gfull[:], gparts[:, :, 0, :], ALU.subtract))
                link(pool.tensor_tensor(gparts[:, :, 1, :], gres[:, 0], one, ALU.mult))
                link(pool.tensor_tensor(gres[:, 1], gres[:, 0], gparts[:, :, 1, :], ALU.subtract))
                pool.tensor_tensor(gparts[:, :, 2, :], gres[:, 1], one, ALU.mult).then_inc(gparts_ready.sem, 1)

                pool.wait_ge(*copied(g, "decay", 1))
                pool.tensor_tensor(pmask[:], decay[:], bc_mid(cst[:, C_UPTO:C_UPTO + C], NCH), ALU.mult) \
                    .then_inc(mask_ready.sem, 1)
                pool.wait_ge(*copied(g, "brow", 1))
                link(pool.tensor_tensor(am1[:], decay[:], brow[:], ALU.mult))
                pool.tensor_tensor(am2[:], am1[:], bc_mid(cst[:, C_BEFORE:C_BEFORE + C], NCH), ALU.mult) \
                    .then_inc(mask_ready.sem, 1)

                pool.wait_ge(*copied(g, "fromstart", 1))
                pool.wait_ge(kq_ready.sem, kq_ready.at(g, 2))
                pool.tensor_tensor(kg[:], kq[:, 0, :].rearrange("p (c i) -> p c i", i=C), fromst[:], ALU.mult) \
                    .then_inc(scaled_ready.sem, 1)
                pool.tensor_tensor(qg[:], kq[:, 1, :].rearrange("p (c i) -> p c i", i=C), fromst[:], ALU.mult) \
                    .then_inc(scaled_ready.sem, 1)
                pool.wait_ge(kcol_ready.sem, kcol_ready.at(g, 1))
                pool.tensor_tensor(kend[:], kcol[:], bc_last(decay[:, :, C - 1], C), ALU.mult) \
                    .then_inc(scaled_ready.sem, 1)

                pool.wait_ge(oms_ready.sem, oms_ready.at(g, 1))
                link(pool.tensor_tensor(omr[:], oms[:], k_(K_EPS).broadcast_to([P, NCH]), ALU.add))
                pool.tensor_tensor(orr[:], omr[:], k_(K_MHALF).broadcast_to([P, NCH]), ALU.pow) \
                    .then_inc(orr_ready.sem, 1)

                pool.wait_ge(stats2.sem, stats2.at(g, 1))
                rsqrt_into(rstd[:, :], mv[:, :, 1], lnw[:, 4, :], K_LNEPS).then_inc(rstd2.sem, 1)
                pool.tensor_tensor(xx2[:], xin[:], x2[:], ALU.add).then_inc(xx2_ready.sem, 1)
                assert chain[0] == pool_chain.per, chain[0]

        @block.scalar
        def _(act):
            act.wait_ge(loaded.sem, 160)
            act.wait_ge(cst_ready.sem, 1)
            nc.scalar.activation(exp_a[:], rowb[:, 2 * H:3 * H], ACT.Exp).then_inc(cst_ready.sem, 1)
            with act.Fori(0, groups) as g:
                chain = [0]

                def link(ins):
                    chain[0] += 1
                    ins.then_inc(act_chain.sem, 1)
                    act.wait_ge(act_chain.sem, act_chain.at(g, chain[0]))

                act.wait_ge(*group_before(g))
                for hf in range(2):
                    act.wait_ge(*full_of(g, "xnT", hf))
                    act.activation(half(xnT, hf), bank(("xnT", hf)), ACT.Copy).then_inc(emptied("xnT", hf), 1)
                for hf in range(2):
                    act.wait_ge(*full_of(g, "xsT", hf))
                    act.activation(half(hT, hf), bank(("xsT", hf)), ACT.Identity,
                                   scale=vecs[:, V_LN1G:V_LN1G + 1], bias=vecs[:, V_LN1B:V_LN1B + 1]) \
                        .then_inc(emptied("xsT", hf), 1)
                    act.wait_ge(*copied(g, "xsT", hf))
                    act.activation(half(sq[:, 0, :], hf), half(hT, hf), ACT.Square).then_inc(hsq_ready.sem, 1)
                for hf in range(2):
                    act.wait_ge(*full_of(g, "rms", hf))
                    act.activation(half(rln[:, 0, :], hf), bank(("rms", hf)), ACT.Ln, bias=k_(K_EPS)) \
                        .then_inc(emptied("rms", hf), 1)
                act.wait_ge(*copied(g, "rms", 1))
                act.activation(rr[:, 0, :], rln[:, 0, :], ACT.Exp, scale=-0.5).then_inc(rms_ready.sem, 1)
                act.wait_ge(*copied(g, "router"))
                act.activation(er[:], lsh[:], ACT.Exp).then_inc(er_ready.sem, 1)
                act.wait_ge(*copied(g, "ab"))
                link(act.activation(zabs[:], zab[:], ACT.Abs))
                act.activation(zexp[:], zabs[:], ACT.Exp, scale=-1.0).then_inc(zexp_ready.sem, 1)
                act.wait_ge(zexp_ready.sem, zexp_ready.at(g, 1))
                act.activation(zln[:], zexp[:, :, 0:H], ACT.Ln, bias=k_(K_ONE)).then_inc(zexp_ready.sem, 1)
                for b4 in range(4):
                    for hf in range(2):
                        act.wait_ge(*full_of(g, "qkv", b4, hf))
                        act.activation(raw[:, b4, 2 * hf:2 * hf + 2, PAD:PAD + T],
                                       bank(("qkv", b4, hf)).rearrange("p (s t) -> p s t", t=T), ACT.Copy)
                        w = vecs[:, V_CONV + TAPS * b4 + PAD:V_CONV + TAPS * b4 + TAPS]
                        act.activation(half(conv[:, b4, :], hf), bank(("qkv", b4, hf)), ACT.Copy, scale=w) \
                            .then_inc(emptied("qkv", b4, hf), 1)
                for b2 in range(2):
                    for hf in range(2):
                        act.wait_ge(*full_of(g, "ogate", b2, hf))
                        act.activation(half(ogate[:, b2, :], hf), bank(("ogate", b2, hf)), ACT.Silu) \
                            .then_inc(emptied("ogate", b2, hf), 1)
                for b4 in range(4):
                    act.wait_ge(conv_ready.sem, conv_ready.at(g, b4 + 1))
                    act.activation(act4[:, b4, :], conv[:, b4, :], ACT.Silu).then_inc(act_ready.sem, 1)
                for b2 in range(2):
                    act.wait_ge(act_ready.sem, act_ready.at(g, b2 + 1))
                    act.activation(sq[:, b2, :], act4[:, b2, :], ACT.Square).then_inc(sq_ready.sem, 1)
                for hf in range(2):
                    act.wait_ge(*full_of(g, "brow", hf))
                    act.activation(brow[:, 16 * hf:16 * hf + 16, :],
                                   bank(("brow", hf)).rearrange("p (c i) -> p c i", i=C), ACT.Copy) \
                        .then_inc(emptied("brow", hf), 1)
                for name, dst in (("decay", decay), ("fromstart", fromst)):
                    for hf in range(2):
                        act.wait_ge(*full_of(g, name, hf))
                        act.activation(dst[:, 16 * hf:16 * hf + 16, :],
                                       bank((name, hf)).rearrange("p (c i) -> p c i", i=C), ACT.Exp) \
                            .then_inc(emptied(name, hf), 1)
                for b2 in range(2):
                    for hf in range(2):
                        act.wait_ge(*full_of(g, "l2", b2, hf))
                        act.activation(half(rln[:, b2, :], hf), bank(("l2", b2, hf)), ACT.Ln,
                                       bias=k_(K_EPSQ if b2 == 0 else K_EPS)).then_inc(emptied("l2", b2, hf), 1)
                    act.wait_ge(*copied(g, "l2", b2, 1))
                    act.activation(rr[:, b2, :], rln[:, b2, :], ACT.Exp, scale=-0.5).then_inc(rl2_ready.sem, 1)
                act.wait_ge(*full_of(g, "gateT"))
                act.activation(gpT[:], ps[0:3 * E, job_at[("gateT",)][0], :].bitcast(BF16), ACT.Copy) \
                    .then_inc(emptied("gateT"), 1)

                def gelu(hf, m):
                    n = hf * BLKS + m
                    act.wait_ge(*full_of(g, "up", hf, m))
                    if n >= 3:
                        act.wait_ge(down_done.sem, down_done.at(g, n - 2))
                    dst = gel if m else hid
                    act.activation(dst[:, n % 3, :], bank(("up", hf, m)), ACT.Gelu) \
                        .then_inc(emptied("up", hf, m), 1)

                for m in range(BLKS):
                    gelu(0, m)
                act.wait_ge(down_done.sem, down_done.at(g, BLKS))
                act.activation(half(ffnT, 0), ps[:, BANK_Y, :], ACT.Copy).then_inc(y_evac.sem, 1)
                for c in range(NC_SEQ):
                    if c == 0:
                        gelu(1, 0)
                        gelu(1, 1)
                    act.wait_ge(d_full.sem, d_full.at(g, c + 1))
                    act.activation(delta[:], ps[:, BANK_D, 0:SEQ * VD].rearrange("p (b v) -> p b v", v=VD),
                                   ACT.Copy).then_inc(d_ready.sem, 1)
                    act.wait_ge(o_full.sem, o_full.at(g, c + 1))
                    act.activation(bseq(o, c), ps[:, BANK_O, 0:SEQ * VD].rearrange("p (b v) -> p b v", v=VD),
                                   ACT.Copy).then_inc(o_ready.sem, 1)
                    if c + 2 < BLKS:
                        gelu(1, c + 2)
                act.wait_ge(o_ready.sem, o_ready.at(g, NC_SEQ))
                act.activation(osq[:], o[:], ACT.Square, scale=VD ** -0.5).then_inc(osq_ready.sem, 1)
                act.wait_ge(down_done.sem, down_done.at(g, 2 * BLKS))
                act.activation(half(ffnT, 1), ps[:, BANK_Y, :], ACT.Copy).then_inc(y_evac.sem, 1)
                for hf in range(2):
                    act.wait_ge(*full_of(g, "h2T", hf))
                    act.activation(half(h2T, hf), bank(("h2T", hf)), ACT.Identity,
                                   scale=vecs[:, V_LN2G:V_LN2G + 1], bias=vecs[:, V_LN2B:V_LN2B + 1]) \
                        .then_inc(emptied("h2T", hf), 1)
                for hf in range(2):
                    act.wait_ge(*full_of(g, "w2", hf))
                    act.activation(half(gelT, hf), bank(("w2", hf)), ACT.Gelu, bias=vecs[:, V_B2:V_B2 + 1]) \
                        .then_inc(emptied("w2", hf), 1)
                assert chain[0] == act_chain.per, chain[0]

        @block.vector
        def _(dve):
            values = (LN_EPS, EPS, KD * EPS, 1.0, -0.5, float(TOPK))
            for i, v in enumerate(values):
                dve.memset(k_(i), v)
            dve.memset(cum[:], 0.0)
            dve.memset(raw[:], 0.0)
            for b in range(RING):
                dve.memset(spare[:, b:b + 1], 0.0).then_inc(free[b].sem, 1)
            dve.memset(spare[:, 4:5], 0.0).then_inc(y_stored.sem, 1)
            dve.memset(spare[:, 5:6], 0.0).then_inc(cst_ready.sem, 1)
            dve.wait_ge(loaded.sem, 160)
            dve.tensor_scalar(wproj[:], wproj_raw[:], vecs[:, V_RMS:V_RMS + 1], None, ALU.mult)
            dve.tensor_scalar(wo[:, 0, :], wo_raw[:, 0, :], vecs[:, V_ON0:V_ON0 + 1], None, ALU.mult)
            dve.tensor_scalar(wo[:, 1, :], wo_raw[:, 1, :], vecs[:, V_ON1:V_ON1 + 1], None, ALU.mult)
            dve.tensor_copy(ident_b[:], ident)
            dve.tensor_copy(sel[:], sel_f[:]).then_inc(cst_ready.sem, 1)
            dve.wait_ge(cst_ready.sem, 3)
            dve.tensor_scalar(neg_a[:], exp_a[:], -1.0, None, ALU.mult).then_inc(cst_ready.sem, 1)
            dve.wait_ge(cst_ready.sem, 4)
            with dve.Fori(0, groups) as g:
                chain = [0]

                def link(ins):
                    chain[0] += 1
                    ins.then_inc(dve_chain.sem, 1)
                    dve.wait_ge(dve_chain.sem, dve_chain.at(g, chain[0]))

                def product(hf, m):
                    n = hf * BLKS + m
                    dve.wait_ge(*copied(g, "up", hf, m))
                    dve.wait_ge(*full_of(g, "gate", hf, m))
                    dve.tensor_tensor(hid[:, n % 3, :], gel[:, n % 3, :], bank(("gate", hf, m)), ALU.mult) \
                        .then_inc(emptied("gate", hf, m), 1)

                dve.wait_ge(x_loaded.sem, x_loaded.at(g, 16))
                for t in range(TILES - 1):
                    dve.bn_stats(st[:, t, :], xin[:, t, :])
                link(dve.bn_stats(st[:, TILES - 1, :], xin[:, TILES - 1, :]))
                dve.memset(state[:], 0.0).then_inc(s_ready.sem, 1)
                for t in range(TILES):
                    last = dve.bn_aggr(mv[:, t, :], st[:, t, :])
                last.then_inc(stats1.sem, 1)
                dve.tensor_copy(lane_t[:], cst[:, C_EYE:].rearrange("p (j i) -> p j i", i=C))
                dve.wait_ge(rstd1.sem, rstd1.at(g, 1))
                dve.wait_ge(stats1.sem, stats1.at(g, 1))
                for t in range(TILES):
                    last = dve.tensor_scalar(xn[:, t, :], xin[:, t, :], mv[:, t, 0:1], rstd[:, t:t + 1],
                                             ALU.subtract, ALU.mult)
                last.then_inc(xn_ready.sem, 1)
                dve.wait_ge(xn_ready.sem, xn_ready.at(g, 1))
                for t in range(TILES):
                    last = dve.tensor_scalar(xs[:, t, :], xn[:, t, :], rs2[:, t:t + 1], None, ALU.mult)
                last.then_inc(xn_ready.sem, 1)

                dve.wait_ge(rms_ready.sem, rms_ready.at(g, 1))
                dve.wait_ge(*copied(g, "xsT", 1))
                dve.tensor_tensor(hn[:], hT[:], rr[:, 0, :], ALU.mult).then_inc(hn_ready.sem, 1)

                logits = bank(("router",))[:, 0:TILES * E].rearrange("p (t e) -> p t e", e=E)
                dve.wait_ge(*full_of(g, "router"))
                link(dve.tensor_reduce(lmax[:], logits, AX.X, ALU.max))
                dve.tensor_tensor(lsh[:], logits, bc_last(lmax[:, :], E), ALU.subtract) \
                    .then_inc(emptied("router"), 1)
                dve.wait_ge(*full_of(g, "ab"))
                dve.tensor_tensor(zab[:], bank(("ab",))[:, 0:TILES * 2 * H].rearrange("p (t n) -> p t n", n=2 * H),
                                  bc_mid(rowb[:, 0:2 * H], TILES), ALU.add).then_inc(emptied("ab"), 1)
                dve.wait_ge(*copied(g, "ab"))
                dve.wait_ge(zexp_ready.sem, zexp_ready.at(g, 1))
                dve.scalar_tensor_tensor(out=znum[:], in0=zab[:, :, H:2 * H], scalar=0.0,
                                         in1=zexp[:, :, H:2 * H], op0=ALU.is_ge, op1=ALU.max)
                link(dve.tensor_scalar(zden[:], zexp[:, :, H:2 * H], 1.0, None, ALU.add))
                link(dve.reciprocal(zrec[:], zden[:]))
                link(dve.tensor_tensor(zbeta[:], znum[:], zrec[:], ALU.mult))
                dve.tensor_copy(gb[:, 1], bc_last(zbeta[:, :, :], C))
                dve.wait_ge(zexp_ready.sem, zexp_ready.at(g, 2))
                link(dve.scalar_tensor_tensor(out=zsp[:], in0=zab[:, :, 0:H], scalar=0.0, in1=zln[:],
                                              op0=ALU.max, op1=ALU.add))
                link(dve.tensor_tensor(zg[:], zsp[:], bc_mid(neg_a[:, :], TILES), ALU.mult))
                dve.tensor_scalar(gb[:, 0], bc_last(zg[:, :, :], C), G_LEAST, None, ALU.max) \
                    .then_inc(gb_ready.sem, 1)

                dve.wait_ge(er_ready.sem, er_ready.at(g, 1))
                link(dve.tensor_reduce(esum[:], er[:], AX.X, ALU.add))
                dve.reciprocal(erec[:], esum[:])
                for t in range(TILES):
                    last = dve.max(top8[:, t, :], er[:, t, :])
                link(last)
                thr = top8[:, :, TOPK - 1:TOPK].broadcast_to([P, TILES, E])
                dve.tensor_tensor(gt[:], er[:], thr, ALU.is_gt)
                link(dve.tensor_tensor(cum[:, 0, :, 8:], er[:], thr, ALU.is_equal))
                dve.tensor_reduce(ngt[:], gt[:], AX.X, ALU.add)
                at_ = 0
                for s, to in ((1, 1), (2, 2), (4, 1), (8, 2)):
                    link(dve.tensor_tensor(cum[:, to, :, 8:], cum[:, at_, :, 8:], cum[:, at_, :, 8 - s:8 + E - s],
                                           ALU.add))
                    at_ = to
                link(dve.tensor_tensor(cnt[:], cum[:, at_, :, 8:], bc_last(ngt[:, :], E), ALU.add))
                link(dve.scalar_tensor_tensor(out=keep[:], in0=cnt[:], scalar=float(TOPK), in1=cum[:, 0, :, 8:],
                                              op0=ALU.is_le, op1=ALU.mult))
                link(dve.tensor_tensor(keep2[:], keep[:], gt[:], ALU.add))
                link(dve.tensor_tensor(gun[:], keep2[:], er[:], ALU.mult))
                dve.tensor_tensor(gfull[:], gun[:], bc_last(erec[:, :], E), ALU.mult).then_inc(gate_ready.sem, 1)

                for b4 in range(4):
                    dve.wait_ge(*copied(g, "qkv", b4, 0))
                    dve.wait_ge(*copied(g, "qkv", b4, 1))
                    cv = conv[:, b4, :].rearrange("p (s t) -> p s t", t=T)
                    for i in range(PAD):
                        w = vecs[:, V_CONV + TAPS * b4 + i:V_CONV + TAPS * b4 + i + 1]
                        ins = dve.scalar_tensor_tensor(out=cv, in0=raw[:, b4, :, i:i + T], scalar=w, in1=cv,
                                                       op0=ALU.mult, op1=ALU.add)
                        if i < PAD - 1:
                            link(ins)
                    ins.then_inc(conv_ready.sem, 1)

                for hf in range(2):
                    dve.wait_ge(*full_of(g, "grow", hf))
                    dve.transpose(gcol[:, 16 * hf:16 * hf + 16, :], bank(("grow", hf)).rearrange("p (c i) -> p c i", i=C)) \
                        .then_inc(emptied("grow", hf), 1)
                dve.wait_ge(*copied(g, "grow", 0))
                dve.wait_ge(*copied(g, "grow", 1))
                dve.tensor_tensor(mcum[:], gcol[:], bc_mid(cst[:, C_UPTO:C_UPTO + C], NCH), ALU.mult) \
                    .then_inc(mcum_ready.sem, 1)
                for v2 in range(2):
                    dve.wait_ge(act_ready.sem, act_ready.at(g, 3 + v2))
                    dve.transpose(vtok[:, :, v2 * 32:v2 * 32 + 32], act4[:, 2 + v2, :].rearrange("p (c i) -> p c i", i=C)) \
                        .then_inc(vtok_ready.sem, 1)
                dve.wait_ge(*copied(g, "brow", 1))
                dve.transpose(bcol[:], brow[:])
                for b2 in range(2):
                    dve.wait_ge(rl2_ready.sem, rl2_ready.at(g, b2 + 1))
                    dve.tensor_tensor(kq[:, 1 - b2, :], act4[:, b2, :], rr[:, b2, :], ALU.mult) \
                        .then_inc(kq_ready.sem, 1)
                dve.wait_ge(kq_ready.sem, kq_ready.at(g, 2))
                dve.transpose(kcol[:], kq[:, 0, :].rearrange("p (c i) -> p c i", i=C)).then_inc(kcol_ready.sem, 1)
                dve.wait_ge(mask_ready.sem, mask_ready.at(g, 2))
                for q in range(4):
                    dve.wait_ge(*full_of(g, "pairs", q))
                    pr = bank(("pairs", q)).rearrange("p (c n) -> p c n", n=2 * C)
                    dve.tensor_tensor(at[:, 8 * q:8 * q + 8, :], pr[:, :, 0:C], am2[:, 8 * q:8 * q + 8, :], ALU.mult) \
                        .then_inc(at_ready.sem, 1)
                    dve.tensor_tensor(pt[:, 8 * q:8 * q + 8, :], pr[:, :, C:2 * C], pmask[:, 8 * q:8 * q + 8, :],
                                      ALU.mult).then_inc(emptied("pairs", q), 1)

                dve.wait_ge(lane_ready.sem, lane_ready.at(g, 64))
                for j in range(C - 1):
                    m = lane_m[:, 0:(j + 1) * (C - 1 - j)].rearrange("p (l i) -> p l i", i=C - 1 - j)
                    link(dve.tensor_tensor(m, bc_mid(lane_a[:, j, j + 1:C], j + 1),
                                           lane_t[:, 0:j + 1, j:j + 1].broadcast_to([P, j + 1, C - 1 - j]), ALU.mult))
                    ins = dve.tensor_tensor(lane_t[:, 0:j + 1, j + 1:C], lane_t[:, 0:j + 1, j + 1:C], m, ALU.subtract)
                    if j < C - 2:
                        link(ins)
                    if j % 3 == 2 and j // 3 + 1 < BLKS:
                        product(0, j // 3 + 1)
                ins.then_inc(inv_ready.sem, 1)
                dve.wait_ge(tt_loaded.sem, tt_loaded.at(g, 64))
                dve.tensor_tensor(ttb[:], ttb0[:], bcol[:], ALU.mult).then_inc(ttb_ready.sem, 1)

                for c in range(NC_SEQ):
                    dve.wait_ge(ks_full.sem, ks_full.at(g, c + 1))
                    dve.tensor_tensor(resid[:], bseq(vtok, c), ps[:, BANK_KS, 0:SEQ * VD]
                                      .rearrange("p (b v) -> p b v", v=VD), ALU.subtract).then_inc(r_ready.sem, 1)
                    dve.wait_ge(s_ready.sem, s_ready.at(g, c + 1))
                    link(dve.tensor_tensor(sdec[:], state[:], bseq(fromst, c)[:, :, C - 1:C]
                                           .broadcast_to([P, SEQ, VD]), ALU.mult))
                    product(1, c + 1)
                    dve.wait_ge(ds_full.sem, ds_full.at(g, c + 1))
                    dve.tensor_tensor(state[:], sdec[:], ps[:, BANK_D, 0:SEQ * VD]
                                      .rearrange("p (b v) -> p b v", v=VD), ALU.add).then_inc(s_ready.sem, 1)

                dve.wait_ge(osq_ready.sem, osq_ready.at(g, 1))
                dve.tensor_reduce(oms[:], osq[:], AX.X, ALU.add).then_inc(oms_ready.sem, 1)
                dve.wait_ge(orr_ready.sem, orr_ready.at(g, 1))
                link(dve.tensor_tensor(on[:], o[:], bc_last(orr[:, :], VD), ALU.mult))
                for v2 in range(2):
                    link(dve.transpose(oT[:, v2, :].rearrange("p (c i) -> p c i", i=C), on[:, :, v2 * 32:v2 * 32 + 32]))
                    dve.tensor_tensor(og[:, v2, :], oT[:, v2, :], ogate[:, v2, :], ALU.mult).then_inc(og_ready.sem, 1)

                for hf in range(2):
                    dve.wait_ge(*full_of(g, "enc", hf))
                    dve.tensor_tensor(x2[:, 4 * hf:4 * hf + 4, :], bank(("enc", hf)).rearrange("p (t d) -> p t d", d=P),
                                      xn[:, 4 * hf:4 * hf + 4, :], ALU.add).then_inc(emptied("enc", hf), 1)
                    dve.wait_ge(*copied(g, "enc", hf))
                    for t in range(4 * hf, 4 * hf + 4):
                        ins = dve.bn_stats(st[:, t, :], x2[:, t, :])
                link(ins)
                dve.memset(spare[:, 6:7], 0.0)
                for t in range(TILES):
                    last = dve.bn_aggr(mv[:, t, :], st[:, t, :])
                last.then_inc(stats2.sem, 1)
                dve.wait_ge(rstd2.sem, rstd2.at(g, 1))
                dve.wait_ge(stats2.sem, stats2.at(g, 1))
                for t in range(TILES):
                    last = dve.tensor_scalar(h2[:, t, :], x2[:, t, :], mv[:, t, 0:1], rstd[:, t:t + 1],
                                             ALU.subtract, ALU.mult)
                last.then_inc(h2_ready.sem, 1)
                dve.wait_ge(*copied(g, "w2", 0))
                dve.wait_ge(*copied(g, "w2", 1))
                dve.wait_ge(y_evac.sem, y_evac.at(g, 2))
                dve.tensor_tensor(sumT[:], gelT[:], ffnT[:], ALU.add).then_inc(sumT_ready.sem, 1)
                dve.wait_ge(xx2_ready.sem, xx2_ready.at(g, 1))
                dve.wait_ge(y_stored.sem, y_stored.at(g, 0))
                for hf in range(2):
                    dve.wait_ge(*full_of(g, "final", hf))
                    dve.tensor_tensor(yout[:, 4 * hf:4 * hf + 4, :], bank(("final", hf)).rearrange("p (t d) -> p t d", d=P),
                                      xx2[:, 4 * hf:4 * hf + 4, :], ALU.add).then_inc(emptied("final", hf), 1)
                assert chain[0] == dve_chain.per, chain[0]

        @block.tensor
        def _(pe):
            pe.wait_ge(loaded.sem, 160)
            pe.wait_ge(cst_ready.sem, 4)
            with pe.Fori(0, groups) as g:
                def one(job, lhs, rhs):
                    pe.wait_ge(*room(g, *job))
                    pe.matmul(bank(job), lhs, rhs, start=True, stop=True).then_inc(filled(*job), 1)

                def turn(job, tiles, ident_, dst=None):
                    pe.wait_ge(*room(g, *job))
                    for n, t in enumerate(tiles):
                        ins = pe.transpose(bank(job)[:, n * P:(n + 1) * P], t, ident_)
                    ins.then_inc(filled(*job), 1)

                def hold():
                    pe.ldweights(ident_b[:], tile_position=(0, 0))

                def heads(b, n, out_bank, width, lhs, rhs, start, stop):
                    for h in range(H):
                        r = slice(h * C, (h + 1) * C)
                        ins = pe.matmul(ps[r, out_bank, n * width:(n + 1) * width], lhs(r), rhs(r),
                                        start=start, stop=stop, skip_group_check=True)
                    return ins

                pe.wait_ge(*group_before(g))
                for name, src, k in (("xnT", xn, 1), ("xsT", xs, 2)):
                    pe.wait_ge(xn_ready.sem, xn_ready.at(g, k))
                    for hf in range(2):
                        turn((name, hf), [src[:, t, :] for t in range(4 * hf, 4 * hf + 4)], ident)
                for hf in range(2):
                    pe.wait_ge(hsq_ready.sem, hsq_ready.at(g, hf + 1))
                    one(("rms", hf), cst[:, C_MEAN:C_MEAN + P], half(sq[:, 0, :], hf))
                pe.wait_ge(*copied(g, "xnT", 1))
                pe.wait_ge(*room(g, "router"))
                for t in range(TILES):
                    ins = pe.matmul(bank(("router",))[:, t * E:(t + 1) * E], xnT[:, t * P:(t + 1) * P], wrout[:],
                                    start=True, stop=True)
                ins.then_inc(filled("router"), 1)
                pe.wait_ge(hn_ready.sem, hn_ready.at(g, 1))
                pe.wait_ge(*room(g, "ab"))
                for t in range(TILES):
                    ins = pe.matmul(bank(("ab",))[:, t * 2 * H:(t + 1) * 2 * H], hn[:, t * P:(t + 1) * P],
                                    wproj[:, W_AB:W_AB + 2 * H], start=True, stop=True)
                ins.then_inc(filled("ab"), 1)
                for b4 in range(4):
                    for hf in range(2):
                        one(("qkv", b4, hf), wproj[:, b4 * P:(b4 + 1) * P], half(hn, hf))
                for b2 in range(2):
                    for hf in range(2):
                        one(("ogate", b2, hf), wproj[:, W_G + b2 * P:W_G + (b2 + 1) * P], half(hn, hf))
                pe.wait_ge(gb_ready.sem, gb_ready.at(g, 1))
                for name, k in (("grow", 0), ("brow", 1)):
                    for hf in range(2):
                        turn((name, hf), [gb[:, k, t].rearrange("p h r -> p (h r)") for t in range(4 * hf, 4 * hf + 4)], ident)
                pe.wait_ge(mcum_ready.sem, mcum_ready.at(g, 1))
                mc = mcum[:].rearrange("p c i -> p (c i)")
                for name, col in (("decay", C_LATER), ("fromstart", C_HEAD)):
                    for hf in range(2):
                        one((name, hf), cst[:, col:col + P], half(mc, hf))
                for b2 in range(2):
                    pe.wait_ge(sq_ready.sem, sq_ready.at(g, b2 + 1))
                    col = (C_HEADQ, C_HEAD)[b2]
                    for hf in range(2):
                        one(("l2", b2, hf), cst[:, col:col + P], half(sq[:, b2, :], hf))
                pe.wait_ge(kq_ready.sem, kq_ready.at(g, 2))
                for q in range(4):
                    pe.wait_ge(*room(g, "pairs", q))
                    hold()
                    for n in range(8):
                        cols = slice((8 * q + n) * C, (8 * q + n + 1) * C)
                        ins = heads(None, n, job_at[("pairs", q)][0], 2 * C, lambda r: kq[r, 0, cols],
                                    lambda r: kq[r, :, cols], True, True)
                    ins.then_inc(filled("pairs", q), 1)
                pe.wait_ge(gparts_ready.sem, gparts_ready.at(g, 1))
                pe.wait_ge(*room(g, "gateT"))
                hold()
                gt_ps = ps[:, job_at[("gateT",)][0], :].bitcast(BF16)
                for t in range(TILES):
                    ins = pe.transpose(gt_ps[0:3 * E, t * P:(t + 1) * P], gparts[:, t].rearrange("p s e -> p (s e)"),
                                       ident_b[:])
                ins.then_inc(filled("gateT"), 1)

                def up(hf, m):
                    one(("up", hf, m), wup[:, m, :], half(xnT, hf))

                def gate(hf, m):
                    one(("gate", hf, m), sel[:, (m - 1) * P:m * P], half(gpT, hf))

                def down(hf, m):
                    n = hf * BLKS + m
                    if m == 0:
                        pe.wait_ge(*copied(g, "up", hf, 0))
                        if hf == 1:
                            pe.wait_ge(y_evac.sem, y_evac.at(g, 1))
                    else:
                        pe.wait_ge(*copied(g, "gate", hf, m))
                    pe.matmul(ps[:, BANK_Y, :], wdown[:, m, :], hid[:, n % 3, :], start=(m == 0),
                              stop=(m == BLKS - 1)).then_inc(down_done.sem, 1)

                def ffn_step(hf, m):
                    if m + 1 < BLKS:
                        up(hf, m + 1)
                        gate(hf, m + 1)
                    down(hf, m)

                pe.wait_ge(*copied(g, "gateT"))
                up(0, 0)
                for m in range(BLKS):
                    ffn_step(0, m)
                up(1, 0)
                ffn_step(1, 0)
                pe.wait_ge(scaled_ready.sem, scaled_ready.at(g, 3))
                pe.wait_ge(vtok_ready.sem, vtok_ready.at(g, 2))
                pe.wait_ge(ttb_ready.sem, ttb_ready.at(g, 1))
                for c in range(NC_SEQ):
                    pe.wait_ge(s_ready.sem, s_ready.at(g, c + 1))
                    hold()
                    for b in range(SEQ):
                        ins = heads(b, b, BANK_KS, VD, lambda r: kg[r, b * NC_SEQ + c, :],
                                    lambda r: state[r, b, :], True, True)
                    ins.then_inc(ks_full.sem, 1)
                    if c:
                        pe.wait_ge(o_ready.sem, o_ready.at(g, c))
                        hold()
                    for b in range(SEQ):
                        heads(b, b, BANK_O, VD, lambda r: qg[r, b * NC_SEQ + c, :],
                              lambda r: state[r, b, :], b == 0, False)
                    pe.wait_ge(r_ready.sem, r_ready.at(g, c + 1))
                    hold()
                    for b in range(SEQ):
                        ins = heads(b, b, BANK_D, VD, lambda r: ttb[r, b * NC_SEQ + c, :],
                                    lambda r: resid[r, b, :], True, True)
                    ins.then_inc(d_full.sem, 1)
                    ffn_step(1, c + 1)
                    pe.wait_ge(d_ready.sem, d_ready.at(g, c + 1))
                    hold()
                    for b in range(SEQ):
                        ins = heads(b, b, BANK_D, VD, lambda r: kend[r, b * NC_SEQ + c, :],
                                    lambda r: delta[r, b, :], True, True)
                    ins.then_inc(ds_full.sem, 1)
                    for b in range(SEQ):
                        ins = heads(b, b, BANK_O, VD, lambda r: pt[r, b * NC_SEQ + c, :],
                                    lambda r: delta[r, b, :], False, True)
                    ins.then_inc(o_full.sem, 1)
                pe.wait_ge(og_ready.sem, og_ready.at(g, 2))
                for hf in range(2):
                    pe.wait_ge(*room(g, "enc", hf))
                    for n in range(4):
                        t = 4 * hf + n
                        for v2 in range(2):
                            ins = pe.matmul(bank(("enc", hf))[:, n * P:(n + 1) * P], og[:, v2, t * P:(t + 1) * P],
                                            wo[:, v2, :], start=(v2 == 0), stop=(v2 == 1))
                    ins.then_inc(filled("enc", hf), 1)
                pe.wait_ge(h2_ready.sem, h2_ready.at(g, 1))
                for hf in range(2):
                    turn(("h2T", hf), [h2[:, t, :] for t in range(4 * hf, 4 * hf + 4)], ident)
                for hf in range(2):
                    pe.wait_ge(*copied(g, "h2T", hf))
                    one(("w2", hf), w2[:], half(h2T, hf))
                pe.wait_ge(sumT_ready.sem, sumT_ready.at(g, 1))
                for hf in range(2):
                    turn(("final", hf), [sumT[:, t * P:(t + 1) * P] for t in range(4 * hf, 4 * hf + 4)], ident)


def _constants():
    import numpy as np

    cst = np.zeros((P, C_COLS), np.float32)
    p = np.arange(P)
    head = (p[:, None] // C == p[None, :] // C).astype(np.float32)
    cst[:, C_IDENT:C_IDENT + P] = np.eye(P)
    cst[:, C_MEAN:C_MEAN + P] = 1.0 / P
    cst[:, C_HEAD:C_HEAD + P] = head
    cst[:, C_HEADQ:C_HEADQ + P] = head * KD
    cst[:, C_LATER:C_LATER + P] = head * (p[:, None] > p[None, :])
    cst[:, C_UPTO:C_UPTO + C] = p[:, None] % C <= np.arange(C)[None, :]
    cst[:, C_BEFORE:C_BEFORE + C] = p[:, None] % C < np.arange(C)[None, :]
    cst[:, C_EYE:] = np.eye(C).reshape(-1)
    sel = np.zeros((3, E, BLKS - 1, 2, P // 2), np.float32)
    for e in range(E):
        sel[:, e, e // 2, e % 2, :] = 1.0
    return cst, sel.reshape(3 * E, (BLKS - 1) * P)


def kernel(L0_attn_x, L0_attn_ln1_g, L0_attn_ln1_b, L0_attn_ln2_g, L0_attn_ln2_b, L0_attn_rms_in_w, L0_attn_Wq,
           L0_attn_Wk, L0_attn_Wv, L0_attn_conv_q_w, L0_attn_conv_k_w, L0_attn_conv_v_w, L0_attn_Wa,
           L0_attn_dt_bias, L0_attn_A_log, L0_attn_Wb, L0_attn_Wg, L0_attn_o_norm_w, L0_attn_Wo, L0_attn_W2,
           L0_attn_b2, L0_ffn_shared_up, L0_ffn_shared_down, L0_ffn_routed_up, L0_ffn_routed_down,
           L0_ffn_router_w):
    import numpy as np
    import concourse.bacc as bacc
    from concourse.bass_utils import run_bass_kernel_spmd

    def a(v):
        return np.asarray(v)

    cst, sel = _constants()

    def halves(w):
        n = w.shape[0]
        return w.reshape(n, H, 2, VD // 2).transpose(0, 2, 1, 3).reshape(n, 2 * P)

    wproj = np.concatenate([a(L0_attn_Wq), a(L0_attn_Wk), halves(a(L0_attn_Wv)), halves(a(L0_attn_Wg)),
                            a(L0_attn_Wa), a(L0_attn_Wb)], axis=1)
    ups = np.concatenate([a(L0_ffn_shared_up), a(L0_ffn_routed_up)], axis=0).reshape(BLKS * P, P)
    downs = np.concatenate([a(L0_ffn_shared_down), a(L0_ffn_routed_down)], axis=0)
    conv_v = halves(a(L0_attn_conv_v_w).transpose()).transpose()
    onorm = np.tile(a(L0_attn_o_norm_w).reshape(2, 1, VD // 2), (1, H, 1)).reshape(2, P)
    vecs = np.stack([a(L0_attn_ln1_g), a(L0_attn_ln1_b), a(L0_attn_ln2_g), a(L0_attn_ln2_b),
                     a(L0_attn_rms_in_w), onorm[0], onorm[1], a(L0_attn_b2)], axis=1)
    vecs = np.concatenate([vecs, a(L0_attn_conv_q_w), a(L0_attn_conv_k_w), conv_v[0:P], conv_v[P:]], axis=1)
    rowb = np.concatenate([a(L0_attn_dt_bias), np.zeros(H, np.float32), a(L0_attn_A_log)])
    arrays = {
        "x": a(L0_attn_x).reshape(-1, P),
        "consts": cst,
        "sel": sel,
        "wproj": wproj,
        "wup": ups.transpose().reshape(P, BLKS, P),
        "wdown": downs.transpose(0, 2, 1).reshape(BLKS, P, P).transpose(1, 0, 2),
        "wo": halves(a(L0_attn_Wo).transpose()).reshape(P, 2, P).transpose(2, 1, 0),
        "w2": a(L0_attn_W2),
        "router": a(L0_ffn_router_w).transpose(),
        "vecs": vecs,
        "rowb": np.broadcast_to(rowb, (P, 3 * H)),
    }
    arrays = {f"in_{k}_dram": np.ascontiguousarray(v) for k, v in arrays.items()}
    nc = bacc.Bacc("TRN2", target_bir_lowering=False, num_devices=1)
    args = [nc.dram_tensor(k, v.shape, mybir.dt.from_np(v.dtype), kind="ExternalInput").ap()
            for k, v in arrays.items()]
    out = nc.dram_tensor("out_dram", (arrays["in_x_dram"].shape[0], P), F32, kind="ExternalOutput").ap()
    scr_a = nc.dram_tensor("scratch_a_dram", (H, C, NCH, C), F32, kind="Internal").ap()
    scr_t = nc.dram_tensor("scratch_t_dram", (H, NCH, C, C), F32, kind="Internal").ap()
    build(nc, *args, out, scr_a, scr_t)
    r = run_bass_kernel_spmd(nc, [arrays], core_ids=[0])
    return r.results[0]["out_dram"].reshape(L0_attn_x.shape)
```

```python
from contextlib import ExitStack

import concourse.bass as bass
from concourse import mybir

F32 = mybir.dt.float32
BF16 = mybir.dt.bfloat16
ALU = mybir.AluOpType
ACT = mybir.ActivationFunctionType
AX = mybir.AxisListType

P = 128
T = 256
SEQ = 4
N = SEQ * T
TILES = N // P
HALF = 512
C = 32
NC_SEQ = T // C
NCH = N // C
H = 4
KD = 32
VD = 64
TAPS = 4
PAD = TAPS - 1
E = 16
TOPK = 4
BLKS = 9
LN_EPS = 1e-5
EPS = 1e-6
G_LEAST = -200.0

C_IDENT, C_MEAN, C_HEAD, C_HEADQ, C_LATER, C_UPTO, C_BEFORE = 0, 128, 256, 384, 512, 640, 672
C_COLS = C_BEFORE + C
W_Q, W_K, W_V, W_G, W_AB = 0, 128, 256, 512, 768
W_COLS = W_AB + 2 * H
(V_LN1G, V_LN1B, V_LN2G, V_LN2B, V_RMS, V_ON0, V_ON1, V_B2, V_CONV) = (0, 1, 2, 3, 4, 5, 6, 7, 8)
V_COLS = V_CONV + 4 * TAPS

RESIDUAL_AT, NORM2_AT = 8, 12
ENC_BEHIND, H2_BEHIND, W2_BEHIND = (0, 5), (1, 1), (1, 3)
GATES_AT = 6


def _jobs_a():
    jobs = [("xnT", 0), ("xnT", 1), ("xsT", 0), ("xsT", 1), ("rms", 0), ("rms", 1), ("router",), ("ab",)]
    jobs += [("qkv", b, hf) for b in range(4) for hf in range(2)]
    jobs += [(name, hf) for name in ("grow", "brow", "decay", "fromstart") for hf in range(2)]
    jobs += [("l2", b, hf) for b in range(2) for hf in range(2)]
    jobs += [("pairs", q) for q in range(4)] + [("gateT",)]
    for hf in range(2):
        jobs.append(("up", hf, 0))
        for m in range(BLKS):
            if m + 1 < BLKS:
                jobs += [("up", hf, m + 1), ("gate", hf, m + 1)]
            if (hf, m) == (0, GATES_AT):
                jobs += [("ogate", b, h2) for b in range(2) for h2 in range(2)]
    return jobs


JOBS_A = _jobs_a()
JOBS_B = [(name, hf) for name in ("enc", "h2T", "w2", "final") for hf in range(2)]
BANKS_A = (0, 1, 2)
BANK_Y, BANK_KS, BANK_D, BANK_O = 3, 4, 5, 6
BANKS_B = (7, BANK_KS)


def build(nc, x, consts, sel_in, wproj_in, wup_in, wdown_in, wo_in, w2_in, router_in, vecs_in, rowb_in,
          out, scr_a, scr_t):
    groups = x.shape[0] // N
    ctx = ExitStack()
    with ctx:
        def sb(name, shape, dt=F32):
            return ctx.enter_context(nc.sbuf_tensor(name, shape, dt))

        class Signal:

            def __init__(self, name, per, first=0):
                self.sem = ctx.enter_context(nc.semaphore(name))
                self.per, self.first = per, first

            def at(self, g, k):
                return g * self.per + (self.first + k)

        def chunks(ap):
            return ap.rearrange("p (c i) -> p c i", i=C)

        def tiles(ap):
            return ap.rearrange("p (t d) -> p t d", d=P)

        cst = sb("cst", [P, C_COLS])
        ident_b = sb("ident_b", [P, P], BF16)
        sel = sb("sel", [3 * E, (BLKS - 1) * P], BF16)
        wproj = sb("wproj", [P, W_COLS])
        wup = sb("wup", [P, BLKS, P])
        wdown = sb("wdown", [P, BLKS, P])
        wo = sb("wo", [P, 2, P])
        w2 = sb("w2", [P, P])
        wrout = sb("wrout", [P, E])
        vecs = sb("vecs", [P, V_COLS])
        rowb = sb("rowb", [P, 3 * H])
        neg_a = sb("neg_a", [P, H])
        exp_a = sb("exp_a", [P, H])
        spare = sb("spare", [P, 8])
        small = sb("small", [P, 8])
        K_LNEPS, K_EPS, K_EPSQ, K_ONE, K_MHALF = range(5)

        def k_(i):
            return small[:, i:i + 1]

        ident = cst[:, C_IDENT:C_IDENT + P]

        xin = sb("xin", [P, TILES, P])
        xn = sb("xn", [P, TILES, P])
        xs_ = sb("xs", [P, N])
        hT = sb("hT", [P, N])
        hn = sb("hn", [P, N])
        xnT = sb("xnT", [P, N])
        sq = sb("sq", [P, 2, N])
        rl = sb("rl", [P, 2, N])
        raw_ = sb("raw", [P, 4 * SEQ * (PAD + T)])
        conv = sb("conv", [P, 4, N])
        brow = sb("brow", [P, NCH, C])
        decay = sb("decay", [P, NCH, C])
        fromst = sb("fromst", [P, NCH, C])
        st = sb("st", [P, TILES, 6])
        mv = sb("mv", [P, TILES, 2])
        lnw = sb("lnw", [P, 4, TILES])
        rstd = sb("rstd", [P, TILES])
        rs2 = sb("rs2", [P, TILES])
        zab = sb("zab", [P, TILES, 2 * H])
        zabs = sb("zabs", [P, TILES, 2 * H])
        zexp = sb("zexp", [P, TILES, 2 * H])
        zln = sb("zln", [P, TILES, H])
        zden = sb("zden", [P, TILES, H])
        zrec = sb("zrec", [P, TILES, H])
        znum = sb("znum", [P, TILES, H])
        zsp = sb("zsp", [P, TILES, H])
        zbeta = sb("zbeta", [P, TILES, H])
        zg = sb("zg", [P, TILES, H])
        lmax = sb("lmax", [P, TILES])
        lsh = sb("lsh", [P, TILES, E])
        er = sb("er", [P, TILES, E])
        top8 = sb("top8", [P, TILES, 8])
        esum = sb("esum", [P, TILES])
        erec = sb("erec", [P, TILES])
        gt = sb("gt", [P, TILES, E])
        ngt = sb("ngt", [P, TILES])
        cum = sb("cum", [P, 3, TILES, 8 + E])
        cnt = sb("cnt", [P, TILES, E])
        keep = sb("keep", [P, TILES, E])
        keep2 = sb("keep2", [P, TILES, E])
        gun = sb("gun", [P, TILES, E])
        gfull = sb("gfull", [P, TILES, E])
        gres = sb("gres", [P, 2, TILES, E])
        gparts = sb("gparts", [P, TILES, 3, E], BF16)
        gpT = sb("gpT", [3 * E, N], BF16)
        gel = sb("gel", [P, 3, HALF])
        hid = sb("hid", [P, 3, HALF])
        xk = sb("xk", [P, TILES, P])
        xpn = sb("xpn", [P, TILES, P])
        ffnT = sb("ffnT", [P, N])
        ogate = sb("ogate", [P, 2, N])
        kg = sb("kg", [P, NCH, C])
        qg = sb("qg", [P, NCH, C])
        kend = sb("kend", [P, NCH, C])
        pt = sb("pt", [P, NCH, C])
        ttb = sb("ttb", [P, NCH, C])
        vtok = sb("vtok", [P, NCH, VD])
        egend = sb("egend", [P, NCH])
        state = sb("state", [P, SEQ, VD])
        sdec = sb("sdec", [P, SEQ, VD])
        resid = sb("resid", [P, SEQ, VD])
        delta = sb("delta", [P, SEQ, VD])
        o = sb("o", [P, NCH, VD])
        on = sb("on", [P, NCH, VD])
        og = sb("og", [P, 2, N])
        oms = sb("oms", [P, NCH])
        omr = sb("omr", [P, NCH])
        orr = sb("orr", [P, NCH])
        st2 = sb("st2", [P, TILES, 6])
        mv2 = sb("mv2", [P, TILES, 2])
        lnw2 = sb("lnw2", [P, TILES])
        rstd2 = sb("rstd2", [P, TILES])

        raw = raw_[:, :].rearrange("p (b s t) -> p b s t", s=SEQ, t=PAD + T)
        pmask, am, lane_m, lane_t = (raw_[:, n * N:(n + 1) * N] for n in range(4))
        pmask, am, lane_t = chunks(pmask), chunks(am), chunks(lane_t)
        xs, gcol, at = tiles(xs_[:, :]), chunks(xs_[:, :]), chunks(xs_[:, :])
        mcum = chunks(hT[:, :])
        ffn_a = hT
        gb = rl[:, :, :].rearrange("p k (t h r) -> p k t h r", h=H, r=C)
        lane_a, ttb0 = chunks(rl[:, 0, :]), chunks(rl[:, 1, :])
        kcol, bcol = chunks(sq[:, 0, :]), chunks(sq[:, 1, :])
        wproj_raw, sel_f = conv[:, 0, 0:W_COLS], conv[0:3 * E, 1, :]
        wo_raw = tiles(conv[:, 2, 0:2 * P])
        onf = on[:, :, :].rearrange("p c v -> p (c v)")
        of = o[:, :, :].rearrange("p c v -> p (c v)")
        x2, h2 = tiles(onf[:, 0:N]), tiles(onf[:, N:2 * N])
        h2T, gelT = of[:, 0:N], of[:, N:2 * N]
        ogf = og[:, :, :].rearrange("p a n -> p (a n)")
        xx2, sumT = tiles(ogf[:, 0:N]), ogf[:, N:2 * N]

        ps = ctx.enter_context(nc.psum_tensor("ps", [P, 8, 512], F32))

        loaded = Signal("weights_loaded", 0)
        cst_ready = Signal("constants_ready", 0)
        bank_at = {job: (BANKS_A[n % 3], n // 3) for n, job in enumerate(JOBS_A)}
        bank_at |= {job: (BANKS_B[n % 2], n // 2) for n, job in enumerate(JOBS_B)}
        uses = {b: sum(at_[0] == b for at_ in bank_at.values()) for b in (*BANKS_A, *BANKS_B)}
        full = {b: Signal(f"bank{b}_full", n) for b, n in uses.items()}
        free = {b: Signal(f"bank{b}_free", n, 1) for b, n in uses.items()}
        pool_a = Signal("pool_chain_a", 10)
        pool_b = Signal("pool_chain_b", 2)
        act_a = Signal("act_chain_a", 1)
        dve_a = Signal("dve_chain_a", 87)
        dve_b = Signal("dve_chain_b", 10)
        x_loaded = Signal("x_loaded", 16)
        y_stored = Signal("y_stored", 16, 1)
        stats1 = Signal("stats1_ready", 1)
        rstd1_ready = Signal("rstd1_ready", 1)
        xn_ready = Signal("xn_ready", 2)
        xpn_ready = Signal("xpn_ready", 1)
        ffn_ready = Signal("ffn_ready", 1)
        hsq_ready = Signal("hsq_ready", 2)
        rms_ready = Signal("rms_ready", 1)
        hn_ready = Signal("hn_ready", 1)
        er_ready = Signal("router_exp_ready", 1)
        gate_ready = Signal("gate_ready", 1)
        gparts_ready = Signal("gate_parts_ready", 1)
        zexp_ready = Signal("zexp_ready", 2)
        gb_ready = Signal("decay_beta_ready", 1)
        conv_ready = Signal("conv_ready", 4)
        act_ready = Signal("act_ready", 4)
        sq_ready = Signal("qk_squares_ready", 2)
        rl2_ready = Signal("qk_scale_ready", 2)
        kq_ready = Signal("kq_ready", 2)
        mcum_ready = Signal("mcum_ready", 1)
        mask_ready = Signal("masked_decay_ready", 2)
        at_ready = Signal("at_ready", 4)
        at_stored = Signal("at_stored", 16)
        lane_ready = Signal("lanes_loaded", 64)
        inv_ready = Signal("inverse_ready", 1)
        inv_stored = Signal("inverse_stored", 16)
        tt_loaded = Signal("tt_loaded", 64)
        ttb_ready = Signal("ttb_ready", 1)
        scaled_ready = Signal("scaled_kq_ready", 3)
        kcol_ready = Signal("kcol_ready", 1)
        down_done = Signal("down_done", 2 * BLKS)
        y_evac = Signal("ffn_copied", 2, 1)
        s_ready = Signal("state_ready", 1 + NC_SEQ)
        ks_full = Signal("ks_full", NC_SEQ)
        r_ready = Signal("resid_ready", NC_SEQ)
        d_full = Signal("delta_full", NC_SEQ)
        d_ready = Signal("delta_ready", NC_SEQ)
        o_full = Signal("o_full", NC_SEQ)
        o_ready = Signal("o_ready", NC_SEQ)
        ds_full = Signal("state_sum_full", NC_SEQ)
        osq_ready = Signal("o_squares_ready", 1)
        oms_ready = Signal("o_mean_ready", 1)
        orr_ready = Signal("o_scale_ready", 1)
        oT_ready = Signal("oT_ready", 2)
        og_ready = Signal("og_ready", 2)
        stats2 = Signal("stats2_ready", 1)
        rstd2_ready = Signal("rstd2_ready", 1)
        h2_ready = Signal("h2_ready", 1)
        sumT_ready = Signal("sumT_ready", 1)

        def bank(*job):
            return ps[:, bank_at[job][0], :]

        def room(g, *job):
            b, n = bank_at[job]
            return free[b].sem, free[b].at(g, n)

        def filled(*job):
            return full[bank_at[job][0]].sem

        def full_of(g, *job):
            b, n = bank_at[job]
            return full[b].sem, full[b].at(g, n + 1)

        def emptied(*job):
            return free[bank_at[job][0]].sem

        def copied(g, *job):
            b, n = bank_at[job]
            return free[b].sem, free[b].at(g, n + 1)

        def half(ap2d, hf):
            return ap2d[:, hf * HALF:(hf + 1) * HALF]

        def bc_mid(ap, n):
            return ap.unsqueeze(1).broadcast_to([ap.shape[0], n, ap.shape[-1]])

        def bc_last(ap, n):
            return ap.unsqueeze(len(ap.shape)).broadcast_to([*ap.shape, n])

        def bseq(t, c):
            return t[:, :, :].rearrange("p (b c) w -> p b c w", c=NC_SEQ)[:, :, c, :]

        def by_seq(b):
            return ps[:, b, 0:SEQ * VD].rearrange("p (b v) -> p b v", v=VD)

        last_p = groups - 1
        block = ctx.enter_context(nc.Block())

        @block.sync
        def _(sp):
            for dst, src in ((cst[:], consts), (sel_f, sel_in), (wproj_raw, wproj_in), (wo_raw, wo_in),
                             (w2[:], w2_in), (wrout[:], router_in), (vecs[:], vecs_in), (rowb[:], rowb_in),
                             (wup[:], wup_in), (wdown[:], wdown_in)):
                sp.dma_start(dst, src).then_inc(loaded.sem, 16)

            def load(g):
                sp.dma_start(xin[:], x[bass.ds(g * N, N), :].rearrange("(t p) d -> p t d", p=P)) \
                    .then_inc(x_loaded.sem, 16)

            def relayout(g):
                sp.wait_ge(at_ready.sem, at_ready.at(g, 4))
                sp.dma_start(scr_a.rearrange("h j c i -> (h j) (c i)"), at.rearrange("p c i -> p (c i)")) \
                    .then_inc(at_stored.sem, 16)
                sp.wait_ge(at_stored.sem, at_stored.at(g, 16))
                for h in range(H):
                    sp.dma_start(lane_a[h * C:(h + 1) * C, :, :], scr_a[h].rearrange("j c i -> c j i")) \
                        .then_inc(lane_ready.sem, 16)

            def relayout_back(g):
                sp.wait_ge(inv_ready.sem, inv_ready.at(g, 1))
                sp.dma_start(scr_t.rearrange("h c j i -> (h c) (j i)"), lane_t.rearrange("p j i -> p (j i)")) \
                    .then_inc(inv_stored.sem, 16)
                sp.wait_ge(inv_stored.sem, inv_stored.at(g, 16))
                for h in range(H):
                    sp.dma_start(ttb0[h * C:(h + 1) * C, :, :], scr_t[h].rearrange("c j i -> j c i")) \
                        .then_inc(tt_loaded.sem, 16)

            def store(p):
                sp.wait_ge(*copied(p, "final", 1))
                sp.dma_start(out[bass.ds(p * N, N), :].rearrange("(t p) d -> p t d", p=P), xx2) \
                    .then_inc(y_stored.sem, 16)

            load(0)
            relayout(0)
            relayout_back(0)
            sp.wait_ge(xpn_ready.sem, xpn_ready.at(0, 1))
            load(1)
            with sp.Fori(0, groups - 2) as p:
                relayout(p + 1)
                relayout_back(p + 1)
                sp.wait_ge(xpn_ready.sem, xpn_ready.at(p + 1, 1))
                load(p + 2)
                store(p)
            relayout(last_p)
            relayout_back(last_p)
            store(last_p - 1)
            store(last_p)
            sp.wait_ge(y_stored.sem, 16 * groups + 1)

        @block.gpsimd
        def _(pool):
            def rsqrt_into(dst, src, tmp, eps, link):
                link(pool.tensor_tensor(tmp, src, k_(eps).broadcast_to(list(src.shape)), ALU.add))
                return pool.tensor_tensor(dst, tmp, k_(K_MHALF).broadcast_to(list(src.shape)), ALU.pow)

            def front(g, link):
                pool.wait_ge(stats1.sem, stats1.at(g, 1))
                link(rsqrt_into(rstd[:, :], mv[:, :, 1], lnw[:, 0, :], K_LNEPS, link))
                link(pool.tensor_tensor(lnw[:, 1, :], mv[:, :, 1], rstd[:, :], ALU.mult))
                link(pool.tensor_tensor(lnw[:, 2, :], lnw[:, 1, :], rstd[:, :], ALU.mult))
                rsqrt_into(rs2[:, :], lnw[:, 2, :], lnw[:, 3, :], K_LNEPS, link).then_inc(rstd1_ready.sem, 1)

            def late(g, link):
                pool.wait_ge(gate_ready.sem, gate_ready.at(g, 1))
                one = k_(K_ONE).unsqueeze(2).broadcast_to([P, TILES, E])
                link(pool.tensor_tensor(gparts[:, :, 0, :], gfull[:], one, ALU.mult))
                link(pool.tensor_tensor(gres[:, 0], gfull[:], gparts[:, :, 0, :], ALU.subtract))
                link(pool.tensor_tensor(gparts[:, :, 1, :], gres[:, 0], one, ALU.mult))
                link(pool.tensor_tensor(gres[:, 1], gres[:, 0], gparts[:, :, 1, :], ALU.subtract))
                pool.tensor_tensor(gparts[:, :, 2, :], gres[:, 1], one, ALU.mult).then_inc(gparts_ready.sem, 1)
                pool.wait_ge(conv_ready.sem, conv_ready.at(g, 4))
                pool.wait_ge(*copied(g, "decay", 1))
                pool.tensor_tensor(pmask, decay[:], bc_mid(cst[:, C_UPTO:C_UPTO + C], NCH), ALU.mult) \
                    .then_inc(mask_ready.sem, 1)
                pool.wait_ge(*copied(g, "brow", 1))
                link(pool.tensor_tensor(am, decay[:], brow[:], ALU.mult))
                pool.tensor_tensor(am, am, bc_mid(cst[:, C_BEFORE:C_BEFORE + C], NCH), ALU.mult) \
                    .then_inc(mask_ready.sem, 1)

            def late2(g):
                pool.wait_ge(*copied(g, "fromstart", 1))
                pool.wait_ge(kq_ready.sem, kq_ready.at(g, 2))
                pool.tensor_tensor(kg[:], chunks(conv[:, 1, :]), fromst[:], ALU.mult).then_inc(scaled_ready.sem, 1)
                pool.tensor_tensor(qg[:], chunks(conv[:, 0, :]), fromst[:], ALU.mult).then_inc(scaled_ready.sem, 1)
                pool.wait_ge(kcol_ready.sem, kcol_ready.at(g, 1))
                pool.tensor_tensor(kend[:], kcol, bc_last(decay[:, :, C - 1], C), ALU.mult) \
                    .then_inc(scaled_ready.sem, 1)

            def residuals(p, g):
                pool.tensor_tensor(xk[:], xn[:], k_(K_ONE).unsqueeze(2).broadcast_to([P, TILES, P]), ALU.mult)
                pool.tensor_tensor(xpn[:], xin[:], xn[:], ALU.add).then_inc(xpn_ready.sem, 1)
                if p is not None:
                    pool.wait_ge(sumT_ready.sem, sumT_ready.at(p, 1))
                pool.wait_ge(y_evac.sem, y_evac.at(g, 2))
                pool.tensor_tensor(ffnT[:], ffn_a[:], k_(K_ONE).broadcast_to([P, N]), ALU.mult) \
                    .then_inc(ffn_ready.sem, 1)

            def out_norm(p, link):
                pool.wait_ge(oms_ready.sem, oms_ready.at(p, 1))
                rsqrt_into(orr[:], oms[:], omr[:], K_EPS, link).then_inc(orr_ready.sem, 1)

            def out_gate(p):
                for v2 in range(2):
                    pool.wait_ge(oT_ready.sem, oT_ready.at(p, v2 + 1))
                    pool.tensor_tensor(og[:, v2, :], og[:, v2, :], ogate[:, v2, :], ALU.mult) \
                        .then_inc(og_ready.sem, 1)

            def tail(p, link):
                pool.wait_ge(stats2.sem, stats2.at(p, 1))
                rsqrt_into(rstd2[:, :], mv2[:, :, 1], lnw2[:, :], K_LNEPS, link).then_inc(rstd2_ready.sem, 1)

            def sums(p):
                pool.wait_ge(*copied(p, "w2", 0))
                pool.wait_ge(*copied(p, "w2", 1))
                pool.tensor_tensor(sumT, gelT, ffnT[:], ALU.add).then_inc(sumT_ready.sem, 1)

            def round_(p, g):
                chain = {"a": 0, "b": 0}

                def link_a(ins):
                    chain["a"] += 1
                    ins.then_inc(pool_a.sem, 1)
                    pool.wait_ge(pool_a.sem, pool_a.at(g, chain["a"]))

                def link_b(ins):
                    chain["b"] += 1
                    ins.then_inc(pool_b.sem, 1)
                    pool.wait_ge(pool_b.sem, pool_b.at(p, chain["b"]))

                if g is not None:
                    front(g, link_a)
                    late(g, link_a)
                if p is not None:
                    out_norm(p, link_b)
                if g is not None:
                    late2(g)
                if p is not None:
                    out_gate(p)
                    tail(p, link_b)
                    sums(p)
                if g is not None:
                    residuals(p, g)
                    assert chain["a"] == pool_a.per, chain
                if p is not None:
                    assert chain["b"] == pool_b.per, chain

            round_(None, 0)
            with pool.Fori(0, groups - 1) as p:
                round_(p, p + 1)
            round_(last_p, None)

        @block.scalar
        def _(act):
            act.wait_ge(loaded.sem, 160)
            act.wait_ge(cst_ready.sem, 1)
            act.activation(exp_a[:], rowb[:, 2 * H:3 * H], ACT.Exp).then_inc(cst_ready.sem, 1)

            def project(g, b4):
                for hf in range(2):
                    act.wait_ge(*full_of(g, "qkv", b4, hf))
                    act.activation(raw[:, b4, 2 * hf:2 * hf + 2, PAD:PAD + T],
                                   bank("qkv", b4, hf).rearrange("p (s t) -> p s t", t=T), ACT.Copy)
                    w = vecs[:, V_CONV + TAPS * b4 + PAD:V_CONV + TAPS * b4 + TAPS]
                    act.activation(half(conv[:, b4, :], hf), bank("qkv", b4, hf), ACT.Copy, scale=w) \
                        .then_inc(emptied("qkv", b4, hf), 1)

            def exp_of(g, name, dst):
                for hf in range(2):
                    act.wait_ge(*full_of(g, name, hf))
                    act.activation(dst[:, 16 * hf:16 * hf + 16, :], chunks(bank(name, hf)), ACT.Exp) \
                        .then_inc(emptied(name, hf), 1)

            def front(g, c, link):
                if c == 1:
                    for hf in range(2):
                        act.wait_ge(*full_of(g, "xnT", hf))
                        act.activation(half(xnT, hf), bank("xnT", hf), ACT.Copy).then_inc(emptied("xnT", hf), 1)
                    for hf in range(2):
                        act.wait_ge(*full_of(g, "xsT", hf))
                        act.activation(half(hT, hf), bank("xsT", hf), ACT.Identity,
                                       scale=vecs[:, V_LN1G:V_LN1G + 1], bias=vecs[:, V_LN1B:V_LN1B + 1]) \
                            .then_inc(emptied("xsT", hf), 1)
                        act.wait_ge(*copied(g, "xsT", hf))
                        act.activation(half(sq[:, 0, :], hf), half(hT, hf), ACT.Square).then_inc(hsq_ready.sem, 1)
                if c == 2:
                    act.preload_act_table_set("natural_log_exp_and_others")
                    for hf in range(2):
                        act.wait_ge(*full_of(g, "rms", hf))
                        act.activation(half(rl[:, 0, :], hf), bank("rms", hf), ACT.Ln, bias=k_(K_EPS)) \
                            .then_inc(emptied("rms", hf), 1)
                    act.wait_ge(*copied(g, "rms", 0))
                    act.wait_ge(*copied(g, "rms", 1))
                    act.activation(rl[:, 0, :], rl[:, 0, :], ACT.Exp, scale=-0.5).then_inc(rms_ready.sem, 1)
                if c == 3:
                    act.wait_ge(*copied(g, "router"))
                    act.activation(er[:], lsh[:], ACT.Exp).then_inc(er_ready.sem, 1)
                    act.wait_ge(*copied(g, "ab"))
                    link(act.activation(zabs[:], zab[:], ACT.Abs))
                    act.activation(zexp[:], zabs[:], ACT.Exp, scale=-1.0).then_inc(zexp_ready.sem, 1)
                    act.wait_ge(zexp_ready.sem, zexp_ready.at(g, 1))
                    act.activation(zln[:], zexp[:, :, 0:H], ACT.Ln, bias=k_(K_ONE)).then_inc(zexp_ready.sem, 1)
                    project(g, 0)
                if c == 4:
                    project(g, 1)
                    project(g, 2)
                if c == 5:
                    project(g, 3)
                    for hf in range(2):
                        act.wait_ge(*full_of(g, "brow", hf))
                        act.activation(brow[:, 16 * hf:16 * hf + 16, :], chunks(bank("brow", hf)), ACT.Copy) \
                            .then_inc(emptied("brow", hf), 1)
                if c == 6:
                    exp_of(g, "decay", decay)
                    exp_of(g, "fromstart", fromst)
                if c == 7:
                    for b4 in range(4):
                        act.wait_ge(conv_ready.sem, conv_ready.at(g, b4 + 1))
                        act.activation(conv[:, b4, :], conv[:, b4, :], ACT.Silu).then_inc(act_ready.sem, 1)
                    for b2 in range(2):
                        act.wait_ge(act_ready.sem, act_ready.at(g, b2 + 1))
                        act.activation(sq[:, b2, :], conv[:, b2, :], ACT.Square).then_inc(sq_ready.sem, 1)

            def norms(g):
                act.preload_act_table_set("natural_log_exp_and_others")
                for b2 in range(2):
                    for hf in range(2):
                        act.wait_ge(*full_of(g, "l2", b2, hf))
                        act.activation(half(rl[:, b2, :], hf), bank("l2", b2, hf), ACT.Ln,
                                       bias=k_(K_EPSQ if b2 == 0 else K_EPS)).then_inc(emptied("l2", b2, hf), 1)
                    act.wait_ge(*copied(g, "l2", b2, 0))
                    act.wait_ge(*copied(g, "l2", b2, 1))
                    act.activation(rl[:, b2, :], rl[:, b2, :], ACT.Exp, scale=-0.5).then_inc(rl2_ready.sem, 1)
                act.wait_ge(*full_of(g, "gateT"))
                act.activation(gpT[:], ps[0:3 * E, bank_at[("gateT",)][0], :].bitcast(BF16), ACT.Copy) \
                    .then_inc(emptied("gateT"), 1)

            def gelu(g, hf, m):
                n = hf * BLKS + m
                act.wait_ge(*full_of(g, "up", hf, m))
                if n >= 3:
                    act.wait_ge(down_done.sem, down_done.at(g, n - 2))
                dst = gel if m else hid
                act.activation(dst[:, n % 3, :], bank("up", hf, m), ACT.Gelu).then_inc(emptied("up", hf, m), 1)

            def y_copy(g, hf):
                act.wait_ge(down_done.sem, down_done.at(g, (hf + 1) * BLKS))
                act.activation(half(ffn_a, hf), ps[:, BANK_Y, :], ACT.Copy).then_inc(y_evac.sem, 1)

            def gates(g):
                for b2 in range(2):
                    for hf in range(2):
                        act.wait_ge(*full_of(g, "ogate", b2, hf))
                        act.activation(half(ogate[:, b2, :], hf), bank("ogate", b2, hf), ACT.Silu) \
                            .then_inc(emptied("ogate", b2, hf), 1)

            def delta_copy(p, c):
                act.wait_ge(d_full.sem, d_full.at(p, c + 1))
                act.activation(delta[:], by_seq(BANK_D), ACT.Copy).then_inc(d_ready.sem, 1)

            def o_copy(p, c):
                act.wait_ge(o_full.sem, o_full.at(p, c + 1))
                act.activation(bseq(o, c), by_seq(BANK_O), ACT.Copy).then_inc(o_ready.sem, 1)

            def o_squares(p):
                act.wait_ge(o_ready.sem, o_ready.at(p, NC_SEQ))
                act.activation(on[:], o[:], ACT.Square, scale=VD ** -0.5).then_inc(osq_ready.sem, 1)

            def norm2(p):
                for hf in range(2):
                    act.wait_ge(*full_of(p, "h2T", hf))
                    act.activation(half(h2T, hf), bank("h2T", hf), ACT.Identity,
                                   scale=vecs[:, V_LN2G:V_LN2G + 1], bias=vecs[:, V_LN2B:V_LN2B + 1]) \
                        .then_inc(emptied("h2T", hf), 1)

            def gelu2(p):
                for hf in range(2):
                    act.wait_ge(*full_of(p, "w2", hf))
                    act.activation(half(gelT, hf), bank("w2", hf), ACT.Gelu, bias=vecs[:, V_B2:V_B2 + 1]) \
                        .then_inc(emptied("w2", hf), 1)

            def round_(p, g):
                chain = [0]

                def link(ins):
                    chain[0] += 1
                    ins.then_inc(act_a.sem, 1)
                    act.wait_ge(act_a.sem, act_a.at(g, chain[0]))

                for c in range(NC_SEQ):
                    if p is not None:
                        delta_copy(p, c)
                    if g is not None:
                        front(g, c, link)
                    if p is not None:
                        o_copy(p, c)
                if p is not None:
                    o_squares(p)
                if g is not None:
                    norms(g)
                    for m in range(BLKS):
                        gelu(g, 0, m)
                        if m == GATES_AT + 1:
                            gates(g)
                    y_copy(g, 0)
                    gelu(g, 1, 0)
                    gelu(g, 1, 1)
                if p is not None:
                    norm2(p)
                if g is not None:
                    gelu(g, 1, 2)
                    gelu(g, 1, 3)
                if p is not None:
                    gelu2(p)
                if g is not None:
                    for m in range(4, BLKS):
                        gelu(g, 1, m)
                    y_copy(g, 1)
                    assert chain[0] == act_a.per, chain

            round_(None, 0)
            with act.Fori(0, groups - 1) as p:
                round_(p, p + 1)
            round_(last_p, None)

        @block.vector
        def _(dve):
            for i, v in enumerate((LN_EPS, EPS, KD * EPS, 1.0, -0.5)):
                dve.memset(k_(i), v)
            dve.memset(cum[:], 0.0)
            for n, s in enumerate((*free.values(), y_stored, y_evac)):
                dve.memset(spare[:, n:n + 1], 0.0).then_inc(s.sem, 1)
            dve.memset(spare[:, 7:8], 0.0).then_inc(cst_ready.sem, 1)
            dve.wait_ge(loaded.sem, 160)
            dve.tensor_scalar(wproj[:], wproj_raw, vecs[:, V_RMS:V_RMS + 1], None, ALU.mult)
            dve.tensor_scalar(wo[:, 0, :], wo_raw[:, 0, :], vecs[:, V_ON0:V_ON0 + 1], None, ALU.mult)
            dve.tensor_scalar(wo[:, 1, :], wo_raw[:, 1, :], vecs[:, V_ON1:V_ON1 + 1], None, ALU.mult)
            dve.tensor_copy(ident_b[:], ident)
            dve.tensor_copy(sel[:], sel_f).then_inc(cst_ready.sem, 1)
            dve.wait_ge(cst_ready.sem, 3)
            dve.tensor_scalar(neg_a[:], exp_a[:], -1.0, None, ALU.mult).then_inc(cst_ready.sem, 1)
            dve.wait_ge(cst_ready.sem, 4)

            def convolve(g, b4, link):
                dve.wait_ge(*copied(g, "qkv", b4, 0))
                dve.wait_ge(*copied(g, "qkv", b4, 1))
                cv = conv[:, b4, :].rearrange("p (s t) -> p s t", t=T)
                for i in range(PAD):
                    w = vecs[:, V_CONV + TAPS * b4 + i:V_CONV + TAPS * b4 + i + 1]
                    ins = dve.scalar_tensor_tensor(out=cv, in0=raw[:, b4, :, i:i + T], scalar=w, in1=cv,
                                                   op0=ALU.mult, op1=ALU.add)
                    if i < PAD - 1:
                        link(ins)
                ins.then_inc(conv_ready.sem, 1)

            def select_experts(g, link):
                dve.wait_ge(er_ready.sem, er_ready.at(g, 1))
                link(dve.tensor_reduce(esum[:], er[:], AX.X, ALU.add))
                dve.reciprocal(erec[:], esum[:])
                for t in range(TILES):
                    last = dve.max(top8[:, t, :], er[:, t, :])
                link(last)
                thr = top8[:, :, TOPK - 1:TOPK].broadcast_to([P, TILES, E])
                dve.tensor_tensor(gt[:], er[:], thr, ALU.is_gt)
                link(dve.tensor_tensor(cum[:, 0, :, 8:], er[:], thr, ALU.is_equal))
                dve.tensor_reduce(ngt[:], gt[:], AX.X, ALU.add)
                at_ = 0
                for s, to in ((1, 1), (2, 2), (4, 1), (8, 2)):
                    link(dve.tensor_tensor(cum[:, to, :, 8:], cum[:, at_, :, 8:], cum[:, at_, :, 8 - s:8 + E - s],
                                           ALU.add))
                    at_ = to
                link(dve.tensor_tensor(cnt[:], cum[:, at_, :, 8:], bc_last(ngt[:, :], E), ALU.add))
                link(dve.scalar_tensor_tensor(out=keep[:], in0=cnt[:], scalar=float(TOPK), in1=cum[:, 0, :, 8:],
                                              op0=ALU.is_le, op1=ALU.mult))
                link(dve.tensor_tensor(keep2[:], keep[:], gt[:], ALU.add))
                link(dve.tensor_tensor(gun[:], keep2[:], er[:], ALU.mult))
                dve.tensor_tensor(gfull[:], gun[:], bc_last(erec[:, :], E), ALU.mult).then_inc(gate_ready.sem, 1)

            def decay_and_beta(g, link):
                dve.wait_ge(zexp_ready.sem, zexp_ready.at(g, 2))
                dve.scalar_tensor_tensor(out=znum[:], in0=zab[:, :, H:2 * H], scalar=0.0,
                                         in1=zexp[:, :, H:2 * H], op0=ALU.is_ge, op1=ALU.max)
                dve.tensor_scalar(zden[:], zexp[:, :, H:2 * H], 1.0, None, ALU.add)
                link(dve.scalar_tensor_tensor(out=zsp[:], in0=zab[:, :, 0:H], scalar=0.0, in1=zln[:],
                                              op0=ALU.max, op1=ALU.add))
                dve.reciprocal(zrec[:], zden[:])
                link(dve.tensor_tensor(zg[:], zsp[:], bc_mid(neg_a[:, :], TILES), ALU.mult))
                link(dve.tensor_tensor(zbeta[:], znum[:], zrec[:], ALU.mult))
                dve.tensor_copy(gb[:, 1], bc_last(zbeta[:, :, :], C))
                dve.tensor_scalar(gb[:, 0], bc_last(zg[:, :, :], C), G_LEAST, None, ALU.max) \
                    .then_inc(gb_ready.sem, 1)

            def front(g, c, link):
                if c == 0:
                    dve.wait_ge(x_loaded.sem, x_loaded.at(g, 16))
                    for t in range(TILES):
                        last = dve.bn_stats(st[:, t, :], xin[:, t, :])
                    link(last)
                    dve.memset(raw[:, :, :, 0:PAD], 0.0)
                    for t in range(TILES):
                        last = dve.bn_aggr(mv[:, t, :], st[:, t, :])
                    last.then_inc(stats1.sem, 1)
                if c == 1:
                    dve.wait_ge(rstd1_ready.sem, rstd1_ready.at(g, 1))
                    dve.wait_ge(stats1.sem, stats1.at(g, 1))
                    for t in range(TILES):
                        last = dve.tensor_scalar(xn[:, t, :], xin[:, t, :], mv[:, t, 0:1], rstd[:, t:t + 1],
                                                 ALU.subtract, ALU.mult)
                    last.then_inc(xn_ready.sem, 1)
                    dve.wait_ge(xn_ready.sem, xn_ready.at(g, 1))
                    for t in range(TILES):
                        last = dve.tensor_scalar(xs[:, t, :], xn[:, t, :], rs2[:, t:t + 1], None, ALU.mult)
                    last.then_inc(xn_ready.sem, 1)
                if c == 3:
                    logits = bank("router")[:, 0:TILES * E].rearrange("p (t e) -> p t e", e=E)
                    dve.wait_ge(*full_of(g, "router"))
                    link(dve.tensor_reduce(lmax[:], logits, AX.X, ALU.max))
                    dve.tensor_tensor(lsh[:], logits, bc_last(lmax[:, :], E), ALU.subtract) \
                        .then_inc(emptied("router"), 1)
                    dve.wait_ge(rms_ready.sem, rms_ready.at(g, 1))
                    dve.wait_ge(*copied(g, "xsT", 1))
                    dve.tensor_tensor(hn[:], hT[:], rl[:, 0, :], ALU.mult).then_inc(hn_ready.sem, 1)
                    dve.wait_ge(*full_of(g, "ab"))
                    dve.tensor_tensor(zab[:], bank("ab")[:, 0:TILES * 2 * H].rearrange("p (t n) -> p t n", n=2 * H),
                                      bc_mid(rowb[:, 0:2 * H], TILES), ALU.add).then_inc(emptied("ab"), 1)
                if c == 4:
                    dve.wait_ge(*copied(g, "ab"))
                    decay_and_beta(g, link)
                if c == 5:
                    convolve(g, 0, link)
                    for hf in range(2):
                        dve.wait_ge(*full_of(g, "grow", hf))
                        dve.transpose(gcol[:, 16 * hf:16 * hf + 16, :], chunks(bank("grow", hf))) \
                            .then_inc(emptied("grow", hf), 1)
                    select_experts(g, link)
                if c == 6:
                    dve.wait_ge(*copied(g, "grow", 0))
                    dve.wait_ge(*copied(g, "grow", 1))
                    dve.tensor_tensor(mcum, gcol, bc_mid(cst[:, C_UPTO:C_UPTO + C], NCH), ALU.mult) \
                        .then_inc(mcum_ready.sem, 1)
                    convolve(g, 1, link)
                if c == 7:
                    convolve(g, 2, link)
                    convolve(g, 3, link)

            def pairs(p, g):
                for b2 in range(2):
                    dve.wait_ge(rl2_ready.sem, rl2_ready.at(g, b2 + 1))
                    dve.tensor_tensor(conv[:, b2, :], conv[:, b2, :], rl[:, b2, :], ALU.mult) \
                        .then_inc(kq_ready.sem, 1)
                dve.wait_ge(kq_ready.sem, kq_ready.at(g, 2))
                dve.transpose(kcol, chunks(conv[:, 1, :])).then_inc(kcol_ready.sem, 1)
                dve.wait_ge(mask_ready.sem, mask_ready.at(g, 2))
                if p is not None:
                    dve.wait_ge(o_full.sem, o_full.at(p, NC_SEQ))
                for q in range(4):
                    dve.wait_ge(*full_of(g, "pairs", q))
                    pr = bank("pairs", q).rearrange("p (c n) -> p c n", n=2 * C)
                    eight = slice(8 * q, 8 * q + 8)
                    dve.tensor_tensor(at[:, eight, :], pr[:, :, C:2 * C], am[:, eight, :], ALU.mult) \
                        .then_inc(at_ready.sem, 1)
                    dve.tensor_tensor(pt[:, eight, :], pr[:, :, 0:C], pmask[:, eight, :],
                                      ALU.mult).then_inc(emptied("pairs", q), 1)

            def to_columns(g, link):
                link(dve.memset(lane_t, 0.0))
                link(dve.memset(raw_[:, 3 * N:4 * N:C + 1], 1.0))
                for v2 in range(2):
                    dve.wait_ge(act_ready.sem, act_ready.at(g, 3 + v2))
                    dve.transpose(vtok[:, :, v2 * 32:v2 * 32 + 32], chunks(conv[:, 2 + v2, :]))
                dve.wait_ge(*copied(g, "brow", 1))
                dve.transpose(bcol, brow[:])
                dve.wait_ge(*copied(g, "fromstart", 1))
                dve.tensor_copy(egend[:], fromst[:, :, C - 1])

            def product(g, hf, m):
                n = hf * BLKS + m
                dve.wait_ge(*copied(g, "up", hf, m))
                dve.wait_ge(*full_of(g, "gate", hf, m))
                dve.tensor_tensor(hid[:, n % 3, :], gel[:, n % 3, :], bank("gate", hf, m), ALU.mult) \
                    .then_inc(emptied("gate", hf, m), 1)

            def chunk_first(p, c, link):
                dve.wait_ge(ks_full.sem, ks_full.at(p, c + 1))
                dve.tensor_tensor(resid[:], bseq(vtok, c), by_seq(BANK_KS), ALU.subtract).then_inc(r_ready.sem, 1)
                dve.wait_ge(s_ready.sem, s_ready.at(p, c + 1))
                link(dve.tensor_tensor(sdec[:], state[:], bc_last(egend[:, c::NC_SEQ], VD), ALU.mult))

            def chunk_last(p, c):
                dve.wait_ge(ds_full.sem, ds_full.at(p, c + 1))
                dve.tensor_tensor(state[:], sdec[:], by_seq(BANK_D), ALU.add).then_inc(s_ready.sem, 1)

            def out_mean(p):
                dve.wait_ge(osq_ready.sem, osq_ready.at(p, 1))
                dve.tensor_reduce(oms[:], on[:], AX.X, ALU.add).then_inc(oms_ready.sem, 1)

            def out_turn(p, link):
                dve.wait_ge(orr_ready.sem, orr_ready.at(p, 1))
                link(dve.tensor_tensor(on[:], o[:], bc_last(orr[:, :], VD), ALU.mult))
                dve.wait_ge(y_stored.sem, y_stored.at(p, 0))
                for v2 in range(2):
                    dve.transpose(chunks(og[:, v2, :]), on[:, :, v2 * 32:v2 * 32 + 32]).then_inc(oT_ready.sem, 1)

            def residual(p, link):
                for hf in range(2):
                    four = slice(4 * hf, 4 * hf + 4)
                    dve.wait_ge(*full_of(p, "enc", hf))
                    ins = dve.tensor_tensor(x2[:, four, :], tiles(bank("enc", hf)), xk[:, four, :], ALU.add)
                link(ins)
                for t in range(TILES):
                    ins = dve.bn_stats(st2[:, t, :], x2[:, t, :])
                for hf in range(2):
                    four = slice(4 * hf, 4 * hf + 4)
                    dve.tensor_tensor(xx2[:, four, :], tiles(bank("enc", hf)), xpn[:, four, :], ALU.add) \
                        .then_inc(emptied("enc", hf), 1)
                dve.wait_ge(*copied(p, "enc", 0))
                dve.memset(spare[:, 0:1], 0.0)
                for t in range(TILES):
                    last = dve.bn_aggr(mv2[:, t, :], st2[:, t, :])
                last.then_inc(stats2.sem, 1)

            def norm2(p):
                dve.wait_ge(rstd2_ready.sem, rstd2_ready.at(p, 1))
                dve.wait_ge(stats2.sem, stats2.at(p, 1))
                for t in range(TILES):
                    last = dve.tensor_scalar(h2[:, t, :], x2[:, t, :], mv2[:, t, 0:1], rstd2[:, t:t + 1],
                                             ALU.subtract, ALU.mult)
                last.then_inc(h2_ready.sem, 1)

            def output(p):
                for hf in range(2):
                    four = slice(4 * hf, 4 * hf + 4)
                    dve.wait_ge(*full_of(p, "final", hf))
                    dve.tensor_tensor(xx2[:, four, :], tiles(bank("final", hf)), xx2[:, four, :], ALU.add) \
                        .then_inc(emptied("final", hf), 1)

            def inverse_step(j, link):
                m = lane_m[:, 0:(j + 1) * (C - 1 - j)].rearrange("p (l i) -> p l i", i=C - 1 - j)
                link(dve.tensor_tensor(m, bc_mid(lane_a[:, j, j + 1:C], j + 1),
                                       lane_t[:, 0:j + 1, j:j + 1].broadcast_to([P, j + 1, C - 1 - j]), ALU.mult))
                return dve.tensor_tensor(lane_t[:, 0:j + 1, j + 1:C], lane_t[:, 0:j + 1, j + 1:C], m,
                                         ALU.subtract)

            def round_(p, g):
                chain = {"a": 0, "b": 0}

                def link_a(ins):
                    chain["a"] += 1
                    ins.then_inc(dve_a.sem, 1)
                    dve.wait_ge(dve_a.sem, dve_a.at(g, chain["a"]))

                def link_b(ins):
                    chain["b"] += 1
                    ins.then_inc(dve_b.sem, 1)
                    dve.wait_ge(dve_b.sem, dve_b.at(p, chain["b"]))

                for c in range(NC_SEQ):
                    if p is not None:
                        chunk_first(p, c, link_b)
                    if g is not None:
                        front(g, c, link_a)
                    if p is not None:
                        chunk_last(p, c)
                if g is not None:
                    pairs(p, g)
                if p is not None:
                    out_mean(p)
                if g is not None:
                    to_columns(g, link_a)
                    product(g, 0, 1)
                if p is not None:
                    out_turn(p, link_b)
                if g is not None:
                    product(g, 0, 2)
                    dve.wait_ge(lane_ready.sem, lane_ready.at(g, 64))
                    for j in range(C - 1):
                        ins = inverse_step(j, link_a)
                        if j < C - 2:
                            link_a(ins)
                        else:
                            ins.then_inc(inv_ready.sem, 1)
                        if j % 2 == 0 and j // 2 + 3 < BLKS:
                            product(g, 0, j // 2 + 3)
                        if j == RESIDUAL_AT and p is not None:
                            residual(p, link_b)
                        if j == NORM2_AT and p is not None:
                            norm2(p)
                        if j % 2 == 1 and 0 < (j - 9) // 2 < BLKS - 1:
                            product(g, 1, (j - 9) // 2)
                        if j == C - 2:
                            product(g, 1, BLKS - 1)
                    if p is not None:
                        output(p)
                    dve.memset(state[:], 0.0).then_inc(s_ready.sem, 1)
                    dve.wait_ge(tt_loaded.sem, tt_loaded.at(g, 64))
                    dve.tensor_tensor(ttb[:], ttb0, bcol, ALU.mult).then_inc(ttb_ready.sem, 1)
                    assert chain["a"] == dve_a.per, chain
                else:
                    residual(p, link_b)
                    norm2(p)
                    output(p)
                if p is not None:
                    assert chain["b"] == dve_b.per, chain

            round_(None, 0)
            with dve.Fori(0, groups - 1) as p:
                round_(p, p + 1)
            round_(last_p, None)

        @block.tensor
        def _(pe):
            pe.wait_ge(loaded.sem, 160)
            pe.wait_ge(cst_ready.sem, 4)

            def one(g, job, lhs, rhs):
                pe.wait_ge(*room(g, *job))
                pe.matmul(bank(*job), lhs, rhs, start=True, stop=True).then_inc(filled(*job), 1)

            def turn(g, job, blocks):
                pe.wait_ge(*room(g, *job))
                for n, t in enumerate(blocks):
                    ins = pe.transpose(bank(*job)[:, n * P:(n + 1) * P], t, ident)
                ins.then_inc(filled(*job), 1)

            def hold():
                pe.ldweights(ident_b[:], tile_position=(0, 0))

            def heads(n, out_bank, width, lhs, rhs, start, stop):
                for h in range(H):
                    r = slice(h * C, (h + 1) * C)
                    ins = pe.matmul(ps[r, out_bank, n * width:(n + 1) * width], lhs(r), rhs(r),
                                    start=start, stop=stop, skip_group_check=True)
                return ins

            def project(g, b4):
                for hf in range(2):
                    one(g, ("qkv", b4, hf), wproj[:, b4 * P:(b4 + 1) * P], half(hn, hf))

            def front(g, c):
                if c == 1:
                    for name, src, k in (("xnT", xn, 1), ("xsT", xs, 2)):
                        pe.wait_ge(xn_ready.sem, xn_ready.at(g, k))
                        for hf in range(2):
                            turn(g, (name, hf), [src[:, t, :] for t in range(4 * hf, 4 * hf + 4)])
                if c == 2:
                    for hf in range(2):
                        pe.wait_ge(hsq_ready.sem, hsq_ready.at(g, hf + 1))
                        one(g, ("rms", hf), cst[:, C_MEAN:C_MEAN + P], half(sq[:, 0, :], hf))
                    pe.wait_ge(*copied(g, "xnT", 0))
                    pe.wait_ge(*copied(g, "xnT", 1))
                    pe.wait_ge(*room(g, "router"))
                    for t in range(TILES):
                        ins = pe.matmul(bank("router")[:, t * E:(t + 1) * E], xnT[:, t * P:(t + 1) * P], wrout[:],
                                        start=True, stop=True)
                    ins.then_inc(filled("router"), 1)
                if c == 3:
                    pe.wait_ge(hn_ready.sem, hn_ready.at(g, 1))
                    pe.wait_ge(*room(g, "ab"))
                    for t in range(TILES):
                        ins = pe.matmul(bank("ab")[:, t * 2 * H:(t + 1) * 2 * H], hn[:, t * P:(t + 1) * P],
                                        wproj[:, W_AB:W_AB + 2 * H], start=True, stop=True)
                    ins.then_inc(filled("ab"), 1)
                    project(g, 0)
                if c == 4:
                    project(g, 1)
                    project(g, 2)
                if c == 5:
                    project(g, 3)
                    pe.wait_ge(gb_ready.sem, gb_ready.at(g, 1))
                    for name, k in (("grow", 0), ("brow", 1)):
                        for hf in range(2):
                            turn(g, (name, hf), [gb[:, k, t].rearrange("p h r -> p (h r)")
                                                 for t in range(4 * hf, 4 * hf + 4)])
                if c == 6:
                    pe.wait_ge(mcum_ready.sem, mcum_ready.at(g, 1))
                    mc = mcum.rearrange("p c i -> p (c i)")
                    for name, col in (("decay", C_LATER), ("fromstart", C_HEAD)):
                        for hf in range(2):
                            one(g, (name, hf), cst[:, col:col + P], half(mc, hf))

            def pairs(g):
                for b2 in range(2):
                    pe.wait_ge(sq_ready.sem, sq_ready.at(g, b2 + 1))
                    col = (C_HEADQ, C_HEAD)[b2]
                    for hf in range(2):
                        one(g, ("l2", b2, hf), cst[:, col:col + P], half(sq[:, b2, :], hf))
                pe.wait_ge(kq_ready.sem, kq_ready.at(g, 2))
                for q in range(4):
                    pe.wait_ge(*room(g, "pairs", q))
                    hold()
                    for n in range(8):
                        cols = slice((8 * q + n) * C, (8 * q + n + 1) * C)
                        ins = heads(n, bank_at[("pairs", q)][0], 2 * C, lambda r: conv[r, 1, cols],
                                    lambda r: conv[r, 0:2, cols], True, True)
                    ins.then_inc(filled("pairs", q), 1)

            def turn_gates(g):
                pe.wait_ge(gparts_ready.sem, gparts_ready.at(g, 1))
                pe.wait_ge(*room(g, "gateT"))
                hold()
                gt_ps = bank("gateT").bitcast(BF16)
                for t in range(TILES):
                    ins = pe.transpose(gt_ps[0:3 * E, t * P:(t + 1) * P], gparts[:, t].rearrange("p s e -> p (s e)"),
                                       ident_b[:])
                ins.then_inc(filled("gateT"), 1)

            def up(g, hf, m):
                one(g, ("up", hf, m), wup[:, m, :], half(xnT, hf))

            def ffn_step(g, hf, m):
                if m + 1 < BLKS:
                    up(g, hf, m + 1)
                    one(g, ("gate", hf, m + 1), sel[:, m * P:(m + 1) * P], half(gpT, hf))
                n = hf * BLKS + m
                if m == 0:
                    pe.wait_ge(*copied(g, "up", hf, 0))
                    pe.wait_ge(y_evac.sem, y_evac.at(g, hf))
                else:
                    pe.wait_ge(*copied(g, "gate", hf, m))
                pe.matmul(ps[:, BANK_Y, :], wdown[:, m, :], hid[:, n % 3, :], start=(m == 0),
                          stop=(m == BLKS - 1)).then_inc(down_done.sem, 1)

            def out_gates(p, g):
                if p is not None:
                    pe.wait_ge(og_ready.sem, og_ready.at(p, 2))
                for b2 in range(2):
                    for hf in range(2):
                        one(g, ("ogate", b2, hf), wproj[:, W_G + b2 * P:W_G + (b2 + 1) * P], half(hn, hf))

            def chunk_first(p, c):
                if c == 0:
                    pe.wait_ge(free[BANK_KS].sem, free[BANK_KS].at(p, 0))
                    pe.wait_ge(scaled_ready.sem, scaled_ready.at(p, 3))
                    pe.wait_ge(ttb_ready.sem, ttb_ready.at(p, 1))
                pe.wait_ge(s_ready.sem, s_ready.at(p, c + 1))
                hold()
                for b in range(SEQ):
                    ins = heads(b, BANK_KS, VD, lambda r: kg[r, b * NC_SEQ + c, :],
                                lambda r: state[r, b, :], True, True)
                ins.then_inc(ks_full.sem, 1)
                if c:
                    pe.wait_ge(o_ready.sem, o_ready.at(p, c))
                    hold()
                for b in range(SEQ):
                    heads(b, BANK_O, VD, lambda r: qg[r, b * NC_SEQ + c, :], lambda r: state[r, b, :],
                          b == 0, False)
                pe.wait_ge(r_ready.sem, r_ready.at(p, c + 1))
                hold()
                for b in range(SEQ):
                    ins = heads(b, BANK_D, VD, lambda r: ttb[r, b * NC_SEQ + c, :],
                                lambda r: resid[r, b, :], True, True)
                ins.then_inc(d_full.sem, 1)

            def chunk_last(p, c):
                pe.wait_ge(d_ready.sem, d_ready.at(p, c + 1))
                hold()
                for b in range(SEQ):
                    ins = heads(b, BANK_D, VD, lambda r: kend[r, b * NC_SEQ + c, :],
                                lambda r: delta[r, b, :], True, True)
                ins.then_inc(ds_full.sem, 1)
                for b in range(SEQ):
                    ins = heads(b, BANK_O, VD, lambda r: pt[r, b * NC_SEQ + c, :],
                                lambda r: delta[r, b, :], False, True)
                ins.then_inc(o_full.sem, 1)

            def project_out(p):
                pe.wait_ge(og_ready.sem, og_ready.at(p, 2))
                for hf in range(2):
                    pe.wait_ge(*room(p, "enc", hf))
                    for n in range(4):
                        t = 4 * hf + n
                        for v2 in range(2):
                            ins = pe.matmul(bank("enc", hf)[:, n * P:(n + 1) * P], og[:, v2, t * P:(t + 1) * P],
                                            wo[:, v2, :], start=(v2 == 0), stop=(v2 == 1))
                    ins.then_inc(filled("enc", hf), 1)

            def turn_h2(p):
                pe.wait_ge(h2_ready.sem, h2_ready.at(p, 1))
                for hf in range(2):
                    turn(p, ("h2T", hf), [h2[:, t, :] for t in range(4 * hf, 4 * hf + 4)])

            def project_w2(p):
                for hf in range(2):
                    pe.wait_ge(*copied(p, "h2T", hf))
                    one(p, ("w2", hf), w2[:], half(h2T, hf))

            def turn_out(p):
                pe.wait_ge(sumT_ready.sem, sumT_ready.at(p, 1))
                for hf in range(2):
                    turn(p, ("final", hf), [sumT[:, t * P:(t + 1) * P] for t in range(4 * hf, 4 * hf + 4)])

            def round_(p, g):
                for c in range(NC_SEQ):
                    if p is not None:
                        chunk_first(p, c)
                    if g is not None:
                        front(g, c)
                    if p is not None:
                        chunk_last(p, c)
                if g is None:
                    project_out(p)
                    turn_h2(p)
                    project_w2(p)
                    turn_out(p)
                    return
                pairs(g)
                turn_gates(g)
                pe.wait_ge(*copied(g, "gateT"))
                for hf in range(2):
                    up(g, hf, 0)
                    for m in range(BLKS):
                        ffn_step(g, hf, m)
                        if p is not None and (hf, m) == ENC_BEHIND:
                            project_out(p)
                        if (hf, m) == (0, GATES_AT):
                            out_gates(p, g)
                        if p is not None and (hf, m) == H2_BEHIND:
                            turn_h2(p)
                        if p is not None and (hf, m) == W2_BEHIND:
                            project_w2(p)
                if p is not None:
                    turn_out(p)

            round_(None, 0)
            with pe.Fori(0, groups - 1) as p:
                round_(p, p + 1)
            round_(last_p, None)


def _constants():
    import numpy as np

    cst = np.zeros((P, C_COLS), np.float32)
    p = np.arange(P)
    head = (p[:, None] // C == p[None, :] // C).astype(np.float32)
    cst[:, C_IDENT:C_IDENT + P] = np.eye(P)
    cst[:, C_MEAN:C_MEAN + P] = 1.0 / P
    cst[:, C_HEAD:C_HEAD + P] = head
    cst[:, C_HEADQ:C_HEADQ + P] = head * KD
    cst[:, C_LATER:C_LATER + P] = head * (p[:, None] > p[None, :])
    cst[:, C_UPTO:C_UPTO + C] = p[:, None] % C <= np.arange(C)[None, :]
    cst[:, C_BEFORE:C_BEFORE + C] = p[:, None] % C < np.arange(C)[None, :]
    sel = np.zeros((3, E, BLKS - 1, 2, P // 2), np.float32)
    for e in range(E):
        sel[:, e, e // 2, e % 2, :] = 1.0
    return cst, sel.reshape(3 * E, (BLKS - 1) * P)


def kernel(L0_attn_x, L0_attn_ln1_g, L0_attn_ln1_b, L0_attn_ln2_g, L0_attn_ln2_b, L0_attn_rms_in_w, L0_attn_Wq,
           L0_attn_Wk, L0_attn_Wv, L0_attn_conv_q_w, L0_attn_conv_k_w, L0_attn_conv_v_w, L0_attn_Wa,
           L0_attn_dt_bias, L0_attn_A_log, L0_attn_Wb, L0_attn_Wg, L0_attn_o_norm_w, L0_attn_Wo, L0_attn_W2,
           L0_attn_b2, L0_ffn_shared_up, L0_ffn_shared_down, L0_ffn_routed_up, L0_ffn_routed_down,
           L0_ffn_router_w):
    import numpy as np
    import concourse.bacc as bacc
    from concourse.bass_utils import run_bass_kernel_spmd

    def a(v):
        return np.asarray(v)

    cst, sel = _constants()

    def halves(w):
        n = w.shape[0]
        return w.reshape(n, H, 2, VD // 2).transpose(0, 2, 1, 3).reshape(n, 2 * P)

    wproj = np.concatenate([a(L0_attn_Wq), a(L0_attn_Wk), halves(a(L0_attn_Wv)), halves(a(L0_attn_Wg)),
                            a(L0_attn_Wa), a(L0_attn_Wb)], axis=1)
    ups = np.concatenate([a(L0_ffn_shared_up), a(L0_ffn_routed_up)], axis=0).reshape(BLKS * P, P)
    downs = np.concatenate([a(L0_ffn_shared_down), a(L0_ffn_routed_down)], axis=0)
    conv_v = halves(a(L0_attn_conv_v_w).transpose()).transpose()
    onorm = np.tile(a(L0_attn_o_norm_w).reshape(2, 1, VD // 2), (1, H, 1)).reshape(2, P)
    vecs = np.stack([a(L0_attn_ln1_g), a(L0_attn_ln1_b), a(L0_attn_ln2_g), a(L0_attn_ln2_b),
                     a(L0_attn_rms_in_w), onorm[0], onorm[1], a(L0_attn_b2)], axis=1)
    vecs = np.concatenate([vecs, a(L0_attn_conv_q_w), a(L0_attn_conv_k_w), conv_v[0:P], conv_v[P:]], axis=1)
    rowb = np.concatenate([a(L0_attn_dt_bias), np.zeros(H, np.float32), a(L0_attn_A_log)])
    arrays = {
        "x": a(L0_attn_x).reshape(-1, P),
        "consts": cst,
        "sel": sel,
        "wproj": wproj,
        "wup": ups.transpose().reshape(P, BLKS, P),
        "wdown": downs.transpose(0, 2, 1).reshape(BLKS, P, P).transpose(1, 0, 2),
        "wo": halves(a(L0_attn_Wo).transpose()).reshape(P, 2, P).transpose(2, 1, 0),
        "w2": a(L0_attn_W2),
        "router": a(L0_ffn_router_w).transpose(),
        "vecs": vecs,
        "rowb": np.broadcast_to(rowb, (P, 3 * H)),
    }
    arrays = {f"in_{k}_dram": np.ascontiguousarray(v) for k, v in arrays.items()}
    nc = bacc.Bacc("TRN2", target_bir_lowering=False, num_devices=1)
    args = [nc.dram_tensor(k, v.shape, mybir.dt.from_np(v.dtype), kind="ExternalInput").ap()
            for k, v in arrays.items()]
    out = nc.dram_tensor("out_dram", (arrays["in_x_dram"].shape[0], P), F32, kind="ExternalOutput").ap()
    scr_a = nc.dram_tensor("scratch_a_dram", (H, C, NCH, C), F32, kind="Internal").ap()
    scr_t = nc.dram_tensor("scratch_t_dram", (H, NCH, C, C), F32, kind="Internal").ap()
    build(nc, *args, out, scr_a, scr_t)
    r = run_bass_kernel_spmd(nc, [arrays], core_ids=[0])
    return r.results[0]["out_dram"].reshape(L0_attn_x.shape)
```

```python
from contextlib import ExitStack

import concourse.bass as bass
from concourse import mybir

F32 = mybir.dt.float32
BF16 = mybir.dt.bfloat16
ALU = mybir.AluOpType
ACT = mybir.ActivationFunctionType
AX = mybir.AxisListType

P = 128
T = 256
SEQ = 4
N = SEQ * T
TILES = N // P
HALF = 512
C = 32
NC_SEQ = T // C
NCH = N // C
H = 4
KD = 32
VD = 64
TAPS = 4
PAD = TAPS - 1
E = 16
TOPK = 4
BLKS = 9
LN_EPS = 1e-5
EPS = 1e-6
G_LEAST = -200.0

C_IDENT, C_MEAN, C_HEAD, C_HEADQ, C_LATER, C_UPTO, C_BEFORE = 0, 128, 256, 384, 512, 640, 672
C_COLS = C_BEFORE + C
W_Q, W_K, W_V, W_G, W_AB = 0, 128, 256, 512, 768
W_COLS = W_AB + 2 * H
(V_LN1G, V_LN1B, V_LN2G, V_LN2B, V_RMS, V_ON0, V_ON1, V_B2, V_CONV) = (0, 1, 2, 3, 4, 5, 6, 7, 8)
V_COLS = V_CONV + 4 * TAPS

INV_IN_SLOTS = 4
TURN_AT, RESIDUAL_AT, NORM2_AT = (5, 7), 10, 14
STATS_AT, NORMALISE_AT = 20, 24
BLOCKS_IN_SLOT = (0, 0, 0, 0, 0, 0, 2, 2)
ENC_OFF, H2_OFF, W2_OFF = 3, 6, 8
STEPS = [(hf, m) for hf in range(2) for m in range(BLKS)]
FIRST_STEP = [sum(BLOCKS_IN_SLOT[:c]) for c in range(T // C + 1)]
IN_TAIL = FIRST_STEP[-1]
ENC_BEHIND, H2_BEHIND, W2_BEHIND = (min(IN_TAIL + n, 2 * BLKS - 1) for n in (ENC_OFF, H2_OFF, W2_OFF))
GATES_BEHIND = 2 * BLKS - 1
CLOCK_FIRST = (8, 6, 7, 5, 6, 6, 0, 4)
CLOCK_LAST = (8, 10, 8, 8, 8, 3, 0, 0)
CLOCK_ROUTER, CLOCK_AB = 0, 0


def _jobs_a():
    jobs = [("xnT", 0), ("xnT", 1), ("xsT", 0), ("xsT", 1), ("rms", 0), ("rms", 1), ("router",), ("ab",)]
    jobs += [("qkv", b, hf) for b in range(2) for hf in range(2)]
    jobs += [(name, hf) for name in ("grow", "brow", "decay", "fromstart") for hf in range(2)]
    jobs += [("qkv", 2, hf) for hf in range(2)]
    jobs += [("l2", b, hf) for b in range(2) for hf in range(2)]
    jobs += [("qkv", 3, hf) for hf in range(2)] + [("gateT",)]
    for n, (hf, m) in enumerate(STEPS):
        if n == FIRST_STEP[5]:
            jobs += [("pairs", q) for q in range(4)]
        jobs += [("up", hf, m), ("gate", hf, m)] if m else [("up", hf, m)]
    return jobs + [("ogate", b, hf) for b in range(2) for hf in range(2)]


JOBS_A = _jobs_a()
JOBS_B = [(name, hf) for name in ("enc", "h2T", "w2", "final") for hf in range(2)]
BANKS_A = (0, 1, 2)
BANK_Y, BANK_KS, BANK_D, BANK_O = 3, 4, 5, 6
BANKS_B = (7, BANK_KS)


def build(nc, x, consts, sel_in, wproj_in, wup_in, wdown_in, wo_in, w2_in, router_in, vecs_in, rowb_in,
          out, scr_a, scr_t):
    groups = x.shape[0] // N
    ctx = ExitStack()
    with ctx:
        def sb(name, shape, dt=F32):
            return ctx.enter_context(nc.sbuf_tensor(name, shape, dt))

        class Signal:

            def __init__(self, name, per, first=0):
                self.sem = ctx.enter_context(nc.semaphore(name))
                self.per, self.first = per, first

            def at(self, g, k):
                return g * self.per + (self.first + k)

        def chunks(ap):
            return ap.rearrange("p (c i) -> p c i", i=C)

        def tiles(ap):
            return ap.rearrange("p (t d) -> p t d", d=P)

        cst = sb("cst", [P, C_COLS])
        ident_b = sb("ident_b", [P, P], BF16)
        sel = sb("sel", [3 * E, (BLKS - 1) * P], BF16)
        wproj = sb("wproj", [P, W_COLS])
        wup = sb("wup", [P, BLKS, P])
        wdown = sb("wdown", [P, BLKS, P])
        wo = sb("wo", [P, 2, P])
        w2 = sb("w2", [P, P])
        wrout = sb("wrout", [P, E])
        vecs = sb("vecs", [P, V_COLS])
        rowb = sb("rowb", [P, 3 * H])
        neg_a = sb("neg_a", [P, H])
        exp_a = sb("exp_a", [P, H])
        spare = sb("spare", [P, 8])
        small = sb("small", [P, 8])
        K_LNEPS, K_EPS, K_EPSQ, K_ONE, K_MHALF = range(5)

        def k_(i):
            return small[:, i:i + 1]

        ident = cst[:, C_IDENT:C_IDENT + P]

        xin = sb("xin", [P, TILES, P])
        xn = sb("xn", [P, TILES, P])
        xs_ = sb("xs", [P, N])
        hT = sb("hT", [P, N])
        hn = sb("hn", [P, N])
        xnT = sb("xnT", [P, N])
        sq = sb("sq", [P, 2, N])
        rl = sb("rl", [P, 2, N])
        raw_ = sb("raw", [P, 4 * SEQ * (PAD + T)])
        conv = sb("conv", [P, 4, N])
        brow = sb("brow", [P, NCH, C])
        decay = sb("decay", [P, NCH, C])
        fromst = sb("fromst", [P, NCH, C])
        st = sb("st", [P, TILES, 6])
        mv = sb("mv", [P, TILES, 2])
        lnw = sb("lnw", [P, 4, TILES])
        rstd = sb("rstd", [P, TILES])
        rs2 = sb("rs2", [P, TILES])
        zab = sb("zab", [P, TILES, 2 * H])
        zabs = sb("zabs", [P, TILES, 2 * H])
        zexp = sb("zexp", [P, TILES, 2 * H])
        zln = sb("zln", [P, TILES, H])
        zden = sb("zden", [P, TILES, H])
        zrec = sb("zrec", [P, TILES, H])
        znum = sb("znum", [P, TILES, H])
        zsp = sb("zsp", [P, TILES, H])
        zbeta = sb("zbeta", [P, TILES, H])
        zg = sb("zg", [P, TILES, H])
        lmax = sb("lmax", [P, TILES])
        lsh = sb("lsh", [P, TILES, E])
        er = sb("er", [P, TILES, E])
        top8 = sb("top8", [P, TILES, 8])
        esum = sb("esum", [P, TILES])
        erec = sb("erec", [P, TILES])
        gt = sb("gt", [P, TILES, E])
        ngt = sb("ngt", [P, TILES])
        cum = sb("cum", [P, 3, TILES, 8 + E])
        cnt = sb("cnt", [P, TILES, E])
        keep = sb("keep", [P, TILES, E])
        keep2 = sb("keep2", [P, TILES, E])
        gun = sb("gun", [P, TILES, E])
        gfull = sb("gfull", [P, TILES, E])
        gres = sb("gres", [P, 2, TILES, E])
        gparts = sb("gparts", [P, TILES, 3, E], BF16)
        gpT = sb("gpT", [3 * E, N], BF16)
        gel = sb("gel", [P, 3, HALF])
        hid = sb("hid", [P, 3, HALF])
        xk = sb("xk", [P, TILES, P])
        xorig = sb("xorig", [P, TILES, P])
        ffnT = sb("ffnT", [P, N])
        ogate = sb("ogate", [P, 2, N])
        kg = sb("kg", [P, NCH, C])
        qg = sb("qg", [P, NCH, C])
        kend = sb("kend", [P, NCH, C])
        pt = sb("pt", [P, NCH, C])
        ttb = sb("ttb", [P, NCH, C])
        vtok = sb("vtok", [P, NCH, VD])
        egend = sb("egend", [P, NCH])
        state = sb("state", [P, SEQ, VD])
        sdec = sb("sdec", [P, SEQ, VD])
        resid = sb("resid", [P, SEQ, VD])
        delta = sb("delta", [P, SEQ, VD])
        o = sb("o", [P, NCH, VD])
        on = sb("on", [P, NCH, VD])
        og = sb("og", [P, 2, N])
        oms = sb("oms", [P, NCH])
        omr = sb("omr", [P, NCH])
        orr = sb("orr", [P, NCH])
        st2 = sb("st2", [P, TILES, 6])
        mv2 = sb("mv2", [P, TILES, 2])
        lnw2 = sb("lnw2", [P, TILES])
        rstd2 = sb("rstd2", [P, TILES])

        raw = raw_[:, :].rearrange("p (b s t) -> p b s t", s=SEQ, t=PAD + T)
        pmask, am, lane_m, lane_t = (raw_[:, n * N:(n + 1) * N] for n in range(4))
        pmask, am, lane_t = chunks(pmask), chunks(am), chunks(lane_t)
        xs, gcol, at = tiles(xs_[:, :]), chunks(xs_[:, :]), chunks(xs_[:, :])
        mcum = chunks(hT[:, :])
        ffn_a = hT
        gb = rl[:, :, :].rearrange("p k (t h r) -> p k t h r", h=H, r=C)
        lane_a, ttb0 = chunks(rl[:, 0, :]), chunks(rl[:, 1, :])
        kcol, bcol = chunks(sq[:, 0, :]), chunks(sq[:, 1, :])
        wproj_raw, sel_f = conv[:, 0, 0:W_COLS], conv[0:3 * E, 1, :]
        wo_raw = tiles(conv[:, 2, 0:2 * P])
        onf = on[:, :, :].rearrange("p c v -> p (c v)")
        of = o[:, :, :].rearrange("p c v -> p (c v)")
        x2, h2 = tiles(onf[:, 0:N]), tiles(onf[:, N:2 * N])
        h2T, gelT = of[:, 0:N], of[:, N:2 * N]
        ogf = og[:, :, :].rearrange("p a n -> p (a n)")
        xx2, sumT = tiles(ogf[:, 0:N]), ogf[:, N:2 * N]

        ps = ctx.enter_context(nc.psum_tensor("ps", [P, 8, 512], F32))

        loaded = Signal("weights_loaded", 0)
        cst_ready = Signal("constants_ready", 0)
        bank_at = {job: (BANKS_A[n % 3], n // 3) for n, job in enumerate(JOBS_A)}
        bank_at |= {job: (BANKS_B[n % 2], n // 2) for n, job in enumerate(JOBS_B)}
        uses = {b: sum(at_[0] == b for at_ in bank_at.values()) for b in (*BANKS_A, *BANKS_B)}
        full = {b: Signal(f"bank{b}_full", n) for b, n in uses.items()}
        free = {b: Signal(f"bank{b}_free", n, 1) for b, n in uses.items()}
        pool_a = Signal("pool_chain_a", 5)
        pool_n = Signal("pool_chain_norm", 5)
        pool_b = Signal("pool_chain_b", 1 + NC_SEQ)
        act_a = Signal("act_chain_a", 1)
        dve_a = Signal("dve_chain_a", 86)
        dve_b = Signal("dve_chain_b", 9 + NC_SEQ)
        x_loaded = Signal("x_loaded", 16)
        y_stored = Signal("y_stored", 16, 1)
        bn1_ready = Signal("bn_stats1_ready", 1)
        stats1 = Signal("stats1_ready", 1)
        rstd1_ready = Signal("rstd1_ready", 1)
        xn_ready = Signal("xn_ready", 1)
        xs_ready = Signal("xs_ready", 1)
        xx2_ready = Signal("residual_sum_ready", 1)
        xkept = Signal("x_kept", 1)
        ffn_ready = Signal("ffn_ready", 1)
        hsq_ready = Signal("hsq_ready", 2)
        rms_ready = Signal("rms_ready", 1)
        hn_ready = Signal("hn_ready", 1)
        er_ready = Signal("router_exp_ready", 1)
        gate_ready = Signal("gate_ready", 1)
        gparts_ready = Signal("gate_parts_ready", 1)
        zexp_ready = Signal("zexp_ready", 2)
        gb_ready = Signal("decay_beta_ready", 1)
        conv_ready = Signal("conv_ready", 4)
        act_ready = Signal("act_ready", 4)
        sq_ready = Signal("qk_squares_ready", 2)
        rl2_ready = Signal("qk_scale_ready", 2)
        kq_ready = Signal("kq_ready", 2)
        mcum_ready = Signal("mcum_ready", 1)
        mask_ready = Signal("masked_decay_ready", 2)
        at_ready = Signal("at_ready", 4)
        at_stored = Signal("at_stored", 16)
        lane_ready = Signal("lanes_loaded", 64)
        inv_ready = Signal("inverse_ready", 1)
        inv_stored = Signal("inverse_stored", 16)
        tt_loaded = Signal("tt_loaded", 64)
        ttb_ready = Signal("ttb_ready", 1)
        scaled_ready = Signal("scaled_kq_ready", 3)
        kcol_ready = Signal("kcol_ready", 1)
        pt_ready = Signal("pt_ready", 1)
        down_done = Signal("down_done", 2 * BLKS)
        y_evac = Signal("ffn_copied", 2, 1)
        s_ready = Signal("state_ready", 1 + NC_SEQ)
        ks_full = Signal("ks_full", NC_SEQ)
        r_ready = Signal("resid_ready", NC_SEQ)
        d_full = Signal("delta_full", NC_SEQ)
        d_ready = Signal("delta_ready", NC_SEQ)
        o_full = Signal("o_full", NC_SEQ)
        o_ready = Signal("o_ready", NC_SEQ)
        ds_full = Signal("state_sum_full", NC_SEQ)
        osq_ready = Signal("o_squares_ready", NC_SEQ)
        oms_ready = Signal("o_mean_ready", NC_SEQ)
        orr_ready = Signal("o_scale_ready", NC_SEQ)
        oT_ready = Signal("oT_ready", NC_SEQ)
        og_ready = Signal("og_ready", NC_SEQ)
        stats2 = Signal("stats2_ready", 1)
        rstd2_ready = Signal("rstd2_ready", 1)
        h2_ready = Signal("h2_ready", 1)
        sumT_ready = Signal("sumT_ready", 1)

        def bank(*job):
            return ps[:, bank_at[job][0], :]

        def room(g, *job):
            b, n = bank_at[job]
            return free[b].sem, free[b].at(g, n)

        def filled(*job):
            return full[bank_at[job][0]].sem

        def full_of(g, *job):
            b, n = bank_at[job]
            return full[b].sem, full[b].at(g, n + 1)

        def emptied(*job):
            return free[bank_at[job][0]].sem

        def copied(g, *job):
            b, n = bank_at[job]
            return free[b].sem, free[b].at(g, n + 1)

        def half(ap2d, hf):
            return ap2d[:, hf * HALF:(hf + 1) * HALF]

        def bc_mid(ap, n):
            return ap.unsqueeze(1).broadcast_to([ap.shape[0], n, ap.shape[-1]])

        def bc_last(ap, n):
            return ap.unsqueeze(len(ap.shape)).broadcast_to([*ap.shape, n])

        def bseq(t, c):
            return t[:, :, :].rearrange("p (b c) w -> p b c w", c=NC_SEQ)[:, :, c, :]

        def bchunk(t, v2, c):
            return t[:, v2, :].rearrange("p (b c i) -> p b c i", c=NC_SEQ, i=C)[:, :, c, :]

        def by_seq(b):
            return ps[:, b, 0:SEQ * VD].rearrange("p (b v) -> p b v", v=VD)

        last_p = groups - 1
        block = ctx.enter_context(nc.Block())

        @block.sync
        def _(sp):
            for dst, src in ((cst[:], consts), (sel_f, sel_in), (wproj_raw, wproj_in), (wo_raw, wo_in),
                             (w2[:], w2_in), (wrout[:], router_in), (vecs[:], vecs_in), (rowb[:], rowb_in),
                             (wup[:], wup_in), (wdown[:], wdown_in)):
                sp.dma_start(dst, src).then_inc(loaded.sem, 16)

            def load(g):
                sp.dma_start(xin[:], x[bass.ds(g * N, N), :].rearrange("(t p) d -> p t d", p=P)) \
                    .then_inc(x_loaded.sem, 16)

            def relayout(g):
                sp.wait_ge(at_ready.sem, at_ready.at(g, 4))
                sp.dma_start(scr_a.rearrange("h j c i -> (h j) (c i)"), at.rearrange("p c i -> p (c i)")) \
                    .then_inc(at_stored.sem, 16)
                sp.wait_ge(at_stored.sem, at_stored.at(g, 16))
                for h in range(H):
                    sp.dma_start(lane_a[h * C:(h + 1) * C, :, :], scr_a[h].rearrange("j c i -> c j i")) \
                        .then_inc(lane_ready.sem, 16)

            def relayout_back(g):
                sp.wait_ge(inv_ready.sem, inv_ready.at(g, 1))
                sp.dma_start(scr_t.rearrange("h c j i -> (h c) (j i)"), lane_t.rearrange("p j i -> p (j i)")) \
                    .then_inc(inv_stored.sem, 16)
                sp.wait_ge(inv_stored.sem, inv_stored.at(g, 16))
                for h in range(H):
                    sp.dma_start(ttb0[h * C:(h + 1) * C, :, :], scr_t[h].rearrange("c j i -> j c i")) \
                        .then_inc(tt_loaded.sem, 16)

            def store(p):
                sp.wait_ge(*copied(p, "final", 1))
                sp.dma_start(out[bass.ds(p * N, N), :].rearrange("(t p) d -> p t d", p=P), xx2) \
                    .then_inc(y_stored.sem, 16)

            def load_next(g):
                sp.wait_ge(xkept.sem, xkept.at(g, 1))
                load(g + 1)

            load(0)
            relayout(0)
            load_next(0)
            relayout_back(0)
            with sp.Fori(0, groups - 2) as p:
                relayout(p + 1)
                load_next(p + 1)
                relayout_back(p + 1)
                store(p)
            relayout(last_p)
            relayout_back(last_p)
            store(last_p - 1)
            store(last_p)
            sp.wait_ge(y_stored.sem, 16 * groups + 1)

        @block.gpsimd
        def _(pool):
            def rsqrt_into(dst, src, tmp, eps, link):
                link(pool.tensor_tensor(tmp, src, k_(eps).broadcast_to(list(src.shape)), ALU.add))
                return pool.tensor_tensor(dst, tmp, k_(K_MHALF).broadcast_to(list(src.shape)), ALU.pow)

            def front(g, link):
                pool.wait_ge(stats1.sem, stats1.at(g, 1))
                link(rsqrt_into(rstd[:, :], mv[:, :, 1], lnw[:, 0, :], K_LNEPS, link))
                link(pool.tensor_tensor(lnw[:, 1, :], mv[:, :, 1], rstd[:, :], ALU.mult))
                link(pool.tensor_tensor(lnw[:, 2, :], lnw[:, 1, :], rstd[:, :], ALU.mult))
                rsqrt_into(rs2[:, :], lnw[:, 2, :], lnw[:, 3, :], K_LNEPS, link).then_inc(rstd1_ready.sem, 1)

            def masks(g, link):
                pool.wait_ge(conv_ready.sem, conv_ready.at(g, 2))
                pool.wait_ge(*copied(g, "decay", 1))
                pool.tensor_tensor(pmask, decay[:], bc_mid(cst[:, C_UPTO:C_UPTO + C], NCH), ALU.mult) \
                    .then_inc(mask_ready.sem, 1)
                pool.wait_ge(*copied(g, "brow", 1))
                link(pool.tensor_tensor(am, decay[:], brow[:], ALU.mult))
                pool.tensor_tensor(am, am, bc_mid(cst[:, C_BEFORE:C_BEFORE + C], NCH), ALU.mult) \
                    .then_inc(mask_ready.sem, 1)

            def split_gates(g, link):
                pool.wait_ge(gate_ready.sem, gate_ready.at(g, 1))
                one = k_(K_ONE).unsqueeze(2).broadcast_to([P, TILES, E])
                link(pool.tensor_tensor(gparts[:, :, 0, :], gfull[:], one, ALU.mult))
                link(pool.tensor_tensor(gres[:, 0], gfull[:], gparts[:, :, 0, :], ALU.subtract))
                link(pool.tensor_tensor(gparts[:, :, 1, :], gres[:, 0], one, ALU.mult))
                link(pool.tensor_tensor(gres[:, 1], gres[:, 0], gparts[:, :, 1, :], ALU.subtract))
                pool.tensor_tensor(gparts[:, :, 2, :], gres[:, 1], one, ALU.mult).then_inc(gparts_ready.sem, 1)

            def scale(p, g):
                if p is not None:
                    pool.wait_ge(o_full.sem, o_full.at(p, NC_SEQ))
                pool.wait_ge(*copied(g, "fromstart", 1))
                pool.wait_ge(kq_ready.sem, kq_ready.at(g, 2))
                pool.tensor_tensor(kg[:], chunks(conv[:, 1, :]), fromst[:], ALU.mult).then_inc(scaled_ready.sem, 1)
                pool.tensor_tensor(qg[:], chunks(conv[:, 0, :]), fromst[:], ALU.mult).then_inc(scaled_ready.sem, 1)
                pool.wait_ge(kcol_ready.sem, kcol_ready.at(g, 1))
                pool.tensor_tensor(kend[:], kcol, bc_last(decay[:, :, C - 1], C), ALU.mult) \
                    .then_inc(scaled_ready.sem, 1)

            def keep_x(p, g):
                one = k_(K_ONE).unsqueeze(2).broadcast_to([P, TILES, P])
                pool.wait_ge(xn_ready.sem, xn_ready.at(g, 1))
                if p is not None:
                    pool.wait_ge(xx2_ready.sem, xx2_ready.at(p, 1))
                pool.tensor_tensor(xk[:], xn[:], one, ALU.mult)
                pool.tensor_tensor(xorig[:], xin[:], one, ALU.mult).then_inc(xkept.sem, 1)

            def keep_ffn(p, g):
                if p is not None:
                    pool.wait_ge(sumT_ready.sem, sumT_ready.at(p, 1))
                pool.wait_ge(y_evac.sem, y_evac.at(g, 2))
                pool.tensor_tensor(ffnT[:], ffn_a[:], k_(K_ONE).broadcast_to([P, N]), ALU.mult) \
                    .then_inc(ffn_ready.sem, 1)

            def out_norm(p, c, link):
                pool.wait_ge(oms_ready.sem, oms_ready.at(p, c + 1))
                rsqrt_into(orr[:, c::NC_SEQ], oms[:, c::NC_SEQ], omr[:, c::NC_SEQ], K_EPS, link) \
                    .then_inc(orr_ready.sem, 1)

            def out_gate(p, c):
                pool.wait_ge(oT_ready.sem, oT_ready.at(p, c + 1))
                for v2 in range(2):
                    ins = pool.tensor_tensor(bchunk(og, v2, c), bchunk(og, v2, c), bchunk(ogate, v2, c), ALU.mult)
                ins.then_inc(og_ready.sem, 1)

            def tail(p, link):
                pool.wait_ge(stats2.sem, stats2.at(p, 1))
                rsqrt_into(rstd2[:, :], mv2[:, :, 1], lnw2[:, :], K_LNEPS, link).then_inc(rstd2_ready.sem, 1)
                pool.tensor_tensor(xx2, x2, xorig[:], ALU.add).then_inc(xx2_ready.sem, 1)

            def sums(p):
                pool.wait_ge(*copied(p, "w2", 0))
                pool.wait_ge(*copied(p, "w2", 1))
                pool.tensor_tensor(sumT, gelT, ffnT[:], ALU.add).then_inc(sumT_ready.sem, 1)

            def norm_scales(g):
                n = [0]

                def link(ins):
                    n[0] += 1
                    ins.then_inc(pool_n.sem, 1)
                    pool.wait_ge(pool_n.sem, pool_n.at(g, n[0]))

                front(g, link)
                assert n[0] == pool_n.per, n

            def round_(p, g, after):
                chain = {"a": 0, "b": 0}

                def link_a(ins):
                    chain["a"] += 1
                    ins.then_inc(pool_a.sem, 1)
                    pool.wait_ge(pool_a.sem, pool_a.at(g, chain["a"]))

                def link_b(ins):
                    chain["b"] += 1
                    ins.then_inc(pool_b.sem, 1)
                    pool.wait_ge(pool_b.sem, pool_b.at(p, chain["b"]))

                for c in range(NC_SEQ):
                    if g is not None and c == 3:
                        split_gates(g, link_a)
                    if g is not None and c == 4:
                        masks(g, link_a)
                    if p is not None and c >= 1:
                        out_norm(p, c - 1, link_b)
                    if p is not None and c >= 2:
                        out_gate(p, c - 2)
                if p is not None:
                    out_norm(p, NC_SEQ - 1, link_b)
                    out_gate(p, NC_SEQ - 2)
                    out_gate(p, NC_SEQ - 1)
                if g is not None:
                    scale(p, g)
                if p is not None:
                    tail(p, link_b)
                if g is not None:
                    keep_x(p, g)
                if after is not None:
                    norm_scales(after)
                if p is not None:
                    sums(p)
                if g is not None:
                    keep_ffn(p, g)
                    assert chain["a"] == pool_a.per, chain
                if p is not None:
                    assert chain["b"] == pool_b.per, chain

            norm_scales(0)
            round_(None, 0, 1)
            with pool.Fori(0, groups - 2) as p:
                round_(p, p + 1, p + 2)
            round_(last_p - 1, last_p, None)
            round_(last_p, None, None)

        @block.scalar
        def _(act):
            act.wait_ge(loaded.sem, 160)
            act.wait_ge(cst_ready.sem, 1)
            act.activation(exp_a[:], rowb[:, 2 * H:3 * H], ACT.Exp).then_inc(cst_ready.sem, 1)

            def project(g, b4):
                for hf in range(2):
                    act.wait_ge(*full_of(g, "qkv", b4, hf))
                    act.activation(raw[:, b4, 2 * hf:2 * hf + 2, PAD:PAD + T],
                                   bank("qkv", b4, hf).rearrange("p (s t) -> p s t", t=T), ACT.Copy)
                    w = vecs[:, V_CONV + TAPS * b4 + PAD:V_CONV + TAPS * b4 + TAPS]
                    act.activation(half(conv[:, b4, :], hf), bank("qkv", b4, hf), ACT.Copy, scale=w) \
                        .then_inc(emptied("qkv", b4, hf), 1)

            def exp_of(g, name, dst):
                for hf in range(2):
                    act.wait_ge(*full_of(g, name, hf))
                    act.activation(dst[:, 16 * hf:16 * hf + 16, :], chunks(bank(name, hf)), ACT.Exp) \
                        .then_inc(emptied(name, hf), 1)

            def normalise_again(g):
                act.wait_ge(xn_ready.sem, xn_ready.at(g, 1))
                for t in range(TILES):
                    ins = act.activation(xs[:, t, :], xn[:, t, :], ACT.Copy, scale=rs2[:, t:t + 1])
                ins.then_inc(xs_ready.sem, 1)

            def features(g, last=None):
                for hf in range(2):
                    act.wait_ge(*full_of(g, "xnT", hf))
                    act.activation(half(xnT, hf), bank("xnT", hf), ACT.Copy).then_inc(emptied("xnT", hf), 1)
                if last is not None:
                    act.wait_ge(ffn_ready.sem, ffn_ready.at(last, 1))
                for hf in range(2):
                    act.wait_ge(*full_of(g, "xsT", hf))
                    act.activation(half(hT, hf), bank("xsT", hf), ACT.Identity,
                                   scale=vecs[:, V_LN1G:V_LN1G + 1], bias=vecs[:, V_LN1B:V_LN1B + 1]) \
                        .then_inc(emptied("xsT", hf), 1)
                    act.wait_ge(*copied(g, "xsT", hf))
                    act.activation(half(sq[:, 0, :], hf), half(hT, hf), ACT.Square).then_inc(hsq_ready.sem, 1)

            def rms(g):
                act.preload_act_table_set("natural_log_exp_and_others")
                for hf in range(2):
                    act.wait_ge(*full_of(g, "rms", hf))
                    act.activation(half(rl[:, 0, :], hf), bank("rms", hf), ACT.Ln, bias=k_(K_EPS)) \
                        .then_inc(emptied("rms", hf), 1)
                act.wait_ge(*copied(g, "rms", 0))
                act.wait_ge(*copied(g, "rms", 1))
                act.activation(rl[:, 0, :], rl[:, 0, :], ACT.Exp, scale=-0.5).then_inc(rms_ready.sem, 1)

            def small_exps(g, link):
                act.wait_ge(*copied(g, "router"))
                act.activation(er[:], lsh[:], ACT.Exp).then_inc(er_ready.sem, 1)
                act.wait_ge(*copied(g, "ab"))
                link(act.activation(zabs[:], zab[:], ACT.Abs))
                act.activation(zexp[:], zabs[:], ACT.Exp, scale=-1.0).then_inc(zexp_ready.sem, 1)
                act.wait_ge(zexp_ready.sem, zexp_ready.at(g, 1))
                act.activation(zln[:], zexp[:, :, 0:H], ACT.Ln, bias=k_(K_ONE)).then_inc(zexp_ready.sem, 1)

            def silu(g, b4):
                act.wait_ge(conv_ready.sem, conv_ready.at(g, b4 + 1))
                act.activation(conv[:, b4, :], conv[:, b4, :], ACT.Silu).then_inc(act_ready.sem, 1)

            def squares(g, b2):
                act.wait_ge(act_ready.sem, act_ready.at(g, b2 + 1))
                act.activation(sq[:, b2, :], conv[:, b2, :], ACT.Square).then_inc(sq_ready.sem, 1)

            def slot(g, c, link):
                if c == 0:
                    rms(g)
                if c == 1:
                    small_exps(g, link)
                    project(g, 0)
                if c == 2:
                    project(g, 1)
                    for hf in range(2):
                        act.wait_ge(*full_of(g, "brow", hf))
                        act.activation(brow[:, 16 * hf:16 * hf + 16, :], chunks(bank("brow", hf)), ACT.Copy) \
                            .then_inc(emptied("brow", hf), 1)
                if c == 3:
                    exp_of(g, "decay", decay)
                    exp_of(g, "fromstart", fromst)
                    for b2 in range(2):
                        silu(g, b2)
                        squares(g, b2)
                if c == 4:
                    project(g, 2)
                    norms(g)
                    project(g, 3)
                if c == 5:
                    silu(g, 2)
                    silu(g, 3)
                if c == 4:
                    act.wait_ge(*full_of(g, "gateT"))
                    act.activation(gpT[:], ps[0:3 * E, bank_at[("gateT",)][0], :].bitcast(BF16), ACT.Copy) \
                        .then_inc(emptied("gateT"), 1)
                for n in range(FIRST_STEP[c], FIRST_STEP[c + 1]):
                    gelu(g, n)

            def norms(g):
                act.preload_act_table_set("natural_log_exp_and_others")
                for b2 in range(2):
                    for hf in range(2):
                        act.wait_ge(*full_of(g, "l2", b2, hf))
                        act.activation(half(rl[:, b2, :], hf), bank("l2", b2, hf), ACT.Ln,
                                       bias=k_(K_EPSQ if b2 == 0 else K_EPS)).then_inc(emptied("l2", b2, hf), 1)
                    act.wait_ge(*copied(g, "l2", b2, 0))
                    act.wait_ge(*copied(g, "l2", b2, 1))
                    act.activation(rl[:, b2, :], rl[:, b2, :], ACT.Exp, scale=-0.5).then_inc(rl2_ready.sem, 1)

            def keep_pt(p, g):
                act.wait_ge(*copied(g, "pairs", 3))
                if p is not None:
                    act.wait_ge(o_full.sem, o_full.at(p, NC_SEQ))
                act.activation(pt[:], pmask, ACT.Copy).then_inc(pt_ready.sem, 1)

            def gelu(g, n):
                hf, m = STEPS[n]
                act.wait_ge(*full_of(g, "up", hf, m))
                if n >= 3:
                    act.wait_ge(down_done.sem, down_done.at(g, n - 2))
                dst = gel if m else hid
                act.activation(dst[:, n % 3, :], bank("up", hf, m), ACT.Gelu).then_inc(emptied("up", hf, m), 1)
                if n == BLKS:
                    y_copy(g, 0)

            def y_copy(g, hf):
                act.wait_ge(down_done.sem, down_done.at(g, (hf + 1) * BLKS))
                act.activation(half(ffn_a, hf), ps[:, BANK_Y, :], ACT.Copy).then_inc(y_evac.sem, 1)

            def gates(g):
                for b2 in range(2):
                    for hf in range(2):
                        act.wait_ge(*full_of(g, "ogate", b2, hf))
                        act.activation(half(ogate[:, b2, :], hf), bank("ogate", b2, hf), ACT.Silu) \
                            .then_inc(emptied("ogate", b2, hf), 1)

            def delta_copy(p, c):
                act.wait_ge(d_full.sem, d_full.at(p, c + 1))
                act.activation(delta[:], by_seq(BANK_D), ACT.Copy).then_inc(d_ready.sem, 1)

            def o_copy(p, c):
                act.wait_ge(o_full.sem, o_full.at(p, c + 1))
                act.activation(bseq(o, c), by_seq(BANK_O), ACT.Copy).then_inc(o_ready.sem, 1)

            def o_squares(p, c):
                act.wait_ge(o_ready.sem, o_ready.at(p, c + 1))
                act.activation(bseq(on, c), bseq(o, c), ACT.Square, scale=VD ** -0.5).then_inc(osq_ready.sem, 1)

            def norm2(p):
                for hf in range(2):
                    act.wait_ge(*full_of(p, "h2T", hf))
                    act.activation(half(h2T, hf), bank("h2T", hf), ACT.Identity,
                                   scale=vecs[:, V_LN2G:V_LN2G + 1], bias=vecs[:, V_LN2B:V_LN2B + 1]) \
                        .then_inc(emptied("h2T", hf), 1)

            def gelu2(p):
                for hf in range(2):
                    act.wait_ge(*full_of(p, "w2", hf))
                    act.activation(half(gelT, hf), bank("w2", hf), ACT.Gelu, bias=vecs[:, V_B2:V_B2 + 1]) \
                        .then_inc(emptied("w2", hf), 1)

            def round_(p, g, after):
                chain = [0]

                def link(ins):
                    chain[0] += 1
                    ins.then_inc(act_a.sem, 1)
                    act.wait_ge(act_a.sem, act_a.at(g, chain[0]))

                for c in range(NC_SEQ):
                    if p is not None:
                        delta_copy(p, c)
                    if g is not None:
                        slot(g, c, link)
                    if p is not None:
                        o_copy(p, c)
                        o_squares(p, c)
                if g is None:
                    norm2(p)
                    gelu2(p)
                    return
                keep_pt(p, g)
                for n in range(IN_TAIL, 2 * BLKS):
                    gelu(g, n)
                    if p is not None and n == H2_BEHIND:
                        norm2(p)
                    if p is not None and n == W2_BEHIND:
                        gelu2(p)
                if after is not None:
                    normalise_again(after)
                gates(g)
                y_copy(g, 1)
                if after is not None:
                    features(after, g)
                assert chain[0] == act_a.per, chain

            normalise_again(0)
            features(0)
            round_(None, 0, 1)
            with act.Fori(0, groups - 2) as p:
                round_(p, p + 1, p + 2)
            round_(last_p - 1, last_p, None)
            round_(last_p, None, None)

        @block.vector
        def _(dve):
            for i, v in enumerate((LN_EPS, EPS, KD * EPS, 1.0, -0.5)):
                dve.memset(k_(i), v)
            dve.memset(cum[:], 0.0)
            for n, s in enumerate((*free.values(), y_stored, y_evac)):
                dve.memset(spare[:, n:n + 1], 0.0).then_inc(s.sem, 1)
            dve.memset(spare[:, 7:8], 0.0).then_inc(cst_ready.sem, 1)
            dve.wait_ge(loaded.sem, 160)
            dve.tensor_scalar(wproj[:], wproj_raw, vecs[:, V_RMS:V_RMS + 1], None, ALU.mult)
            dve.tensor_scalar(wo[:, 0, :], wo_raw[:, 0, :], vecs[:, V_ON0:V_ON0 + 1], None, ALU.mult)
            dve.tensor_scalar(wo[:, 1, :], wo_raw[:, 1, :], vecs[:, V_ON1:V_ON1 + 1], None, ALU.mult)
            dve.tensor_copy(ident_b[:], ident)
            dve.tensor_copy(sel[:], sel_f).then_inc(cst_ready.sem, 1)
            dve.wait_ge(cst_ready.sem, 3)
            dve.tensor_scalar(neg_a[:], exp_a[:], -1.0, None, ALU.mult).then_inc(cst_ready.sem, 1)
            dve.wait_ge(cst_ready.sem, 4)

            def convolve(g, b4, link):
                dve.wait_ge(*copied(g, "qkv", b4, 0))
                dve.wait_ge(*copied(g, "qkv", b4, 1))
                cv = conv[:, b4, :].rearrange("p (s t) -> p s t", t=T)
                for i in range(PAD):
                    w = vecs[:, V_CONV + TAPS * b4 + i:V_CONV + TAPS * b4 + i + 1]
                    ins = dve.scalar_tensor_tensor(out=cv, in0=raw[:, b4, :, i:i + T], scalar=w, in1=cv,
                                                   op0=ALU.mult, op1=ALU.add)
                    if i < PAD - 1:
                        link(ins)
                ins.then_inc(conv_ready.sem, 1)

            def select_experts(g, link):
                dve.wait_ge(er_ready.sem, er_ready.at(g, 1))
                link(dve.tensor_reduce(esum[:], er[:], AX.X, ALU.add))
                dve.reciprocal(erec[:], esum[:])
                for t in range(TILES):
                    last = dve.max(top8[:, t, :], er[:, t, :])
                link(last)
                thr = top8[:, :, TOPK - 1:TOPK].broadcast_to([P, TILES, E])
                dve.tensor_tensor(gt[:], er[:], thr, ALU.is_gt)
                link(dve.tensor_tensor(cum[:, 0, :, 8:], er[:], thr, ALU.is_equal))
                dve.tensor_reduce(ngt[:], gt[:], AX.X, ALU.add)
                at_ = 0
                for s, to in ((1, 1), (2, 2), (4, 1), (8, 2)):
                    link(dve.tensor_tensor(cum[:, to, :, 8:], cum[:, at_, :, 8:], cum[:, at_, :, 8 - s:8 + E - s],
                                           ALU.add))
                    at_ = to
                link(dve.tensor_tensor(cnt[:], cum[:, at_, :, 8:], bc_last(ngt[:, :], E), ALU.add))
                link(dve.scalar_tensor_tensor(out=keep[:], in0=cnt[:], scalar=float(TOPK), in1=cum[:, 0, :, 8:],
                                              op0=ALU.is_le, op1=ALU.mult))
                link(dve.tensor_tensor(keep2[:], keep[:], gt[:], ALU.add))
                link(dve.tensor_tensor(gun[:], keep2[:], er[:], ALU.mult))
                dve.tensor_tensor(gfull[:], gun[:], bc_last(erec[:, :], E), ALU.mult).then_inc(gate_ready.sem, 1)

            def decay_and_beta(g, link):
                dve.wait_ge(zexp_ready.sem, zexp_ready.at(g, 2))
                dve.scalar_tensor_tensor(out=znum[:], in0=zab[:, :, H:2 * H], scalar=0.0,
                                         in1=zexp[:, :, H:2 * H], op0=ALU.is_ge, op1=ALU.max)
                dve.tensor_scalar(zden[:], zexp[:, :, H:2 * H], 1.0, None, ALU.add)
                link(dve.scalar_tensor_tensor(out=zsp[:], in0=zab[:, :, 0:H], scalar=0.0, in1=zln[:],
                                              op0=ALU.max, op1=ALU.add))
                dve.reciprocal(zrec[:], zden[:])
                link(dve.tensor_tensor(zg[:], zsp[:], bc_mid(neg_a[:, :], TILES), ALU.mult))
                link(dve.tensor_tensor(zbeta[:], znum[:], zrec[:], ALU.mult))
                dve.tensor_copy(gb[:, 1], bc_last(zbeta[:, :, :], C))
                dve.tensor_scalar(gb[:, 0], bc_last(zg[:, :, :], C), G_LEAST, None, ALU.max) \
                    .then_inc(gb_ready.sem, 1)

            def statistics(g):
                dve.wait_ge(x_loaded.sem, x_loaded.at(g, 16))
                for t in range(TILES):
                    last = dve.bn_stats(st[:, t, :], xin[:, t, :])
                last.then_inc(bn1_ready.sem, 1)
                dve.wait_ge(bn1_ready.sem, bn1_ready.at(g, 1))
                dve.memset(spare[:, 0:1], 0.0)
                for t in range(TILES):
                    last = dve.bn_aggr(mv[:, t, :], st[:, t, :])
                last.then_inc(stats1.sem, 1)

            def normalise(g):
                dve.wait_ge(rstd1_ready.sem, rstd1_ready.at(g, 1))
                dve.wait_ge(stats1.sem, stats1.at(g, 1))
                for t in range(TILES):
                    last = dve.tensor_scalar(xn[:, t, :], xin[:, t, :], mv[:, t, 0:1], rstd[:, t:t + 1],
                                             ALU.subtract, ALU.mult)
                last.then_inc(xn_ready.sem, 1)

            def take_inverse(p):
                dve.memset(state[:], 0.0).then_inc(s_ready.sem, 1)
                dve.wait_ge(tt_loaded.sem, tt_loaded.at(p, 64))
                dve.tensor_tensor(ttb[:], ttb0, bcol, ALU.mult).then_inc(ttb_ready.sem, 1)

            def slot(p, g, c, link):
                if c == 0:
                    dve.memset(raw[:, :, :, 0:PAD], 0.0)
                    logits = bank("router")[:, 0:TILES * E].rearrange("p (t e) -> p t e", e=E)
                    dve.wait_ge(*full_of(g, "router"))
                    link(dve.tensor_reduce(lmax[:], logits, AX.X, ALU.max))
                    dve.tensor_tensor(lsh[:], logits, bc_last(lmax[:, :], E), ALU.subtract) \
                        .then_inc(emptied("router"), 1)
                    dve.wait_ge(rms_ready.sem, rms_ready.at(g, 1))
                    dve.wait_ge(*copied(g, "xsT", 1))
                    dve.tensor_tensor(hn[:], hT[:], rl[:, 0, :], ALU.mult).then_inc(hn_ready.sem, 1)
                if c == 1:
                    dve.wait_ge(*full_of(g, "ab"))
                    dve.tensor_tensor(zab[:], bank("ab")[:, 0:TILES * 2 * H].rearrange("p (t n) -> p t n", n=2 * H),
                                      bc_mid(rowb[:, 0:2 * H], TILES), ALU.add).then_inc(emptied("ab"), 1)
                    select_experts(g, link)
                    dve.wait_ge(*copied(g, "ab"))
                    decay_and_beta(g, link)
                if c == 2:
                    convolve(g, 0, link)
                    for hf in range(2):
                        dve.wait_ge(*full_of(g, "grow", hf))
                        dve.transpose(gcol[:, 16 * hf:16 * hf + 16, :], chunks(bank("grow", hf))) \
                            .then_inc(emptied("grow", hf), 1)
                    dve.wait_ge(*copied(g, "grow", 0))
                    dve.wait_ge(*copied(g, "grow", 1))
                    dve.tensor_tensor(mcum, gcol, bc_mid(cst[:, C_UPTO:C_UPTO + C], NCH), ALU.mult) \
                        .then_inc(mcum_ready.sem, 1)
                if c == 3:
                    convolve(g, 1, link)
                if c == 4:
                    convolve(g, 2, link)
                    scale_pairs(g)
                if c == 5:
                    convolve(g, 3, link)
                    pairs(g)
                if c == 6:
                    start_inverse(g, link)
                for n in range(FIRST_STEP[c], FIRST_STEP[c + 1]):
                    product(g, n)
                if c == 7:
                    dve.wait_ge(lane_ready.sem, lane_ready.at(g, 64))
                    for j in range(INV_IN_SLOTS):
                        link(inverse_step(j, link))

            def scale_pairs(g):
                for b2 in range(2):
                    dve.wait_ge(rl2_ready.sem, rl2_ready.at(g, b2 + 1))
                    dve.tensor_tensor(conv[:, b2, :], conv[:, b2, :], rl[:, b2, :], ALU.mult) \
                        .then_inc(kq_ready.sem, 1)
                dve.wait_ge(kq_ready.sem, kq_ready.at(g, 2))
                dve.transpose(kcol, chunks(conv[:, 1, :])).then_inc(kcol_ready.sem, 1)

            def pairs(g):
                dve.wait_ge(mask_ready.sem, mask_ready.at(g, 2))
                for q in range(4):
                    dve.wait_ge(*full_of(g, "pairs", q))
                    pr = bank("pairs", q).rearrange("p (c n) -> p c n", n=2 * C)
                    eight = slice(8 * q, 8 * q + 8)
                    dve.tensor_tensor(at[:, eight, :], pr[:, :, C:2 * C], am[:, eight, :], ALU.mult) \
                        .then_inc(at_ready.sem, 1)
                    dve.tensor_tensor(pmask[:, eight, :], pr[:, :, 0:C], pmask[:, eight, :],
                                      ALU.mult).then_inc(emptied("pairs", q), 1)

            def start_inverse(g, link):
                dve.wait_ge(conv_ready.sem, conv_ready.at(g, 4))
                link(dve.memset(lane_t, 0.0))
                link(dve.memset(raw_[:, 3 * N:4 * N:C + 1], 1.0))
                dve.wait_ge(*copied(g, "brow", 1))
                dve.transpose(bcol, brow[:])

            def to_columns(g):
                for v2 in range(2):
                    dve.wait_ge(act_ready.sem, act_ready.at(g, 3 + v2))
                    dve.transpose(vtok[:, :, v2 * 32:v2 * 32 + 32], chunks(conv[:, 2 + v2, :]))
                dve.wait_ge(*copied(g, "fromstart", 1))
                dve.tensor_copy(egend[:], fromst[:, :, C - 1])

            def product(g, n):
                hf, m = STEPS[n]
                if m:
                    dve.wait_ge(*copied(g, "up", hf, m))
                    dve.wait_ge(*full_of(g, "gate", hf, m))
                    dve.tensor_tensor(hid[:, n % 3, :], gel[:, n % 3, :], bank("gate", hf, m), ALU.mult) \
                        .then_inc(emptied("gate", hf, m), 1)

            def chunk_first(p, c, link):
                dve.wait_ge(ks_full.sem, ks_full.at(p, c + 1))
                dve.tensor_tensor(resid[:], bseq(vtok, c), by_seq(BANK_KS), ALU.subtract).then_inc(r_ready.sem, 1)
                dve.wait_ge(s_ready.sem, s_ready.at(p, c + 1))
                link(dve.tensor_tensor(sdec[:], state[:], bc_last(egend[:, c::NC_SEQ], VD), ALU.mult))

            def chunk_last(p, c):
                dve.wait_ge(ds_full.sem, ds_full.at(p, c + 1))
                dve.tensor_tensor(state[:], sdec[:], by_seq(BANK_D), ALU.add).then_inc(s_ready.sem, 1)

            def out_mean(p, c):
                dve.wait_ge(osq_ready.sem, osq_ready.at(p, c + 1))
                dve.tensor_reduce(oms[:, c::NC_SEQ], bseq(on, c), AX.X, ALU.add).then_inc(oms_ready.sem, 1)

            def out_turn(p, c, link):
                dve.wait_ge(orr_ready.sem, orr_ready.at(p, c + 1))
                link(dve.tensor_tensor(bseq(on, c), bseq(o, c), bc_last(orr[:, c::NC_SEQ], VD), ALU.mult))
                if c == 0:
                    dve.wait_ge(y_stored.sem, y_stored.at(p, 0))
                for v2 in range(2):
                    ins = dve.transpose(bchunk(og, v2, c), bseq(on, c)[:, :, v2 * 32:v2 * 32 + 32])
                ins.then_inc(oT_ready.sem, 1)

            def residual(p, link):
                for hf in range(2):
                    four = slice(4 * hf, 4 * hf + 4)
                    dve.wait_ge(*full_of(p, "enc", hf))
                    dve.tensor_tensor(x2[:, four, :], tiles(bank("enc", hf)), xk[:, four, :], ALU.add) \
                        .then_inc(emptied("enc", hf), 1)
                for hf in range(2):
                    dve.wait_ge(*copied(p, "enc", hf))
                for t in range(TILES):
                    ins = dve.bn_stats(st2[:, t, :], x2[:, t, :])
                link(ins)
                dve.memset(spare[:, 0:1], 0.0)
                for t in range(TILES):
                    last = dve.bn_aggr(mv2[:, t, :], st2[:, t, :])
                last.then_inc(stats2.sem, 1)

            def norm2(p):
                dve.wait_ge(rstd2_ready.sem, rstd2_ready.at(p, 1))
                dve.wait_ge(stats2.sem, stats2.at(p, 1))
                for t in range(TILES):
                    last = dve.tensor_scalar(h2[:, t, :], x2[:, t, :], mv2[:, t, 0:1], rstd2[:, t:t + 1],
                                             ALU.subtract, ALU.mult)
                last.then_inc(h2_ready.sem, 1)

            def output(p):
                for hf in range(2):
                    four = slice(4 * hf, 4 * hf + 4)
                    dve.wait_ge(*full_of(p, "final", hf))
                    dve.tensor_tensor(xx2[:, four, :], tiles(bank("final", hf)), xx2[:, four, :], ALU.add) \
                        .then_inc(emptied("final", hf), 1)

            def inverse_step(j, link):
                m = lane_m[:, 0:(j + 1) * (C - 1 - j)].rearrange("p (l i) -> p l i", i=C - 1 - j)
                link(dve.tensor_tensor(m, bc_mid(lane_a[:, j, j + 1:C], j + 1),
                                       lane_t[:, 0:j + 1, j:j + 1].broadcast_to([P, j + 1, C - 1 - j]), ALU.mult))
                return dve.tensor_tensor(lane_t[:, 0:j + 1, j + 1:C], lane_t[:, 0:j + 1, j + 1:C], m,
                                         ALU.subtract)

            def round_(p, g, after):
                chain = {"a": 0, "b": 0}

                def link_a(ins):
                    chain["a"] += 1
                    ins.then_inc(dve_a.sem, 1)
                    dve.wait_ge(dve_a.sem, dve_a.at(g, chain["a"]))

                def link_b(ins):
                    chain["b"] += 1
                    ins.then_inc(dve_b.sem, 1)
                    dve.wait_ge(dve_b.sem, dve_b.at(p, chain["b"]))

                if p is not None:
                    take_inverse(p)
                for c in range(NC_SEQ):
                    if p is not None:
                        chunk_first(p, c, link_b)
                        if c >= 1:
                            out_mean(p, c - 1)
                    if g is not None:
                        slot(p, g, c, link_a)
                    if p is not None and c >= 2:
                        out_turn(p, c - 2, link_b)
                    if p is not None:
                        chunk_last(p, c)
                if g is not None:
                    to_columns(g)
                    left = list(range(IN_TAIL, 2 * BLKS))
                    for j in range(INV_IN_SLOTS, C - 1):
                        ins = inverse_step(j, link_a)
                        if j < C - 2:
                            link_a(ins)
                        else:
                            ins.then_inc(inv_ready.sem, 1)
                        if j % 2 == 0 and left:
                            product(g, left.pop(0))
                        if j == INV_IN_SLOTS and p is not None:
                            out_mean(p, NC_SEQ - 1)
                        if j in TURN_AT and p is not None:
                            out_turn(p, NC_SEQ - 2 + TURN_AT.index(j), link_b)
                        if j == RESIDUAL_AT and p is not None:
                            residual(p, link_b)
                        if j == NORM2_AT and p is not None:
                            norm2(p)
                        if j == STATS_AT and after is not None:
                            statistics(after)
                        if j == NORMALISE_AT and after is not None:
                            normalise(after)
                    if p is not None:
                        output(p)
                    assert chain["a"] == dve_a.per, chain
                else:
                    out_mean(p, NC_SEQ - 1)
                    out_turn(p, NC_SEQ - 2, link_b)
                    out_turn(p, NC_SEQ - 1, link_b)
                    residual(p, link_b)
                    norm2(p)
                    output(p)
                if p is not None:
                    assert chain["b"] == dve_b.per, chain

            statistics(0)
            normalise(0)
            round_(None, 0, 1)
            with dve.Fori(0, groups - 2) as p:
                round_(p, p + 1, p + 2)
            round_(last_p - 1, last_p, None)
            round_(last_p, None, None)

        @block.tensor
        def _(pe):
            pe.wait_ge(loaded.sem, 160)
            pe.wait_ge(cst_ready.sem, 4)

            def one(g, job, lhs, rhs):
                pe.wait_ge(*room(g, *job))
                pe.matmul(bank(*job), lhs, rhs, start=True, stop=True).then_inc(filled(*job), 1)

            def turn(g, job, blocks):
                pe.wait_ge(*room(g, *job))
                for n, t in enumerate(blocks):
                    ins = pe.transpose(bank(*job)[:, n * P:(n + 1) * P], t, ident)
                ins.then_inc(filled(*job), 1)

            def hold():
                pe.ldweights(ident_b[:], tile_position=(0, 0))

            def heads(n, out_bank, width, lhs, rhs, start, stop):
                for h in range(H):
                    r = slice(h * C, (h + 1) * C)
                    ins = pe.matmul(ps[r, out_bank, n * width:(n + 1) * width], lhs(r), rhs(r),
                                    start=start, stop=stop, skip_group_check=True)
                return ins

            def keep_clock(n):
                for _ in range(n):
                    pe.matmul(ps[:, BANK_KS, :], ident_b[:], bc_mid(ident_b[:, :], HALF // P), start=True, stop=True)

            def project(g, b4):
                for hf in range(2):
                    one(g, ("qkv", b4, hf), wproj[:, b4 * P:(b4 + 1) * P], half(hn, hf))

            def features(g):
                for name, src, ready in (("xnT", xn, xn_ready), ("xsT", xs, xs_ready)):
                    pe.wait_ge(ready.sem, ready.at(g, 1))
                    for hf in range(2):
                        turn(g, (name, hf), [src[:, t, :] for t in range(4 * hf, 4 * hf + 4)])

            def slot(p, g, c):
                if c == 0:
                    for hf in range(2):
                        pe.wait_ge(hsq_ready.sem, hsq_ready.at(g, hf + 1))
                        one(g, ("rms", hf), cst[:, C_MEAN:C_MEAN + P], half(sq[:, 0, :], hf))
                    pe.wait_ge(*copied(g, "xnT", 0))
                    pe.wait_ge(*copied(g, "xnT", 1))
                    pe.wait_ge(*room(g, "router"))
                    for t in range(TILES):
                        ins = pe.matmul(bank("router")[:, t * E:(t + 1) * E], xnT[:, t * P:(t + 1) * P], wrout[:],
                                        start=True, stop=True)
                        if p is not None and t < TILES - 1:
                            keep_clock(CLOCK_ROUTER)
                    ins.then_inc(filled("router"), 1)
                if c == 1:
                    pe.wait_ge(hn_ready.sem, hn_ready.at(g, 1))
                    pe.wait_ge(*room(g, "ab"))
                    for t in range(TILES):
                        ins = pe.matmul(bank("ab")[:, t * 2 * H:(t + 1) * 2 * H], hn[:, t * P:(t + 1) * P],
                                        wproj[:, W_AB:W_AB + 2 * H], start=True, stop=True)
                        if p is not None and t < TILES - 1:
                            keep_clock(CLOCK_AB)
                    ins.then_inc(filled("ab"), 1)
                    project(g, 0)
                if c == 2:
                    project(g, 1)
                    pe.wait_ge(gb_ready.sem, gb_ready.at(g, 1))
                    for name, k in (("grow", 0), ("brow", 1)):
                        for hf in range(2):
                            turn(g, (name, hf), [gb[:, k, t].rearrange("p h r -> p (h r)")
                                                 for t in range(4 * hf, 4 * hf + 4)])
                if c == 3:
                    pe.wait_ge(mcum_ready.sem, mcum_ready.at(g, 1))
                    mc = mcum.rearrange("p c i -> p (c i)")
                    for name, col in (("decay", C_LATER), ("fromstart", C_HEAD)):
                        for hf in range(2):
                            one(g, (name, hf), cst[:, col:col + P], half(mc, hf))
                    project(g, 2)
                if c == 4:
                    for b2 in range(2):
                        pe.wait_ge(sq_ready.sem, sq_ready.at(g, b2 + 1))
                        col = (C_HEADQ, C_HEAD)[b2]
                        for hf in range(2):
                            one(g, ("l2", b2, hf), cst[:, col:col + P], half(sq[:, b2, :], hf))
                    project(g, 3)
                if c == 5:
                    pairs(g)
                if c == 4:
                    turn_gates(g)
                for n in range(FIRST_STEP[c], FIRST_STEP[c + 1]):
                    experts(g, n)

            def pairs(g):
                pe.wait_ge(kq_ready.sem, kq_ready.at(g, 2))
                for q in range(4):
                    pe.wait_ge(*room(g, "pairs", q))
                    hold()
                    for n in range(8):
                        cols = slice((8 * q + n) * C, (8 * q + n + 1) * C)
                        ins = heads(n, bank_at[("pairs", q)][0], 2 * C, lambda r: conv[r, 1, cols],
                                    lambda r: conv[r, 0:2, cols], True, True)
                    ins.then_inc(filled("pairs", q), 1)

            def turn_gates(g):
                pe.wait_ge(gparts_ready.sem, gparts_ready.at(g, 1))
                pe.wait_ge(*room(g, "gateT"))
                hold()
                gt_ps = bank("gateT").bitcast(BF16)
                for t in range(TILES):
                    ins = pe.transpose(gt_ps[0:3 * E, t * P:(t + 1) * P], gparts[:, t].rearrange("p s e -> p (s e)"),
                                       ident_b[:])
                ins.then_inc(filled("gateT"), 1)

            def experts(g, n):
                if n < 2 * BLKS:
                    hf, m = STEPS[n]
                    one(g, ("up", hf, m), wup[:, m, :], half(xnT, hf))
                    if m:
                        pe.wait_ge(*copied(g, "gateT"))
                        one(g, ("gate", hf, m), sel[:, (m - 1) * P:m * P], half(gpT, hf))
                if n > 0:
                    hf, m = STEPS[n - 1]
                    if m == 0:
                        pe.wait_ge(*copied(g, "up", hf, 0))
                        pe.wait_ge(y_evac.sem, y_evac.at(g, hf))
                    else:
                        pe.wait_ge(*copied(g, "gate", hf, m))
                    pe.matmul(ps[:, BANK_Y, :], wdown[:, m, :], hid[:, (n - 1) % 3, :], start=(m == 0),
                              stop=(m == BLKS - 1)).then_inc(down_done.sem, 1)

            def out_gates(p, g):
                if p is not None:
                    pe.wait_ge(og_ready.sem, og_ready.at(p, NC_SEQ))
                for b2 in range(2):
                    for hf in range(2):
                        one(g, ("ogate", b2, hf), wproj[:, W_G + b2 * P:W_G + (b2 + 1) * P], half(hn, hf))

            def chunk_first(p, c):
                if c == 0:
                    pe.wait_ge(free[BANK_KS].sem, free[BANK_KS].at(p, 0))
                    pe.wait_ge(scaled_ready.sem, scaled_ready.at(p, 3))
                    pe.wait_ge(ttb_ready.sem, ttb_ready.at(p, 1))
                    pe.wait_ge(pt_ready.sem, pt_ready.at(p, 1))
                pe.wait_ge(s_ready.sem, s_ready.at(p, c + 1))
                hold()
                for b in range(SEQ):
                    ins = heads(b, BANK_KS, VD, lambda r: kg[r, b * NC_SEQ + c, :],
                                lambda r: state[r, b, :], True, True)
                ins.then_inc(ks_full.sem, 1)
                if c:
                    pe.wait_ge(o_ready.sem, o_ready.at(p, c))
                    hold()
                for b in range(SEQ):
                    heads(b, BANK_O, VD, lambda r: qg[r, b * NC_SEQ + c, :], lambda r: state[r, b, :],
                          b == 0, False)
                pe.wait_ge(r_ready.sem, r_ready.at(p, c + 1))
                hold()
                for b in range(SEQ):
                    ins = heads(b, BANK_D, VD, lambda r: ttb[r, b * NC_SEQ + c, :],
                                lambda r: resid[r, b, :], True, True)
                ins.then_inc(d_full.sem, 1)

            def chunk_last(p, c):
                pe.wait_ge(d_ready.sem, d_ready.at(p, c + 1))
                hold()
                for b in range(SEQ):
                    ins = heads(b, BANK_D, VD, lambda r: kend[r, b * NC_SEQ + c, :],
                                lambda r: delta[r, b, :], True, True)
                ins.then_inc(ds_full.sem, 1)
                for b in range(SEQ):
                    ins = heads(b, BANK_O, VD, lambda r: pt[r, b * NC_SEQ + c, :],
                                lambda r: delta[r, b, :], False, True)
                ins.then_inc(o_full.sem, 1)

            def project_out(p):
                pe.wait_ge(og_ready.sem, og_ready.at(p, NC_SEQ))
                for hf in range(2):
                    pe.wait_ge(*room(p, "enc", hf))
                    for n in range(4):
                        t = 4 * hf + n
                        for v2 in range(2):
                            ins = pe.matmul(bank("enc", hf)[:, n * P:(n + 1) * P], og[:, v2, t * P:(t + 1) * P],
                                            wo[:, v2, :], start=(v2 == 0), stop=(v2 == 1))
                    ins.then_inc(filled("enc", hf), 1)

            def turn_h2(p):
                pe.wait_ge(h2_ready.sem, h2_ready.at(p, 1))
                for hf in range(2):
                    turn(p, ("h2T", hf), [h2[:, t, :] for t in range(4 * hf, 4 * hf + 4)])

            def project_w2(p):
                for hf in range(2):
                    pe.wait_ge(*copied(p, "h2T", hf))
                    one(p, ("w2", hf), w2[:], half(h2T, hf))

            def turn_out(p):
                pe.wait_ge(sumT_ready.sem, sumT_ready.at(p, 1))
                for hf in range(2):
                    turn(p, ("final", hf), [sumT[:, t * P:(t + 1) * P] for t in range(4 * hf, 4 * hf + 4)])

            def round_(p, g, after):
                if p is not None:
                    pe.wait_ge(free[BANK_KS].sem, free[BANK_KS].at(p, 0))
                for c in range(NC_SEQ):
                    if p is not None:
                        keep_clock(CLOCK_FIRST[c])
                        chunk_first(p, c)
                    if g is not None:
                        slot(p, g, c)
                    if p is not None:
                        keep_clock(CLOCK_LAST[c])
                        chunk_last(p, c)
                if g is None:
                    project_out(p)
                    turn_h2(p)
                    project_w2(p)
                    turn_out(p)
                    return
                for n in range(IN_TAIL, 2 * BLKS):
                    experts(g, n)
                    if p is not None and n == ENC_BEHIND:
                        project_out(p)
                    if n == GATES_BEHIND:
                        out_gates(p, g)
                    if p is not None and n == H2_BEHIND:
                        turn_h2(p)
                    if p is not None and n == W2_BEHIND:
                        project_w2(p)
                experts(g, 2 * BLKS)
                if after is not None:
                    features(after)
                if p is not None:
                    turn_out(p)

            features(0)
            round_(None, 0, 1)
            with pe.Fori(0, groups - 2) as p:
                round_(p, p + 1, p + 2)
            round_(last_p - 1, last_p, None)
            round_(last_p, None, None)


def _constants():
    import numpy as np

    cst = np.zeros((P, C_COLS), np.float32)
    p = np.arange(P)
    head = (p[:, None] // C == p[None, :] // C).astype(np.float32)
    cst[:, C_IDENT:C_IDENT + P] = np.eye(P)
    cst[:, C_MEAN:C_MEAN + P] = 1.0 / P
    cst[:, C_HEAD:C_HEAD + P] = head
    cst[:, C_HEADQ:C_HEADQ + P] = head * KD
    cst[:, C_LATER:C_LATER + P] = head * (p[:, None] > p[None, :])
    cst[:, C_UPTO:C_UPTO + C] = p[:, None] % C <= np.arange(C)[None, :]
    cst[:, C_BEFORE:C_BEFORE + C] = p[:, None] % C < np.arange(C)[None, :]
    sel = np.zeros((3, E, BLKS - 1, 2, P // 2), np.float32)
    for e in range(E):
        sel[:, e, e // 2, e % 2, :] = 1.0
    return cst, sel.reshape(3 * E, (BLKS - 1) * P)


def kernel(L0_attn_x, L0_attn_ln1_g, L0_attn_ln1_b, L0_attn_ln2_g, L0_attn_ln2_b, L0_attn_rms_in_w, L0_attn_Wq,
           L0_attn_Wk, L0_attn_Wv, L0_attn_conv_q_w, L0_attn_conv_k_w, L0_attn_conv_v_w, L0_attn_Wa,
           L0_attn_dt_bias, L0_attn_A_log, L0_attn_Wb, L0_attn_Wg, L0_attn_o_norm_w, L0_attn_Wo, L0_attn_W2,
           L0_attn_b2, L0_ffn_shared_up, L0_ffn_shared_down, L0_ffn_routed_up, L0_ffn_routed_down,
           L0_ffn_router_w):
    import numpy as np
    import concourse.bacc as bacc
    from concourse.bass_utils import run_bass_kernel_spmd

    def a(v):
        return np.asarray(v)

    cst, sel = _constants()

    def halves(w):
        n = w.shape[0]
        return w.reshape(n, H, 2, VD // 2).transpose(0, 2, 1, 3).reshape(n, 2 * P)

    wproj = np.concatenate([a(L0_attn_Wq), a(L0_attn_Wk), halves(a(L0_attn_Wv)), halves(a(L0_attn_Wg)),
                            a(L0_attn_Wa), a(L0_attn_Wb)], axis=1)
    ups = np.concatenate([a(L0_ffn_shared_up), a(L0_ffn_routed_up)], axis=0).reshape(BLKS * P, P)
    downs = np.concatenate([a(L0_ffn_shared_down), a(L0_ffn_routed_down)], axis=0)
    conv_v = halves(a(L0_attn_conv_v_w).transpose()).transpose()
    onorm = np.tile(a(L0_attn_o_norm_w).reshape(2, 1, VD // 2), (1, H, 1)).reshape(2, P)
    vecs = np.stack([a(L0_attn_ln1_g), a(L0_attn_ln1_b), a(L0_attn_ln2_g), a(L0_attn_ln2_b),
                     a(L0_attn_rms_in_w), onorm[0], onorm[1], a(L0_attn_b2)], axis=1)
    vecs = np.concatenate([vecs, a(L0_attn_conv_q_w), a(L0_attn_conv_k_w), conv_v[0:P], conv_v[P:]], axis=1)
    rowb = np.concatenate([a(L0_attn_dt_bias), np.zeros(H, np.float32), a(L0_attn_A_log)])
    arrays = {
        "x": a(L0_attn_x).reshape(-1, P),
        "consts": cst,
        "sel": sel,
        "wproj": wproj,
        "wup": ups.transpose().reshape(P, BLKS, P),
        "wdown": downs.transpose(0, 2, 1).reshape(BLKS, P, P).transpose(1, 0, 2),
        "wo": halves(a(L0_attn_Wo).transpose()).reshape(P, 2, P).transpose(2, 1, 0),
        "w2": a(L0_attn_W2),
        "router": a(L0_ffn_router_w).transpose(),
        "vecs": vecs,
        "rowb": np.broadcast_to(rowb, (P, 3 * H)),
    }
    arrays = {f"in_{k}_dram": np.ascontiguousarray(v) for k, v in arrays.items()}
    nc = bacc.Bacc("TRN2", target_bir_lowering=False, num_devices=1)
    args = [nc.dram_tensor(k, v.shape, mybir.dt.from_np(v.dtype), kind="ExternalInput").ap()
            for k, v in arrays.items()]
    out = nc.dram_tensor("out_dram", (arrays["in_x_dram"].shape[0], P), F32, kind="ExternalOutput").ap()
    scr_a = nc.dram_tensor("scratch_a_dram", (H, C, NCH, C), F32, kind="Internal").ap()
    scr_t = nc.dram_tensor("scratch_t_dram", (H, NCH, C, C), F32, kind="Internal").ap()
    build(nc, *args, out, scr_a, scr_t)
    r = run_bass_kernel_spmd(nc, [arrays], core_ids=[0])
    return r.results[0]["out_dram"].reshape(L0_attn_x.shape)
```
